# Optimizing a Trainium2 kernel written in Bass

```python
import numpy as np
import jax
import jax.numpy as jnp

def _softmax(x, axis=-1):
    return jax.nn.softmax(x, axis=axis)

def _gelu(x):
    return jax.nn.gelu(x, approximate=True)

def _silu(x):
    return jax.nn.silu(x)

def _sigmoid(x):
    return jax.nn.sigmoid(x)

def _layernorm(x, axis=-1, eps=1e-05):
    m = jnp.mean(x, axis=axis, keepdims=True)
    v = jnp.var(x, axis=axis, keepdims=True)
    return (x - m) / jnp.sqrt(v + eps)

def _scatter_add(tgt, idx, src, axis=0):
    return tgt.at[idx].add(src)

def _segment_sum(src, seg, n):
    return jax.ops.segment_sum(src, seg, n)
kernel_name = 'mk_lm_tower_d1_tok_ids1024_r4_e9320c'

def setup_inputs(seed: int=0):
    np.random.seed(seed)
    _w = jnp.asarray

    def _rec_inputs():
        import jax
        import jax.numpy as jnp
        _rk = jax.random.key(seed)
        x = jax.random.randint(jax.random.fold_in(_rk, 1), (8, 1024), 0, 12564, jnp.int32)
        return x
    x = _rec_inputs()

    def _L0_tok_setup():
        import jax, jax.numpy as jnp
        import numpy as np
        VOCAB, DIM, MODEL_DIM = (65536, 64, 256)
        B, S = (4, 2048)
        key = jax.random.key(seed)
        k1, k2, k3 = jax.random.split(key, 3)
        ids = jax.random.randint(k1, (B, S), 0, 50257, dtype=jnp.int32)
        embed = jax.random.normal(k2, (VOCAB, DIM), dtype=jnp.float32) * 0.02
        proj_w = jax.random.normal(k3, (MODEL_DIM, DIM), dtype=jnp.float32) * 0.02
        scale = jnp.float32(0.05)
        return {'ids': ids, 'embed': embed, 'proj_w': proj_w, 'scale': scale}
    _L0_tok_all = _L0_tok_setup()
    _L0_tok_in = {k: v for k, v in _L0_tok_all.items() if k in ('embed', 'proj_w', 'scale')}
    del _L0_tok_all

    def _L0_attn_setup():
        import jax, jax.numpy as jnp
        import numpy as np
        import math
        B, T, C = (2, 512, 256)
        H, L = (16, 64)
        DH = C // H
        DHE = DH // 2
        THETA = 10000.0

        def _rope_cache(t, dim):
            inv_freq = 1.0 / THETA ** (jnp.arange(0, dim, 2, dtype=jnp.float32) / dim)
            freqs = jnp.arange(t, dtype=jnp.float32)[:, None] * inv_freq[None, :]
            emb = jnp.concatenate((freqs, freqs), axis=-1)
            return (jnp.cos(emb), jnp.sin(emb))

        def _apply_rope(x, cos, sin):
            x1 = x[..., 0::2]
            x2 = x[..., 1::2]
            rot = jnp.stack((-x2, x1), axis=-1).reshape(x.shape)
            return x * cos[None, None] + rot * sin[None, None]
        key = jax.random.key(seed)
        ks = jax.random.split(key, 10)
        s = 0.02
        return {'x': jax.random.normal(ks[0], (B, T, C), jnp.float32), 'Wq_down': jax.random.normal(ks[1], (C, H * L), jnp.float32) * s, 'Wk_down': jax.random.normal(ks[2], (C, H * L), jnp.float32) * s, 'Wv_down': jax.random.normal(ks[3], (C, H * L), jnp.float32) * s, 'Wq_up_c': jax.random.normal(ks[4], (L, DHE), jnp.float32) * s, 'Wq_up_e': jax.random.normal(ks[5], (L, DHE), jnp.float32) * s, 'Wk_up_c': jax.random.normal(ks[6], (L, DHE), jnp.float32) * s, 'Wk_up_e': jax.random.normal(ks[7], (L, DHE), jnp.float32) * s, 'Wv_up': jax.random.normal(ks[8], (L, DH), jnp.float32) * s, 'Wc': jax.random.normal(ks[9], (C, C), jnp.float32) * s}
    _L0_attn_all = _L0_attn_setup()
    _L0_attn_in = {k: v for k, v in _L0_attn_all.items() if k in ('Wq_down', 'Wk_down', 'Wv_down', 'Wq_up_c', 'Wq_up_e', 'Wk_up_c', 'Wk_up_e', 'Wv_up', 'Wc')}
    del _L0_attn_all

    def _L0_ffn_setup():
        import math
        import jax, jax.numpy as jnp
        import numpy as np
        B, S, H = (4, 512, 256)
        E, K, I = (8, 2, 256)
        NSH = 2
        CF, RSF = (1.25, 1.0)
        key = jax.random.key(seed)
        ks = jax.random.split(key, 8)
        w = lambda k, sh: jax.random.normal(k, sh, dtype=jnp.float32) * 0.02
        return {'hidden_states': jax.random.normal(ks[0], (B, S, H), dtype=jnp.float32), 'gate_w': w(ks[1], (E, H)), 'we_gate': w(ks[2], (E, I, H)), 'we_up': w(ks[3], (E, I, H)), 'we_down': w(ks[4], (E, H, I)), 'ws_gate': w(ks[5], (NSH * I, H)), 'ws_up': w(ks[6], (NSH * I, H)), 'ws_down': w(ks[7], (H, NSH * I))}
    _L0_ffn_all = _L0_ffn_setup()
    _L0_ffn_in = {k: v for k, v in _L0_ffn_all.items() if k in ('gate_w', 'we_gate', 'we_up', 'we_down', 'ws_gate', 'ws_up', 'ws_down')}
    del _L0_ffn_all
    return {'x': x, 'L0_tok_embed': _L0_tok_in['embed'], 'L0_tok_proj_w': _L0_tok_in['proj_w'], 'L0_tok_scale': _L0_tok_in['scale'], 'L0_attn_Wq_down': _L0_attn_in['Wq_down'], 'L0_attn_Wk_down': _L0_attn_in['Wk_down'], 'L0_attn_Wv_down': _L0_attn_in['Wv_down'], 'L0_attn_Wq_up_c': _L0_attn_in['Wq_up_c'], 'L0_attn_Wq_up_e': _L0_attn_in['Wq_up_e'], 'L0_attn_Wk_up_c': _L0_attn_in['Wk_up_c'], 'L0_attn_Wk_up_e': _L0_attn_in['Wk_up_e'], 'L0_attn_Wv_up': _L0_attn_in['Wv_up'], 'L0_attn_Wc': _L0_attn_in['Wc'], 'L0_ffn_gate_w': _L0_ffn_in['gate_w'], 'L0_ffn_we_gate': _L0_ffn_in['we_gate'], 'L0_ffn_we_up': _L0_ffn_in['we_up'], 'L0_ffn_we_down': _L0_ffn_in['we_down'], 'L0_ffn_ws_gate': _L0_ffn_in['ws_gate'], 'L0_ffn_ws_up': _L0_ffn_in['ws_up'], 'L0_ffn_ws_down': _L0_ffn_in['ws_down']}

def reference(x, L0_tok_embed, L0_tok_proj_w, L0_tok_scale, L0_attn_Wq_down, L0_attn_Wk_down, L0_attn_Wv_down, L0_attn_Wq_up_c, L0_attn_Wq_up_e, L0_attn_Wk_up_c, L0_attn_Wk_up_e, L0_attn_Wv_up, L0_attn_Wc, L0_ffn_gate_w, L0_ffn_we_gate, L0_ffn_we_up, L0_ffn_we_down, L0_ffn_ws_gate, L0_ffn_ws_up, L0_ffn_ws_down):
    import jax
    import jax.numpy as jnp

    def _L0_tok_ref(ids, embed, proj_w, scale):
        import jax, jax.numpy as jnp
        import numpy as np
        VOCAB, DIM, MODEL_DIM = (65536, 64, 256)
        B, S = (4, 2048)
        mod = embed.shape[0] - 1
        t = ids.astype(jnp.int32)
        hashed = jnp.mod(36313 * t[..., 1:] ^ 27191 * t[..., :-1], mod)
        first = jnp.full(t[..., :1].shape, mod, dtype=jnp.int32)
        h = jnp.concatenate([first, hashed], axis=-1)
        out = embed[h]
        out = jnp.einsum('bsd,md->bsm', out, proj_w)
        return out * scale.astype(out.dtype)

    def _L0_attn_ref(x, Wq_down, Wk_down, Wv_down, Wq_up_c, Wq_up_e, Wk_up_c, Wk_up_e, Wv_up, Wc):
        import jax, jax.numpy as jnp
        import numpy as np
        import math
        B, T, C = (2, 512, 256)
        H, L = (16, 64)
        DH = C // H
        DHE = DH // 2
        THETA = 10000.0

        def _rope_cache(t, dim):
            inv_freq = 1.0 / THETA ** (jnp.arange(0, dim, 2, dtype=jnp.float32) / dim)
            freqs = jnp.arange(t, dtype=jnp.float32)[:, None] * inv_freq[None, :]
            emb = jnp.concatenate((freqs, freqs), axis=-1)
            return (jnp.cos(emb), jnp.sin(emb))

        def _apply_rope(x, cos, sin):
            x1 = x[..., 0::2]
            x2 = x[..., 1::2]
            rot = jnp.stack((-x2, x1), axis=-1).reshape(x.shape)
            return x * cos[None, None] + rot * sin[None, None]
        b, t, c = x.shape
        q_lat = (x @ Wq_down).reshape(b, t, H, L)
        k_lat = (x @ Wk_down).reshape(b, t, H, L)
        v_lat = (x @ Wv_down).reshape(b, t, H, L)
        q_c = jnp.einsum('bthl,ld->bhtd', q_lat, Wq_up_c)
        q_e = jnp.einsum('bthl,ld->bhtd', q_lat, Wq_up_e)
        k_c = jnp.einsum('bthl,ld->bhtd', k_lat, Wk_up_c)
        k_e = jnp.einsum('bthl,ld->bhtd', k_lat, Wk_up_e)
        v = jnp.einsum('bthl,ld->bhtd', v_lat, Wv_up)
        cos, sin = _rope_cache(t, DHE)
        q = jnp.concatenate([q_c, _apply_rope(q_e, cos, sin)], axis=-1)
        k = jnp.concatenate([k_c, _apply_rope(k_e, cos, sin)], axis=-1)
        scale = 1.0 / math.sqrt(DH)
        scores = jnp.einsum('bhqd,bhkd->bhqk', q, k) * scale
        causal = jnp.tril(jnp.ones((t, t), dtype=bool))
        scores = jnp.where(causal[None, None], scores, -jnp.inf)
        att = jax.nn.softmax(scores, axis=-1)
        y = jnp.einsum('bhqk,bhkd->bhqd', att, v)
        y = y.transpose(0, 2, 1, 3).reshape(b, t, c)
        return y @ Wc

    def _L0_ffn_ref(hidden_states, gate_w, we_gate, we_up, we_down, ws_gate, ws_up, ws_down):
        import math
        import jax, jax.numpy as jnp
        import numpy as np
        B, S, H = (4, 512, 256)
        E, K, I = (8, 2, 256)
        NSH = 2
        CF, RSF = (1.25, 1.0)
        orig_shape = hidden_states.shape
        x = hidden_states.reshape(-1, H)
        N = x.shape[0]
        logits = x.astype(jnp.float32) @ gate_w.astype(jnp.float32).T
        scores = jax.nn.softmax(logits, axis=-1)
        topk_w, topk_idx = jax.lax.top_k(scores, K)
        topk_w = topk_w / (topk_w.sum(-1, keepdims=True) + 1e-20) * RSF
        capacity = math.ceil(CF * N * K / E)
        flat = topk_idx.reshape(-1)
        one_hot = jax.nn.one_hot(flat, E, dtype=jnp.int32)
        pos = jnp.cumsum(one_hot, axis=0) - 1
        pos_tok = jnp.take_along_axis(pos, flat[:, None], axis=1)[:, 0]
        keep = (pos_tok < capacity).reshape(N, K)
        topk_w = topk_w * keep.astype(topk_w.dtype)
        comb = jnp.zeros((N, E), jnp.float32).at[jnp.arange(N)[:, None], topk_idx].add(topk_w)
        g = jnp.einsum('nh,eih->nei', x, we_gate)
        u = jnp.einsum('nh,eih->nei', x, we_up)
        eo = jnp.einsum('nei,ehi->neh', jax.nn.silu(g) * u, we_down)
        y = jnp.einsum('neh,ne->nh', eo, comb)
        sh = jax.nn.silu(x @ ws_gate.T) * (x @ ws_up.T) @ ws_down.T
        return (y + sh).reshape(orig_shape)
    h = _L0_tok_ref(x, L0_tok_embed, L0_tok_proj_w, L0_tok_scale)
    h = h + _L0_attn_ref(_layernorm(h, axis=-1), L0_attn_Wq_down, L0_attn_Wk_down, L0_attn_Wv_down, L0_attn_Wq_up_c, L0_attn_Wq_up_e, L0_attn_Wk_up_c, L0_attn_Wk_up_e, L0_attn_Wv_up, L0_attn_Wc)
    h = h + _L0_ffn_ref(_layernorm(h, axis=-1), L0_ffn_gate_w, L0_ffn_we_gate, L0_ffn_we_up, L0_ffn_we_down, L0_ffn_ws_gate, L0_ffn_ws_up, L0_ffn_ws_down)
    return h

_drawn_inputs = setup_inputs


def setup_inputs(seed=0):
    import zlib

    import numpy as np

    out = dict(_drawn_inputs(seed))
    spreads = {}
    factors = {'L0_attn_Wq_down': 8.0,
     'L0_attn_Wk_down': 8.0,
     'L0_attn_Wq_up_c': 8.0,
     'L0_attn_Wq_up_e': 8.0,
     'L0_attn_Wk_up_c': 8.0,
     'L0_attn_Wk_up_e': 21.393}
    for name, (base, spread) in spreads.items():
        noise = np.random.default_rng([zlib.crc32(name.encode()), seed]).standard_normal(out[name].shape)
        drawn = base * np.exp(spread * noise) if base else spread * noise
        out[name] = jnp.asarray(drawn.astype(out[name].dtype))
    for name, factor in factors.items():
        out[name] = (out[name] * factor).astype(out[name].dtype)
    return out
```

```python
from contextlib import ExitStack

import numpy as np

import concourse.bass as bass
from concourse import mybir

ALU = mybir.AluOpType
ACT = mybir.ActivationFunctionType
AX = mybir.AxisListType
F32 = mybir.dt.float32
BF16 = mybir.dt.bfloat16
I32 = mybir.dt.int32
U32 = mybir.dt.uint32

P = 128
BANK = 512
B, T, C = 8, 1024, 256
N = B * T
DIM = 64
H, DH, HALF = 16, 16, 8
LAT = 64
KT = C // P
TILES = T // P
ALLT = N // P
HASH_MOD = 65535
MUL_CUR, MUL_PREV = 36313, 27191
EPS = 1e-5
UNITS = 2 * B
UH = H // 2
PARTS = 3
AUG = 6 * DH
VW = DH + 1
E, EI, TOPK = 8, 256, 2
CAP = 2560
SH = 512
CH = 512
QC = CAP // CH
MASKED = -1e30

assert CAP == -(-5 * N * TOPK // (4 * E))


class Steps:

    def __init__(self, sem, names, free=0):
        self.sem, self.free, self.per = sem, free, len(names)
        self.at = {name: n + 1 for n, name in enumerate(names)}
        assert len(self.at) == self.per

    def by(self, name, run=0):
        return run * self.per + (self.at[name] + self.free)

    def before(self, run):
        return run * self.per + self.free

    def end(self, run=0):
        return run * self.per + (self.per + self.free)



def prepare(nc, io, keep):
    with ExitStack() as ctx:
        sb = lambda name, shape, dt=F32: ctx.enter_context(nc.sbuf_tensor(name, shape, dt))
        sem = lambda name: ctx.enter_context(nc.semaphore(name))
        R = ALLT
        ids = sb("ids", [R, 2 * P], I32)
        ia, ib, ic, id_ = (sb(f"hash_{n}", [R, 2 * P], I32) for n in "abcd")
        hashed = sb("hashed", [R, P])
        hash_f = sb("hash_f", [R, P])
        index = sb("index", [P, R], U32)
        identf = sb("identf_p", [P, P])
        rows = sb("rows", [P, ALLT, DIM])
        down_t = sb("down_t", [P, 3, H // 2, C])
        up = sb("up", [P, 3, 2, 3 * HALF])
        ps = ctx.enter_context(nc.psum_tensor("ps_prepare", [P, 8, BANK], F32))
        loaded, up_loaded, down_loaded = sem("ids_loaded"), sem("up_loaded"), sem("down_loaded")
        up_zero, up_rot, chain = sem("up_zero"), sem("up_rot"), sem("hash_chain")
        index_t, index_ok, gathered, stored = sem("index_t"), sem("index_ok"), sem("gathered"), sem("rows_stored")
        eff_made, eff_kept = sem("eff_made"), sem("eff_kept")
        zeroed, zero_tile = sem("queues_zeroed"), sem("zero_tile")
        zero = sb("zero", [P, 2048])
        block = ctx.enter_context(nc.Block())

        @block.sync
        def _(sp):
            sp.dma_start(ids[:], io["ids"]).then_inc(loaded, 16)
            sp.dma_start(identf[:], io["identity"]).then_inc(loaded, 16)
            sp.wait_ge(up_zero, 1)
            for m, w in enumerate(("up_q", "up_k", "up_v")):
                for half in range(2):
                    sp.dma_start(up[LAT * half:LAT * (half + 1), m, half, 0:DH], io[w]).then_inc(up_loaded, 16)
            for m, w in enumerate(("down_q", "down_k", "down_v")):
                sp.dma_start(down_t[:, m], io[w].rearrange("(g p) c -> p g c", p=P)).then_inc(down_loaded, 16)
            sp.wait_ge(zero_tile, 1)
            fill = keep["queue"].rearrange("(n p r) c -> n p (r c)", p=P, r=8)
            for n in range(fill.shape[0]):
                sp.dma_start(fill[n], zero[:]).then_inc(zeroed, 16)
            sp.wait_ge(gathered, 16 * ALLT)
            sp.dma_start(keep["emb"].rearrange("(t p) d -> p t d", p=P), rows[:]).then_inc(stored, 16)
            sp.wait_ge(stored, 16)
            sp.wait_ge(zeroed, 16 * fill.shape[0])

        @block.gpsimd
        def _(pool):
            nc.gpsimd.memset(zero[:], 0.0).then_inc(zero_tile, 1)
            pool.wait_ge(index_ok, 1)
            for t in range(ALLT):
                nc.gpsimd.indirect_dma_start(
                    out=rows[:, t, :], out_offset=None, in_=io["embed"],
                    in_offset=bass.IndirectOffsetOnAxis(ap=index[:, t:t + 1], axis=0),
                ).then_inc(gathered, 16)

        @block.vector
        def _(dve):
            steps = [0]

            def link(ins):
                steps[0] += 1
                ins.then_inc(chain, 1)
                dve.wait_ge(chain, steps[0])

            ts = nc.vector.tensor_scalar
            tt = nc.vector.tensor_tensor
            nc.vector.memset(up[:], 0.0).then_inc(up_zero, 1)
            dve.wait_ge(loaded, 32)
            halves = ((slice(0, P), MUL_CUR), (slice(P, 2 * P), MUL_PREV))
            link(ts(ia[:], ids[:], 8, None, ALU.logical_shift_right))
            link(ts(ib[:], ids[:], 255, None, ALU.bitwise_and))
            for cols, mul in halves:
                link(ts(ia[:, cols], ia[:, cols], float(mul), None, ALU.mult))
                link(ts(ib[:, cols], ib[:, cols], float(mul), None, ALU.mult))
            link(ts(ic[:], ia[:], 255, 8, ALU.bitwise_and, ALU.logical_shift_left))
            link(ts(id_[:], ib[:], 65535, None, ALU.bitwise_and))
            link(tt(ic[:], ic[:], id_[:], ALU.add))
            link(ts(ia[:], ia[:], 8, None, ALU.logical_shift_right))
            link(ts(ib[:], ib[:], 16, None, ALU.logical_shift_right))
            link(tt(ia[:], ia[:], ib[:], ALU.add))
            link(ts(ib[:], ic[:], 16, None, ALU.logical_shift_right))
            link(tt(ia[:], ia[:], ib[:], ALU.add))
            link(ts(ic[:], ic[:], 65535, None, ALU.bitwise_and))
            link(tt(ia[:, 0:P], ia[:, 0:P], ia[:, P:2 * P], ALU.bitwise_xor))
            link(tt(ic[:, 0:P], ic[:, 0:P], ic[:, P:2 * P], ALU.bitwise_xor))
            link(ts(ib[:, 0:P], ia[:, 0:P], 15, None, ALU.logical_shift_right))
            link(tt(ia[:, 0:P], ia[:, 0:P], ic[:, 0:P], ALU.add))
            link(tt(ia[:, 0:P], ia[:, 0:P], ib[:, 0:P], ALU.subtract))
            link(ts(ib[:, 0:P], ia[:, 0:P], 16, None, ALU.logical_shift_right))
            link(ts(ic[:, 0:P], ia[:, 0:P], 65535, None, ALU.bitwise_and))
            link(tt(ia[:, 0:P], ib[:, 0:P], ic[:, 0:P], ALU.add))
            link(nc.vector.tensor_copy(hashed[:], ia[:, 0:P]))
            link(ts(hash_f[:], hashed[:], float(HASH_MOD), -float(HASH_MOD), ALU.is_ge, ALU.mult))
            link(tt(hashed[:], hashed[:], hash_f[:], ALU.add))
            dve.wait_ge(index_t, 1)
            link(nc.vector.tensor_copy(index[:], ps[:, 0, 0:R]))
            nc.vector.memset(index[0:1, 0:R:TILES], HASH_MOD).then_inc(index_ok, 1)

            dve.wait_ge(up_loaded, 16 * 6)
            for m in range(2):
                for half in range(2):
                    at = up[LAT * half:LAT * (half + 1), m, half]
                    ts(at[:, DH:DH + HALF:2], at[:, HALF + 1:DH:2], -1.0, None, ALU.mult).then_inc(up_rot, 1)
                    nc.vector.tensor_copy(at[:, DH + 1:DH + HALF:2], at[:, HALF:DH:2]).then_inc(up_rot, 1)
            for m in range(3):
                for ct in range(KT):
                    for g in range(H // 2):
                        n = (m * KT + ct) * (H // 2) + g
                        dve.wait_ge(eff_made, n + 1)
                        src = ps[:, 1 + n % 7, 0:2 * 3 * HALF].rearrange("p (h y d) -> p h y d", h=2, d=HALF)
                        if m < 2:
                            dst = keep["w_qk"][:, ct, m].rearrange("p y (h d) -> p h y d", d=HALF)[:, 2 * g:2 * g + 2]
                            ts(dst, src, DH ** -0.5 if m == 0 else 1.0, None, ALU.mult).then_inc(eff_kept, 1)
                        else:
                            dst = keep["w_v"][:, ct, 2 * DH * g:2 * DH * (g + 1)].rearrange("p (h y d) -> p h y d", h=2, d=HALF)
                            nc.vector.tensor_copy(dst, src[:, :, 0:2, :]).then_inc(eff_kept, 1)

        @block.tensor
        def _(pe):
            pe.wait_ge(chain, 26)
            pe.transpose(ps[:, 0, 0:R], hashed[:], identf[0:R, 0:R]).then_inc(index_t, 1)
            pe.wait_ge(down_loaded, 16 * 3)
            pe.wait_ge(up_rot, 8)
            for m in range(3):
                for ct in range(KT):
                    for g in range(H // 2):
                        n = (m * KT + ct) * (H // 2) + g
                        if n >= 7:
                            pe.wait_ge(eff_kept, n - 6)
                        pe.matmul(ps[:, 1 + n % 7, 0:2 * 3 * HALF], down_t[:, m, g, P * ct:P * (ct + 1)],
                                  up[:, m].rearrange("p a b -> p (a b)"), start=True, stop=True).then_inc(eff_made, 1)



MAX_BLOCKS = [(i, 0, min(BANK, P * (i + 1))) for i in range(TILES)] + \
             [(i, BANK, P * (i + 1) - BANK) for i in range(BANK // P, TILES)]
MAXES = UH * len(MAX_BLOCKS)
STEPS = [(g, c, j) for g in range(2) for c in range(2) for j in range(4 * (c + 1))]
NS = len(STEPS)
DIAG = [s for s, (g, c, j) in enumerate(STEPS) if j >= 4 * c]
MAX_FROM, MAX_PER = 3, 6
LAST_OF = {s: 2 * g + c for s, (g, c, j) in enumerate(STEPS) if j == 4 * (c + 1) - 1}


def alone(eng, sem, value, waited):
    eng.wait_ge(sem, value)
    if not isinstance(value, int):
        eng.sem_inc(waited, 1)


def at_first(x):
    return isinstance(x, int) and x == 0


def towers(nc, io, keep):
    with ExitStack() as ctx:
        sb = lambda name, shape, dt=F32: ctx.enter_context(nc.sbuf_tensor(name, shape, dt))
        sem = lambda name: ctx.enter_context(nc.semaphore(name))

        st = ctx.enter_context(nc.psum_tensor("st", [P, 4, BANK], F32))
        sm = ctx.enter_context(nc.psum_tensor("sm", [P, 2, BANK], F32))
        pv = ctx.enter_context(nc.psum_tensor("pv", [P, 2, BANK], F32))

        identf, maskf = sb("identf", [P, P]), sb("maskf", [P, P])
        identb, maskb = sb("identb", [P, P], BF16), sb("maskb", [P, P], BF16)
        proj, scale = sb("proj", [P, C]), sb("scale", [P, 1])
        w_out, w_gate = sb("w_out", [P, KT, C]), sb("w_gate", [P, KT, E])
        cos, sin = sb("cos", [P, T]), sb("sin", [P, T])
        emb = sb("emb", [P, TILES, P])
        h = sb("h", [P, TILES, C])
        x2 = sb("x2", [P, TILES, C])
        stats, mv = sb("stats", [P, TILES, 6]), sb("mv", [P, TILES, 2])
        var, lnv, rstd, tmp = (sb(n, [P, TILES]) for n in ("var", "lnv", "rstd", "tmp"))
        big = sb("big", [P, 4, T])
        xn = big[:, 0:2].rearrange("p a t -> p (a t)").rearrange("p (t c) -> p t c", c=C)
        xnT = big[:, 2:4]
        yT_raw = big
        small = sb("small", [P, TILES * C])
        embT = small[:, 0:T]
        y = small[:].rearrange("p (t c) -> p t c", c=C)
        yT = sb("yT", [P, KT, T])
        parts = sb("parts", [P, 2, 2, PARTS, BANK], BF16)
        res = sb("res", [P, 2, BANK])
        rot_a, rot_b, rot_c = sb("rot_a", [P, BANK]), sb("rot_b", [P, BANK]), sb("rot_c", [P, BANK])
        v_next = sb("v_next", [P, TILES, H, DH])
        v = sb("v", [P, TILES, H * VW + DH])
        qa, ka = sb("qa", [P, 2, UH, T], BF16), sb("ka", [P, 2, UH, T], BF16)
        prob = sb("prob", [P, 4, 2, BANK])
        mx = sb("mx", [P, UH, len(MAX_BLOCKS)])
        nmax = sb("nmax", [P, UH, TILES])
        m_parts, m_res = sb("m_parts", [UH * TILES, PARTS, P], BF16), sb("m_res", [UH * TILES, P])
        rden = sb("rden", [P, 2, H])
        lg_sb = sb("lg_sb", [P, TILES, E])

        qk = [f"{a}{s}" for s in range(4) for a in ("c", "e", "r")]
        f_pe = Steps(sem("front_pe"), ["et0", "et1", "h0", "h1", "h2", "h3", "x0", "x1", "x2", "x3"] + qk
                     + [f"v{k}" for k in range(4)])
        f_act = Steps(sem("front_act"), ["et0", "et1", "h0", "h1", "h2", "h3", "ln", "rs", "x0", "x2"]
                      + [f"{a}{s}" for s in range(4) for a in ("hc", "he")] + [f"v{k}" for k in range(4)])
        norm_steps = [f"st{t}" for t in range(TILES)] + [f"ag{t}" for t in range(TILES)] + ["var", "n1", "n2", "n3", "n4"] \
            + [f"xn{t}" for t in range(TILES)]
        f_dve = Steps(sem("front_dve"), norm_steps + ["x1", "x3"]
                      + [f"{a}{s}" for s in range(4) for a in ("rc", "t1", "t2", "qe", "re")])
        f_pool = Steps(sem("front_pool"), [f"{a}{s}" for s in range(4) for a in ("mc", "lc", "me", "le")])
        emb_loaded, h_stored = sem("emb_loaded"), sem("h_stored")
        parts_stored = [sem("q_parts_stored"), sem("k_parts_stored")]
        v_moved = sem("v_moved")
        aug_loaded = [sem("aug_loaded_0"), sem("aug_loaded_1")]
        m_pe = Steps(sem("max_pe"), [f"m{k}" for k in range(MAXES)] + ["t"])
        m_dve = Steps(sem("max_dve"), [f"m{k}" for k in range(MAXES)] + ["cp", "mn", "hi", "res", "mid", "lo"])
        m_stored, m_loaded = sem("m_stored"), sem("m_loaded")
        a_st = Steps(sem("scores"), [f"{n}" for n in range(2 * NS)])
        a_exp = Steps(sem("exps"), [f"{n}" for n in range(2 * NS)], free=2)
        a_mask = Steps(sem("masked"), [f"{2 * s + p}" for s in DIAG for p in range(2)])
        a_pv = Steps(sem("summed"), [f"{s}" for s in range(NS)], free=2)
        a_out = Steps(sem("sums_kept"), [f"{q}" for q in range(4)], free=2)
        b_pe = Steps(sem("back_pe"), [f"yt{t}" for t in range(TILES)] + [f"z{n}" for n in range(4)]
                     + [f"w{k}" for k in range(4)] + [f"p{n}" for n in range(4)] + ["gate"])
        b_act = Steps(sem("back_act"), ["z0", "z2", "ln", "rs", "p0", "p2"])
        b_dve = Steps(sem("back_dve"), [f"{a}{t}" for t in range(TILES) for a in ("rc", "y")] + ["z1", "z3"]
                      + [f"a{k}" for k in range(4)] + norm_steps + ["p1", "p3", "gate"])
        h_loaded, h2_stored, x2_stored, x2T_stored, lg_stored = (sem(n) for n in (
            "h_loaded", "h2_stored", "x2_stored", "x2T_stored", "lg_stored"))
        const_loaded, const_made = sem("const_loaded"), sem("const_made")
        waited_sp, waited_pool, waited_dve, waited_pe = (sem(f"waited_{n}") for n in ("sp", "pool", "dve", "pe"))

        block = ctx.enter_context(nc.Block())

        def in_order(eng, front, maxima, attend, back1, back2):
            front(0)
            maxima(0)
            front(1)

            def batch(b, ahead, more):
                attend(2 * b, b, 0, True)
                attend(2 * b + 1, b, 1, more)
                back1(b, more)
                if ahead:
                    front(b + 2)
                back2(b, ahead)

            with eng.Fori(0, B - 2) as b:
                batch(b, True, True)
            batch(B - 2, False, True)
            batch(B - 1, False, False)

        @block.sync
        def _(sp):
            for dst, src in ((identf[:], io["identity"]), (maskf[:], io["mask"]), (proj[0:DIM, :], io["proj_t"]),
                             (scale[:], io["scale"]), (w_out[:], io["w_out"].rearrange("(k p) c -> p k c", p=P)),
                             (w_gate[:], io["gate_t"].rearrange("(k p) e -> p k e", p=P)),
                             (cos[:], io["cos"]), (sin[:], io["sin"])):
                sp.dma_start(dst, src).then_inc(const_loaded, 16)
            sp.wait_ge(const_made, 4)

            def load_emb(b):
                sp.dma_start(emb[:, :, 0:DIM], keep["emb"].rearrange("(b t p) d -> b p t d", p=P, t=TILES)[b]
                             ).then_inc(emb_loaded, 16)

            def front(b):
                if at_first(b):
                    load_emb(0)
                    alone(sp, f_pe.sem, f_pe.by("et1", 0), waited_sp)
                    load_emb(1)
                alone(sp, f_act.sem, f_act.by("h3", b), waited_sp)
                sp.dma_start(keep["h"].rearrange("(b t p) c -> b p t c", p=P, t=TILES)[b], h[:]).then_inc(h_stored, 16)
                for s in range(4):
                    c, side = divmod(s, 2)
                    alone(sp, f_pool.sem, f_pool.by(f"le{s}", b), waited_sp)
                    alone(sp, f_act.sem, f_act.by(f"he{s}", b), waited_sp)
                    for y_ in range(2):
                        sp.dma_start(
                            keep["parts"][b, side, :, y_, :, BANK * c:BANK * (c + 1)].rearrange("p r t -> r p t"),
                            parts[:, side, y_]).then_inc(parts_stored[side], 16)

            def load_aug(b, half):
                for side in range(2):
                    alone(sp, parts_stored[side], b * 64 + 64, waited_sp)
                slot = half
                rows_ = slice(UH * HALF * half, UH * HALF * (half + 1))
                for blk, (qp, kp) in enumerate(((0, 0), (1, 0), (2, 0), (0, 1), (1, 1), (0, 2))):
                    for side, part, dst in ((0, qp, qa), (1, kp, ka)):
                        for y_ in range(2):
                            r0 = DH * blk + HALF * y_
                            sp.dma_start(dst[r0:r0 + HALF, slot],
                                         keep["parts"][b, side, part, y_, rows_, :].rearrange("(h d) t -> d h t", d=HALF)
                                         ).then_inc(aug_loaded[slot], 16)

            def move_max(u, slot):
                alone(sp, m_dve.sem, m_dve.by("lo", u), waited_sp)
                sp.dma_start(keep["max"][u].rearrange("p r q -> r p q"), m_parts[:]).then_inc(m_stored, 16)
                alone(sp, m_stored, u * 16 + 16, waited_sp)
                sp.dma_start(qa[AUG:AUG + PARTS, slot].rearrange("p h t -> p (h t)"),
                             keep["max"][u].rearrange("p r q -> p (r q)")).then_inc(m_loaded, 16)

            def maxima(u):
                load_aug(0, 0)
                move_max(0, 0)

            def attend(u, b, half, more):
                if half == 0 and not isinstance(b, int):
                    alone(sp, f_pe.sem, f_pe.by("et1", b + 1), waited_sp)
                    load_emb(b + 2)
                alone(sp, a_st.sem, a_st.before(u), waited_sp)
                if more:
                    load_aug(b + half, 1 - half)
                    move_max(u + 1, 1 - half)
                if half == 1:
                    load_h(b)

            def load_h(b):
                if not (isinstance(b, int) and b == B - 1):
                    alone(sp, f_dve.sem, f_dve.by("xn7", b + 1), waited_sp)
                    alone(sp, h_stored, b * 16 + 32, waited_sp)
                if isinstance(b, int) and b == B - 1:
                    alone(sp, b_dve.sem, b_dve.by("xn7", b - 1), waited_sp)
                    alone(sp, h2_stored, b * 16, waited_sp)
                sp.dma_start(h[:], keep["h"].rearrange("(b t p) c -> b p t c", p=P, t=TILES)[b]).then_inc(h_loaded, 16)

            def back1(b, more):
                alone(sp, b_dve.sem, b_dve.by("a3", b), waited_sp)
                sp.dma_start(keep["h2"].rearrange("(b t p) c -> b p t c", p=P, t=TILES)[b], h[:]).then_inc(h2_stored, 16)
                alone(sp, b_dve.sem, b_dve.by("xn7", b), waited_sp)
                sp.dma_start(keep["x2"].rearrange("(b t p) c -> b p t c", p=P, t=TILES)[b], x2[:]).then_inc(x2_stored, 16)

            def back2(b, ahead):
                alone(sp, b_act.sem, b_act.by("p2", b), waited_sp)
                alone(sp, b_dve.sem, b_dve.by("p3", b), waited_sp)
                sp.dma_start(keep["x2T"][:, :, bass.ds(b * T, T)] if not isinstance(b, int) else keep["x2T"][:, :, b * T:(b + 1) * T],
                             xnT).then_inc(x2T_stored, 16)
                alone(sp, b_dve.sem, b_dve.by("gate", b), waited_sp)
                sp.dma_start(keep["logits"][b], lg_sb[:]).then_inc(lg_stored, 16)

            in_order(sp, front, maxima, attend, back1, back2)
            for s_ in (h_stored, h2_stored, x2_stored, x2T_stored, lg_stored):
                alone(sp, s_, 16 * B, waited_sp)

        @block.tensor
        def _(pe):
            pe.wait_ge(const_loaded, 16 * 8)
            pe.wait_ge(const_made, 9)
            pe.sem_inc(a_pv.sem, 2)

            def front(b):
                pe.wait_ge(emb_loaded, b * 16 + 16)
                if isinstance(b, int) and b == 1:
                    pe.wait_ge(f_act.sem, f_act.end(0))
                elif not at_first(b):
                    pe.wait_ge(b_dve.sem, b_dve.by("a3", b - 2))
                for half in range(2):
                    for q in range(4):
                        ins = pe.transpose(st[:, half, P * q:P * (q + 1)], emb[:, 4 * half + q, :], identf[:])
                    ins.then_inc(f_pe.sem, 1)
                for k, bank in enumerate((2, 3, 0, 1)):
                    pe.wait_ge(f_act.sem, f_act.by("et0" if k < 2 else "et1", b))
                    for q in range(2):
                        t = 2 * k + q
                        ins = pe.matmul(st[:, bank, C * q:C * (q + 1)], embT[:, P * t:P * (t + 1)], proj[:],
                                        start=True, stop=True)
                    ins.then_inc(f_pe.sem, 1)
                for ct in range(KT):
                    for half in range(2):
                        for q in range(4):
                            t = 4 * half + q
                            pe.wait_ge(f_dve.sem, f_dve.by(f"xn{t}", b))
                            ins = pe.transpose(st[:, 2 * ct + half, P * q:P * (q + 1)], xn[:, t, P * ct:P * (ct + 1)], identf[:])
                        ins.then_inc(f_pe.sem, 1)
                pe.wait_ge(f_act.sem, f_act.by("x2", b))
                pe.wait_ge(f_dve.sem, f_dve.by("x3", b))
                readers = ("rc", "t1", "t2")
                for s in range(4):
                    c, side = divmod(s, 2)
                    for k in range(3):
                        n = 3 * s + k
                        if n >= 4:
                            pe.wait_ge(f_dve.sem, f_dve.by(f"{readers[(n - 4) % 3]}{(n - 4) // 3}", b))
                        for ct in range(KT):
                            ins = pe.matmul(st[:, n % 4, :], keep["w_qk"][:, ct, side, k], xnT[:, ct, BANK * c:BANK * (c + 1)],
                                            start=(ct == 0), stop=(ct == KT - 1))
                        ins.then_inc(f_pe.sem, 1)
                for k in range(4):
                    n = 8 + k
                    pe.wait_ge(f_dve.sem, f_dve.by(f"{readers[n % 3]}{n // 3}", b))
                    for q in range(2):
                        t = 2 * k + q
                        for ct in range(KT):
                            ins = pe.matmul(st[:, k, C * q:C * (q + 1)], xnT[:, ct, P * t:P * (t + 1)], keep["w_v"][:, ct],
                                            start=(ct == 0), stop=(ct == KT - 1))
                    ins.then_inc(f_pe.sem, 1)

            def max_block(u, slot, k):
                hh, (i, k0, w) = k // len(MAX_BLOCKS), MAX_BLOCKS[k % len(MAX_BLOCKS)]
                if k >= 2:
                    pe.wait_ge(m_dve.sem, m_dve.by(f"m{k - 2}", u))
                elif not at_first(u):
                    pe.wait_ge(m_dve.sem, m_dve.before(u))
                diag = k0 + w == P * (i + 1)
                ins = pe.matmul(sm[:, k % 2, 0:w], qa[0:AUG, slot, hh, P * i:P * (i + 1)], ka[0:AUG, slot, hh, k0:k0 + w],
                                start=True, stop=not diag)
                if diag:
                    ins = pe.matmul(sm[:, k % 2, w - P:w], identb[:], maskb[:], start=False, stop=True)
                ins.then_inc(m_pe.sem, 1)

            def max_turn(u):
                alone(pe, m_dve.sem, m_dve.by("mn", u), waited_pe)
                pe.transpose(sm[0:UH * TILES, 0, 0:P], nmax[:].rearrange("p h t -> p (h t)"), identf[:]).then_inc(m_pe.sem, 1)

            def maxima(u):
                pe.wait_ge(aug_loaded[0], 16 * 24)
                for k in range(MAXES):
                    max_block(u, 0, k)
                max_turn(u)

            def attend(u, b, half, more):
                pe.wait_ge(m_loaded, u * 16 + 16)
                pe.wait_ge(v_moved, b * 2 + 2)
                if half == 0:
                    if at_first(b):
                        pe.wait_ge(f_act.sem, f_act.end(1))
                    elif isinstance(b, int):
                        pe.wait_ge(b_dve.sem, b_dve.end(b - 1))
                    else:
                        pe.wait_ge(f_act.sem, f_act.end(b + 1))
                        pe.wait_ge(b_dve.sem, b * b_dve.per)

                def sums(s):
                    g, c, j = STEPS[s]
                    off = max(0, P * j - BANK * c)
                    if j == 0:
                        pe.wait_ge(a_out.sem, a_out.by(str(2 * g + c), u) - 2)
                    if s in DIAG:
                        pe.wait_ge(a_mask.sem, a_mask.by(str(2 * s + 1), u))
                    else:
                        pe.wait_ge(a_exp.sem, a_exp.by(str(2 * s + 1), u))
                    for q in range(4):
                        hh = UH * half + 4 * g + q
                        ins = pe.matmul(pv[32 * q:32 * (q + 1), c, off:BANK], v[:, j, VW * hh:VW * hh + 32],
                                        prob[:, (2 * s + q // 2) % 4, q % 2, off:BANK],
                                        start=(j == 0), stop=(j == 4 * (c + 1) - 1))
                    ins.then_inc(a_pv.sem, 1)

                for s, (g, c, j) in enumerate(STEPS):
                    off = max(0, P * j - BANK * c)
                    for p in range(2):
                        n = 2 * s + p
                        pe.wait_ge(a_exp.sem, a_exp.by(str(n), u) - 2)
                        for q in range(2):
                            hh = 4 * g + 2 * p + q
                            ins = pe.matmul(st[:, 2 * p + q, off:BANK], ka[0:AUG + PARTS, half, hh, P * j:P * (j + 1)],
                                            qa[0:AUG + PARTS, half, hh, BANK * c + off:BANK * (c + 1)],
                                            start=True, stop=True)
                        ins.then_inc(a_st.sem, 1)
                    if s:
                        sums(s - 1)
                    if more and s == MAX_FROM:
                        pe.wait_ge(aug_loaded[1 - half], (b + half) * 384 + 384)
                    if more and 0 <= s - MAX_FROM < MAXES // MAX_PER:
                        for k in range(MAX_PER * (s - MAX_FROM), MAX_PER * (s - MAX_FROM + 1)):
                            max_block(u + 1, 1 - half, k)
                    if more and s - MAX_FROM == MAXES // MAX_PER:
                        max_turn(u + 1)
                sums(NS - 1)

            def back1(b, more):
                pe.wait_ge(a_out.sem, a_out.end(b * 2 + 1))
                pe.wait_ge(a_exp.sem, a_exp.end(b * 2 + 1))
                for t in range(TILES):
                    if t >= 4:
                        pe.wait_ge(b_dve.sem, b_dve.by(f"y{t - 4}", b))
                    for g in range(4):
                        ins = pe.transpose(st[:, t % 4, P * g:P * (g + 1)], yT_raw[:, g, P * t:P * (t + 1)], identf[:])
                    ins.then_inc(b_pe.sem, 1)
                for n in range(4):
                    half, ct = divmod(n, 2)
                    pe.wait_ge(b_dve.sem, b_dve.by(f"y{4 + n if n < 2 else 7}", b))
                    for q in range(4):
                        ins = pe.transpose(st[:, n, P * q:P * (q + 1)], y[:, 4 * half + q, P * ct:P * (ct + 1)], identf[:])
                    ins.then_inc(b_pe.sem, 1)
                pe.wait_ge(b_act.sem, b_act.by("z2", b))
                pe.wait_ge(b_dve.sem, b_dve.by("z3", b))
                for k in range(4):
                    for q in range(2):
                        t = 2 * k + q
                        for ct in range(KT):
                            ins = pe.matmul(st[:, k, C * q:C * (q + 1)], yT[:, ct, P * t:P * (t + 1)], w_out[:, ct],
                                            start=(ct == 0), stop=(ct == KT - 1))
                    ins.then_inc(b_pe.sem, 1)

            def back2(b, ahead):
                if ahead:
                    pe.wait_ge(f_act.sem, f_act.end(b + 2))
                pe.wait_ge(b_dve.sem, b_dve.by("xn7", b))
                for n in range(4):
                    half, ct = divmod(n, 2)
                    for q in range(4):
                        ins = pe.transpose(st[:, n, P * q:P * (q + 1)], x2[:, 4 * half + q, P * ct:P * (ct + 1)], identf[:])
                    ins.then_inc(b_pe.sem, 1)
                pe.wait_ge(b_act.sem, b_act.by("p2", b))
                pe.wait_ge(b_dve.sem, b_dve.by("p3", b))
                for t in range(TILES):
                    for ct in range(KT):
                        ins = pe.matmul(st[:, 0, E * t:E * (t + 1)], xnT[:, ct, P * t:P * (t + 1)], w_gate[:, ct],
                                        start=(ct == 0), stop=(ct == KT - 1))
                ins.then_inc(b_pe.sem, 1)

            in_order(pe, front, maxima, attend, back1, back2)

        @block.scalar
        def _(act):
            a = nc.scalar.activation
            act.wait_ge(const_loaded, 16 * 8)
            act.sem_inc(a_exp.sem, 2)

            def front(b):
                for k in range(2):
                    act.wait_ge(f_pe.sem, f_pe.by(f"et{k}", b))
                    if k == 0 and not (isinstance(b, int) and b < 2):
                        act.wait_ge(b_pe.sem, b_pe.by("z3", b - 2))
                    a(embT[:, BANK * k:BANK * (k + 1)], st[:, k, :], ACT.Copy).then_inc(f_act.sem, 1)
                if isinstance(b, int) and b == 1:
                    act.wait_ge(f_dve.sem, f_dve.by("xn7", 0))
                    act.wait_ge(h_stored, 16)
                elif not at_first(b):
                    act.wait_ge(b_dve.sem, b_dve.by("xn7", b - 2))
                    act.wait_ge(h2_stored, b * 16 - 16)
                for k, bank in enumerate((2, 3, 0, 1)):
                    act.wait_ge(f_pe.sem, f_pe.by(f"h{k}", b))
                    a(h[:, 2 * k:2 * k + 2, :].rearrange("p t c -> p (t c)"), st[:, bank, :], ACT.Identity,
                      scale=scale[:, 0:1]).then_inc(f_act.sem, 1)
                rsqrt(f_dve, f_act, b)
                for k in (0, 2):
                    act.wait_ge(f_pe.sem, f_pe.by(f"x{k}", b))
                    a(xnT[:, k // 2, 0:BANK], st[:, k, :], ACT.Copy).then_inc(f_act.sem, 1)
                for s in range(4):
                    c, side = divmod(s, 2)
                    if s >= 2 or not at_first(b):
                        act.wait_ge(parts_stored[side], b * 64 + 32 * (s // 2))
                    act.wait_ge(f_pe.sem, f_pe.by(f"c{s}", b))
                    a(parts[:, side, 0, 0, :], st[:, 3 * s % 4, :], ACT.Copy).then_inc(f_act.sem, 1)
                    act.wait_ge(f_dve.sem, f_dve.by(f"qe{s}", b))
                    a(parts[:, side, 1, 0, :], rot_c[:], ACT.Copy).then_inc(f_act.sem, 1)
                if not at_first(b):
                    act.wait_ge(v_moved, b * 2)
                for k in range(4):
                    act.wait_ge(f_pe.sem, f_pe.by(f"v{k}", b))
                    a(v_next[:, 2 * k:2 * k + 2].rearrange("p t h d -> p (t h d)"), st[:, k, :], ACT.Copy).then_inc(f_act.sem, 1)

            def rsqrt(dve_steps, act_steps, b):
                act.wait_ge(dve_steps.sem, dve_steps.by("var", b))
                a(lnv[:], var[:], ACT.Ln).then_inc(act_steps.sem, 1)
                act.wait_ge(act_steps.sem, act_steps.by("ln", b))
                a(rstd[:], lnv[:], ACT.Exp, scale=-0.5).then_inc(act_steps.sem, 1)

            def attend(u, b, half, more):
                for s, (g, c, j) in enumerate(STEPS):
                    off = max(0, P * j - BANK * c)
                    act.wait_ge(a_pv.sem, a_pv.by(str(s), u) - 2)
                    for p in range(2):
                        n = 2 * s + p
                        act.wait_ge(a_st.sem, a_st.by(str(n), u))
                        a(prob[:, n % 4, :, off:BANK], st[:, 2 * p:2 * p + 2, off:BANK], ACT.Exp).then_inc(a_exp.sem, 1)

            def back1(b, more):
                for n in (0, 2):
                    half, ct = divmod(n, 2)
                    act.wait_ge(b_pe.sem, b_pe.by(f"z{n}", b))
                    a(yT[:, ct, BANK * half:BANK * (half + 1)], st[:, n, :], ACT.Copy).then_inc(b_act.sem, 1)
                rsqrt(b_dve, b_act, b)

            def back2(b, ahead):
                for n in (0, 2):
                    half, ct = divmod(n, 2)
                    act.wait_ge(b_pe.sem, b_pe.by(f"p{n}", b))
                    a(xnT[:, ct, BANK * half:BANK * (half + 1)], st[:, n, :], ACT.Copy).then_inc(b_act.sem, 1)

            in_order(act, front, lambda u: None, attend, back1, back2)

        @block.gpsimd
        def _(pool):
            pool.wait_ge(const_loaded, 16 * 8)

            def front(b):
                for s in range(4):
                    c, side = divmod(s, 2)
                    if s >= 2 or not at_first(b):
                        alone(pool, parts_stored[side], b * 64 + 32 * (s // 2), waited_pool)
                    for y_, (r, m_, l_) in enumerate((("rc", "mc", "lc"), ("re", "me", "le"))):
                        alone(pool, f_dve.sem, f_dve.by(f"{r}{s}", b), waited_pool)
                        nc.gpsimd.tensor_copy(parts[:, side, y_, 1, :], res[:, y_, :]).then_inc(f_pool.sem, 1)
                        alone(pool, f_pool.sem, f_pool.by(f"{m_}{s}", b), waited_pool)
                        nc.gpsimd.tensor_tensor(parts[:, side, y_, 2, :], res[:, y_, :], parts[:, side, y_, 1, :],
                                                ALU.subtract).then_inc(f_pool.sem, 1)

            def attend(u, b, half, more):
                for s in DIAG:
                    g, c, j = STEPS[s]
                    off = P * j - BANK * c
                    for p in range(2):
                        n = 2 * s + p
                        alone(pool, a_exp.sem, a_exp.by(str(n), u), waited_pool)
                        at = prob[:, n % 4, :, off:off + P]
                        nc.gpsimd.affine_select(out=at, in_=at, compare_op=ALU.is_ge, fill=0.0, base=0,
                                                pattern=[[0, 2], [1, P]], channel_multiplier=-1).then_inc(a_mask.sem, 1)

            nothing = lambda *_: None
            in_order(pool, front, nothing, attend, nothing, nothing)

        @block.vector
        def _(dve):
            ts, tt = nc.vector.tensor_scalar, nc.vector.tensor_tensor
            nc.vector.memset(emb[:], 0.0).then_inc(const_made, 1)
            nc.vector.memset(ka[96:96 + PARTS, :], 1.0).then_inc(const_made, 1)
            nc.vector.memset(v[:], 1.0).then_inc(const_made, 1)
            nc.vector.memset(lg_sb[:], 0.0).then_inc(const_made, 1)
            dve.wait_ge(const_made, 4)
            nc.vector.memset(proj[64:P, :], 0.0).then_inc(const_made, 1)
            dve.sem_inc(a_out.sem, 2)
            dve.wait_ge(const_loaded, 16 * 8)
            nc.vector.tensor_copy(identb[:], identf[:]).then_inc(const_made, 1)
            nc.vector.tensor_copy(maskb[:], maskf[:]).then_inc(const_made, 1)
            dve.sem_inc(const_made, 2)
            dve.wait_ge(const_made, 9)

            def norm(steps, run, out):
                for t in range(TILES):
                    nc.vector.bn_stats(stats[:, t, :], h[:, t, :]).then_inc(steps.sem, 1)
                for t in range(TILES):
                    alone(dve, steps.sem, steps.by(f"st{t}", run), waited_dve)
                    nc.vector.bn_aggr(mv[:, t, :], stats[:, t, :]).then_inc(steps.sem, 1)
                dve.wait_ge(steps.sem, steps.by("ag7", run))
                ts(var[:], mv[:, :, 1], EPS, None, ALU.add).then_inc(steps.sem, 1)
                act_steps = f_act if steps is f_dve else b_act
                dve.wait_ge(act_steps.sem, act_steps.by("rs", run))
                dve.wait_ge(steps.sem, steps.by("var", run))
                tt(tmp[:], rstd[:], rstd[:], ALU.mult).then_inc(steps.sem, 1)
                dve.wait_ge(steps.sem, steps.by("n1", run))
                tt(tmp[:], tmp[:], var[:], ALU.mult).then_inc(steps.sem, 1)
                dve.wait_ge(steps.sem, steps.by("n2", run))
                ts(tmp[:], tmp[:], -0.5, 1.5, ALU.mult, ALU.add).then_inc(steps.sem, 1)
                dve.wait_ge(steps.sem, steps.by("n3", run))
                tt(rstd[:], rstd[:], tmp[:], ALU.mult).then_inc(steps.sem, 1)
                dve.wait_ge(steps.sem, steps.by("n4", run))
                for t in range(TILES):
                    ts(out[:, t, :], h[:, t, :], mv[:, t, 0:1], rstd[:, t:t + 1], ALU.subtract, ALU.mult).then_inc(steps.sem, 1)
                dve.wait_ge(steps.sem, steps.by(f"xn{TILES - 1}", run))

            def front(b):
                dve.wait_ge(f_act.sem, f_act.by("h3", b))
                norm(f_dve, b, xn)
                for k in (1, 3):
                    dve.wait_ge(f_pe.sem, f_pe.by(f"x{k}", b))
                    nc.vector.tensor_copy(xnT[:, k // 2, BANK:], st[:, k, :]).then_inc(f_dve.sem, 1)
                for s in range(4):
                    c, side = divmod(s, 2)
                    cols = slice(BANK * c, BANK * (c + 1))
                    bank = [(3 * s + k) % 4 for k in range(3)]
                    if s:
                        dve.wait_ge(f_pool.sem, f_pool.by(f"le{s - 1}", b))
                    elif not at_first(b):
                        dve.wait_ge(f_pool.sem, b * f_pool.per)
                    dve.wait_ge(f_act.sem, f_act.by(f"hc{s}", b))
                    tt(res[:, 0, :], st[:, bank[0], :], parts[:, side, 0, 0, :], ALU.subtract).then_inc(f_dve.sem, 1)
                    dve.wait_ge(f_pe.sem, f_pe.by(f"e{s}", b))
                    tt(rot_a[:], st[:, bank[1], :], cos[:, cols], ALU.mult).then_inc(f_dve.sem, 1)
                    dve.wait_ge(f_pe.sem, f_pe.by(f"r{s}", b))
                    tt(rot_b[:], st[:, bank[2], :], sin[:, cols], ALU.mult).then_inc(f_dve.sem, 1)
                    dve.wait_ge(f_dve.sem, f_dve.by(f"t2{s}", b))
                    tt(rot_c[:], rot_a[:], rot_b[:], ALU.add).then_inc(f_dve.sem, 1)
                    dve.wait_ge(f_dve.sem, f_dve.by(f"qe{s}", b))
                    dve.wait_ge(f_act.sem, f_act.by(f"he{s}", b))
                    tt(res[:, 1, :], rot_c[:], parts[:, side, 1, 0, :], ALU.subtract).then_inc(f_dve.sem, 1)
                    dve.wait_ge(f_dve.sem, f_dve.by(f"re{s}", b))
                if at_first(b):
                    move_v(0)

            def move_v(b):
                dve.wait_ge(f_act.sem, f_act.end(b))
                out = v[:, :, 0:H * VW].rearrange("p t (h d) -> p t h d", d=VW)
                for k in range(2):
                    tiles = slice(4 * k, 4 * k + 4)
                    nc.vector.tensor_copy(out[:, tiles, :, 0:DH], v_next[:, tiles]).then_inc(v_moved, 1)

            def max_block(u, k):
                hh, kk = divmod(k, len(MAX_BLOCKS))
                w = MAX_BLOCKS[kk][2]
                dve.wait_ge(m_pe.sem, m_pe.by(f"m{k}", u))
                nc.vector.tensor_reduce(mx[:, hh, kk:kk + 1], sm[:, k % 2, 0:w], AX.X, ALU.max, negate=True).then_inc(m_dve.sem, 1)

            def max_end(u):
                dve.wait_ge(m_dve.sem, m_dve.by(f"m{MAXES - 1}", u))
                q = BANK // P
                nc.vector.tensor_copy(nmax[:, :, 0:q], mx[:, :, 0:q]).then_inc(m_dve.sem, 1)
                tt(nmax[:, :, q:], mx[:, :, q:2 * q], mx[:, :, 2 * q:], ALU.min).then_inc(m_dve.sem, 1)
                dve.wait_ge(m_pe.sem, m_pe.by("t", u))
                if not at_first(u):
                    dve.wait_ge(m_stored, u * 16)
                turned = sm[0:UH * TILES, 0, 0:P]
                nc.vector.tensor_copy(m_parts[:, 0, :], turned).then_inc(m_dve.sem, 1)
                dve.wait_ge(m_dve.sem, m_dve.by("hi", u))
                tt(m_res[:], turned, m_parts[:, 0, :], ALU.subtract).then_inc(m_dve.sem, 1)
                dve.wait_ge(m_dve.sem, m_dve.by("res", u))
                nc.vector.tensor_copy(m_parts[:, 1, :], m_res[:]).then_inc(m_dve.sem, 1)
                dve.wait_ge(m_dve.sem, m_dve.by("mid", u))
                tt(m_parts[:, 2, :], m_res[:], m_parts[:, 1, :], ALU.subtract).then_inc(m_dve.sem, 1)
                dve.wait_ge(m_dve.sem, m_dve.by("lo", u))

            def maxima(u):
                for k in range(MAXES):
                    max_block(u, k)
                max_end(u)

            def attend(u, b, half, more):
                def sums_out(q):
                    g, c = divmod(q, 2)
                    s = max(s_ for s_, q_ in LAST_OF.items() if q_ == q)
                    dve.wait_ge(a_pv.sem, a_pv.by(str(s), u))
                    nc.vector.tensor_copy(yT_raw[:, 2 * half + g, BANK * c:BANK * (c + 1)], pv[:, c, :]).then_inc(a_out.sem, 1)

                if half == 0 and not at_first(b):
                    dve.wait_ge(x2T_stored, b * 16)
                if half == 0:
                    if isinstance(b, int):
                        dve.wait_ge(f_pe.sem, f_pe.end(min(b + 1, B - 1)))
                    else:
                        dve.wait_ge(f_pe.sem, f_pe.end(b + 1))
                    if not at_first(b):
                        dve.wait_ge(b_pe.sem, b * b_pe.per)
                for s in range(NS):
                    if s and s - 1 in LAST_OF:
                        sums_out(LAST_OF[s - 1])
                    if more and 0 <= s - MAX_FROM < MAXES // MAX_PER:
                        for k in range(MAX_PER * (s - MAX_FROM), MAX_PER * (s - MAX_FROM + 1)):
                            max_block(u + 1, k)
                    if more and s - MAX_FROM == MAXES // MAX_PER:
                        max_end(u + 1)
                sums_out(3)

            def back1(b, more):
                for t in range(TILES):
                    dve.wait_ge(b_pe.sem, b_pe.by(f"yt{t}", b))
                    src = st[:, t % 4, :].rearrange("p (h d) -> p h d", d=32)
                    if t >= 2:
                        dve.wait_ge(b_dve.sem, b_dve.by(f"y{t - 2}", b))
                    nc.vector.reciprocal(rden[:, t % 2, :], src[:, :, DH]).then_inc(b_dve.sem, 1)
                    dve.wait_ge(b_dve.sem, b_dve.by(f"rc{t}", b))
                    tt(y[:, t, :].rearrange("p (h d) -> p h d", d=DH), src[:, :, 0:DH],
                       rden[:, t % 2, :].unsqueeze(2).to_broadcast([P, H, DH]), ALU.mult).then_inc(b_dve.sem, 1)
                for n in (1, 3):
                    half, ct = divmod(n, 2)
                    dve.wait_ge(b_pe.sem, b_pe.by(f"z{n}", b))
                    nc.vector.tensor_copy(yT[:, ct, BANK * half:BANK * (half + 1)], st[:, n, :]).then_inc(b_dve.sem, 1)
                dve.wait_ge(h_loaded, b * 16 + 16)
                for k in range(4):
                    dve.wait_ge(b_pe.sem, b_pe.by(f"w{k}", b))
                    at = h[:, 2 * k:2 * k + 2, :].rearrange("p t c -> p (t c)")
                    tt(at, st[:, k, :], at, ALU.add).then_inc(b_dve.sem, 1)
                dve.wait_ge(b_dve.sem, b_dve.by("a3", b))
                if not at_first(b):
                    dve.wait_ge(x2_stored, b * 16)
                norm(b_dve, b, x2)
                if more:
                    dve.wait_ge(a_pv.sem, a_pv.end(b * 2 + 1))
                    move_v(b + 1)

            def back2(b, ahead):
                for n in (1, 3):
                    half, ct = divmod(n, 2)
                    dve.wait_ge(b_pe.sem, b_pe.by(f"p{n}", b))
                    nc.vector.tensor_copy(xnT[:, ct, BANK * half:BANK * (half + 1)], st[:, n, :]).then_inc(b_dve.sem, 1)
                dve.wait_ge(b_pe.sem, b_pe.by("gate", b))
                if not at_first(b):
                    dve.wait_ge(lg_stored, b * 16)
                nc.vector.tensor_copy(lg_sb[:].rearrange("p t e -> p (t e)"), st[:, 0, 0:TILES * E]).then_inc(b_dve.sem, 1)

            in_order(dve, front, maxima, attend, back1, back2)



def route(nc, io, keep):
    shape = [P, ALLT, E]
    with ExitStack() as ctx:
        sb = lambda name, shape, dt=F32: ctx.enter_context(nc.sbuf_tensor(name, shape, dt))
        sem = lambda name: ctx.enter_context(nc.semaphore(name))
        lg, ex, eq, l2, sel = (sb(f"r_{n}", shape) for n in ("lg", "ex", "eq", "l2", "sel"))
        hot = [sb(f"r_hot{k}", shape) for k in range(TOPK)]
        pre_a, pre_b, pos, tmp = (sb(f"r_{n}", shape) for n in ("pre_a", "pre_b", "pos", "tmp"))
        first, start = sb("r_first", shape), sb("r_start", shape)
        best = sb("r_best", [P, ALLT])
        pk, kept, slot = (sb(f"r_{n}", [P, ALLT, TOPK]) for n in ("pk", "kept", "slot"))
        gone = sb("r_gone", [P, ALLT, TOPK])
        total, score = sb("r_total", [P, ALLT]), sb("r_score", [P, ALLT, TOPK])
        before, ones = sb("r_before", [P, P]), sb("r_ones", [P, P])
        ps = ctx.enter_context(nc.psum_tensor("ps_route", [P, 2, BANK], F32))
        loaded, chain, shifted, exped, counted = (sem(n) for n in (
            "route_loaded", "route_chain", "shifted_ready", "exp_ready", "counts_ready"))
        sel_ready = sem("sel_ready")
        block = ctx.enter_context(nc.Block())
        flat = lambda x: x[:].rearrange("p t e -> p (t e)")

        @block.sync
        def _(sp):
            for dst, src in ((lg[:].rearrange("p (b t) e -> p b t e", t=TILES), keep["logits"].rearrange("b p t e -> p b t e")),
                             (first[:], io["first"]), (start[:], io["start"]),
                             (before[:], io["before"]), (ones[:], io["ones"])):
                sp.dma_start(dst, src).then_inc(loaded, 16)

        @block.scalar
        def _(act):
            act.wait_ge(shifted, 1)
            nc.scalar.activation(flat(ex), flat(ex), ACT.Exp).then_inc(exped, 1)

        @block.tensor
        def _(pe):
            pe.wait_ge(loaded, 16 * 5)
            pe.wait_ge(sel_ready, 1)
            pe.matmul(ps[:, 0, :], before[:], flat(sel), start=True, stop=True)
            pe.matmul(ps[:, 1, :], ones[:], flat(sel), start=True, stop=True).then_inc(counted, 1)

        @block.vector
        def _(dve):
            ts, tt, red = nc.vector.tensor_scalar, nc.vector.tensor_tensor, nc.vector.tensor_reduce
            steps = [0]

            def link(ins):
                steps[0] += 1
                ins.then_inc(chain, 1)
                dve.wait_ge(chain, steps[0])

            wide = lambda x: x.unsqueeze(2).to_broadcast(shape)
            dve.wait_ge(loaded, 16 * 5)
            src = lg
            for k in range(TOPK):
                link(red(best[:], src[:], AX.X, ALU.max))
                link(tt(eq[:], src[:], wide(best[:]), ALU.is_equal))
                if k == 0:
                    tt(ex[:], lg[:], wide(best[:]), ALU.subtract).then_inc(shifted, 1)
                link(tt(eq[:], eq[:], first[:], ALU.mult))
                if k == 0:
                    dve.wait_ge(shifted, 1)
                link(red(best[:], eq[:], AX.X, ALU.max))
                link(tt(hot[k][:], eq[:], wide(best[:]), ALU.is_equal))
                if k == 0:
                    link(ts(l2[:], hot[0][:], MASKED, None, ALU.mult))
                    link(tt(l2[:], l2[:], lg[:], ALU.add))
                    src = l2
            tt(sel[:], hot[0][:], hot[1][:], ALU.add).then_inc(sel_ready, 1)
            dve.wait_ge(exped, 1)
            link(red(total[:], ex[:], AX.X, ALU.add))
            link(nc.vector.reciprocal(total[:], total[:]))
            for k in range(TOPK):
                link(tt(tmp[:], hot[k][:], ex[:], ALU.mult))
                link(red(score[:, :, k], tmp[:], AX.X, ALU.add))
                link(tt(score[:, :, k], score[:, :, k], total[:], ALU.mult))
            link(tt(total[:], score[:, :, 0], score[:, :, 1], ALU.add))
            link(ts(total[:], total[:], 1e-20, None, ALU.add))
            link(nc.vector.reciprocal(total[:], total[:]))
            link(tt(score[:], score[:], total[:].unsqueeze(2).to_broadcast([P, ALLT, TOPK]), ALU.mult))
            dve.wait_ge(counted, 1)
            link(nc.vector.tensor_copy(flat(pre_a), ps[:, 1, :]))
            link(tt(flat(pos), ps[:, 0, :], flat(pre_a), ALU.subtract))
            a, b, d = pre_a, pre_b, 1
            while d < ALLT:
                link(nc.vector.tensor_copy(b[:, 0:d, :], a[:, 0:d, :]))
                link(tt(b[:, d:, :], a[:, d:, :], a[:, :ALLT - d, :], ALU.add))
                a, b, d = b, a, 2 * d
            link(tt(pos[:], pos[:], a[:], ALU.add))
            for k in range(TOPK):
                link(tt(tmp[:], hot[k][:], pos[:], ALU.mult))
                link(red(pk[:, :, k], tmp[:], AX.X, ALU.add))
                link(tt(tmp[:], hot[k][:], start[:], ALU.mult))
                link(red(slot[:, :, k], tmp[:], AX.X, ALU.add))
            link(tt(slot[:], slot[:], pk[:], ALU.add))
            link(ts(kept[:], pk[:], float(CAP), None, ALU.is_lt))
            link(tt(keep["weight"][:], score[:], kept[:], ALU.mult))
            link(tt(slot[:], slot[:], kept[:], ALU.mult))
            link(nc.vector.tensor_copy(keep["gather"][:], slot[:]))
            link(ts(gone[:], kept[:], -float(E * CAP), float(E * CAP), ALU.mult, ALU.add))
            link(tt(slot[:], slot[:], gone[:], ALU.add))
            link(nc.vector.tensor_copy(keep["scatter"][:], slot[:]))



RUNS = 4
RT = ALLT // RUNS
RING = 4
ITEMS = 2 * QC


def experts(nc, io, keep):
    with ExitStack() as ctx:
        sb = lambda name, shape, dt=F32: ctx.enter_context(nc.sbuf_tensor(name, shape, dt))
        sem = lambda name: ctx.enter_context(nc.semaphore(name))
        tr = ctx.enter_context(nc.psum_tensor("tr", [P, KT, BANK], F32))
        gu = ctx.enter_context(nc.psum_tensor("gu", [P, 4, BANK], F32))
        dn = ctx.enter_context(nc.psum_tensor("dn", [P, 2, BANK], F32))
        MS, QT = SH // P, CH // P
        identf = sb("identf_e", [P, P])
        wsg, wsu = sb("wsg", [P, KT, SH]), sb("wsu", [P, KT, SH])
        wsd = sb("wsd", [P, MS, C])
        xs, hs = sb("xs", [P, 2, KT, CH]), sb("hs", [P, 2, QT, C])
        sil = sb("sil", [P, 2, CH])
        inner = sb("inner", [P, 2, MS, CH])
        out_s = sb("out_s", [P, 2, QT, C])
        row = sb("row", [P, RING, C])
        g_row = sb("g_row", [P, RING, TOPK, C])
        done = sb("done", [P, RING, C])
        idx = sb("idx", [P, RT, TOPK], U32)
        w_now = sb("w_now", [P, RT, TOPK])
        weg, weu, wed = (sb(n, [P, 2, KT, EI]) for n in ("weg", "weu", "wed"))
        xg, xgT = sb("xg", [P, 2, QT, C]), sb("xgT", [P, 2, KT, CH])
        e_sil, e_in = sb("e_sil", [P, 2, CH]), sb("e_in", [P, 2, KT, CH])
        eo = sb("eo", [P, 2, QT, C])

        s_pe = Steps(sem("shared_pe"), [f"{x}g{m}" for x in range(2) for m in range(MS)] + [f"{x}d{k}" for x in range(2) for k in range(2)])
        s_act = Steps(sem("shared_act"), [f"{x}s{m}" for x in range(2) for m in range(MS)])
        s_dve = Steps(sem("shared_dve"), [f"{x}a{m}" for x in range(2) for m in range(MS)] + [f"{x}o{k}" for x in range(2) for k in range(2)])
        xs_loaded = [sem("xs0_loaded"), sem("xs1_loaded")]
        sum_stored = [sem("sum0_stored"), sem("sum1_stored")]
        const_loaded = sem("const_e_loaded")
        waited_sp, waited_pool = sem("waited_sp_e"), sem("waited_pool_e")
        idx_ready = sem("idx_ready")
        row_loaded = [sem(f"row{k}_loaded") for k in range(RING)]
        scattered = [sem(f"row{k}_scattered") for k in range(RING)]
        gathered = [sem(f"row{k}_gathered") for k in range(RING)]
        base_loaded = [sem(f"base{k}_loaded") for k in range(RING)]
        w_ready, half_sum, combined = sem("w_ready"), sem("half_sum"), sem("combined")
        out_stored = [sem(f"out{k}_stored") for k in range(RING)]
        e_pe = Steps(sem("expert_pe"), ["t0"] + [n for x in range(ITEMS) for n in (
            [f"g{x}_0", f"g{x}_1"] + ([f"t{x + 1}"] if x < ITEMS - 1 else []) + [f"d{x}_0", f"d{x}_1"])])
        e_act = Steps(sem("expert_act"), ["t0"] + [n for x in range(ITEMS) for n in (
            [f"s{x}_0", f"s{x}_1"] + ([f"t{x + 1}"] if x < ITEMS - 1 else []) + [f"o{x}"])])
        e_dve = Steps(sem("expert_dve"), ["t0"] + [n for x in range(ITEMS) for n in (
            [f"a{x}_0", f"a{x}_1"] + ([f"t{x + 1}"] if x < ITEMS - 1 else []) + [f"o{x}"])])
        xg_loaded = [sem("xg0_loaded"), sem("xg1_loaded")]
        eo_stored = [sem("eo0_stored"), sem("eo1_stored")]
        w_loaded = [sem("we0_loaded"), sem("we1_loaded")]

        tiles_of = lambda ap: ap.rearrange("(t p) c -> t p c", p=P)
        chunk_of = lambda ap: ap.rearrange("(n t p) c -> n p t c", p=P, t=CH // P)
        queue_of = lambda ap: ap.rearrange("(n p t) c -> n p t c", p=P, t=CH // P)
        block = ctx.enter_context(nc.Block())

        def in_order(eng, shared, expert_run, scatter=None, combine=None):
            with eng.Fori(0, RUNS) as i:
                if shared:
                    shared(i, i)
                if scatter:
                    scatter(i)
            if expert_run:
                with eng.Fori(0, E // 2 - 1) as r:
                    expert_run(r, False)
                expert_run(E // 2 - 1, True)
            with eng.Fori(0, RUNS) as i:
                if shared:
                    shared(i + RUNS, i)
                if combine:
                    combine(i)

        @block.sync
        def _(sp):
            for dst, src in ((identf[:], io["identity"]), (wsg[:], io["ws_gate"].rearrange("(k p) i -> p k i", p=P)),
                             (wsu[:], io["ws_up"].rearrange("(k p) i -> p k i", p=P)),
                             (wsd[:], io["ws_down"].rearrange("(k p) c -> p k c", p=P))):
                sp.dma_start(dst, src).then_inc(const_loaded, 16)

            def load_weights(e, par):
                for dst, src in ((weg, io["we_gate"]), (weu, io["we_up"]), (wed, io["we_down"])):
                    sp.dma_start(dst[:, par], src[e].rearrange("(k p) i -> p k i", p=P)).then_inc(w_loaded[par], 16)

            load_weights(0, 0)
            load_weights(1, 1)

            def shared(run, i):
                for x in range(2):
                    alone(sp, s_pe.sem, s_pe.before(run), waited_sp)
                    alone(sp, s_dve.sem, s_dve.before(run), waited_sp)
                    sp.dma_start(xs[:, x], keep["x2T"].rearrange("p k (n t) -> n p k t", t=CH)[2 * run + x]).then_inc(xs_loaded[x], 16)
                    sp.dma_start(hs[:, x], chunk_of(keep["h2"])[2 * run + x]).then_inc(xs_loaded[x], 16)

            def store_sums(run):
                for x in range(2):
                    alone(sp, s_dve.sem, s_dve.by(f"{x}o1", run), waited_sp)
                    sp.dma_start(chunk_of(keep["sum"])[2 * run + x], out_s[:, x]).then_inc(sum_stored[x], 16)

            def scatter(i):
                for t in range(RT):
                    k = t % RING
                    alone(sp, scattered[k], i * (RT // RING * 32) + 32 * (t // RING), waited_sp)
                    sp.dma_start(row[:, k], tiles_of(keep["x2"])[i * RT + t]).then_inc(row_loaded[k], 16)
                store_sums(i)

            def expert_run(r, last):
                def load_rows(run, x):
                    sp.dma_start(xg[:, x % 2], queue_of(keep["queue"])[run * ITEMS + x]).then_inc(xg_loaded[x % 2], 16)

                for x in range(ITEMS):
                    alone(sp, e_pe.sem, e_pe.by(f"t{x}", r), waited_sp)
                    if x + 2 < ITEMS:
                        load_rows(r, x + 2)
                    elif not last:
                        load_rows(r + 1, x + 2 - ITEMS)
                    alone(sp, e_act.sem, e_act.by(f"o{x}", r), waited_sp)
                    alone(sp, e_dve.sem, e_dve.by(f"o{x}", r), waited_sp)
                    sp.dma_start(queue_of(keep["expert_out"])[r * ITEMS + x], eo[:, x % 2]).then_inc(eo_stored[x % 2], 16)
                    if x % QC == QC - 1 and not last:
                        load_weights(2 * r + 2 + x // QC, x // QC)

            def combine(i):
                store_sums(i + RUNS)
                for x in range(2):
                    alone(sp, sum_stored[x], i * 16 + 16 * (RUNS + 1), waited_sp)
                for t in range(RT):
                    k = t % RING
                    alone(sp, combined, i * RT + t, waited_sp)
                    sp.dma_start(row[:, k], tiles_of(keep["sum"])[i * RT + t]).then_inc(base_loaded[k], 16)
                    if t:
                        store_out(i, t - 1)
                alone(sp, combined, i * RT + RT, waited_sp)
                store_out(i, RT - 1)

            def store_out(i, t):
                sp.dma_start(tiles_of(io["out"])[i * RT + t], done[:, t % RING]).then_inc(out_stored[t % RING], 16)

            with sp.Fori(0, RUNS) as i:
                shared(i, i)
                scatter(i)
            for k in range(RING):
                alone(sp, scattered[k], ALLT // RING * 32, waited_sp)
            for x in range(2):
                sp.dma_start(xg[:, x], queue_of(keep["queue"])[x]).then_inc(xg_loaded[x], 16)
            with sp.Fori(0, E // 2 - 1) as r:
                expert_run(r, False)
            expert_run(E // 2 - 1, True)
            with sp.Fori(0, RUNS) as i:
                shared(i + RUNS, i)
                combine(i)
            for k in range(RING):
                alone(sp, out_stored[k], ALLT // RING * 16, waited_sp)

        @block.gpsimd
        def _(pool):
            def scatter(i):
                alone(pool, idx_ready, i * 1, waited_pool)
                nc.gpsimd.tensor_copy(idx[:], keep["scatter"][:, bass.ds(i * RT, RT), :]).then_inc(idx_ready, 1)
                alone(pool, idx_ready, i * 1 + 1, waited_pool)
                for t in range(RT):
                    k = t % RING
                    alone(pool, row_loaded[k], i * (RT // RING * 16) + 16 * (t // RING + 1), waited_pool)
                    for n in range(TOPK):
                        nc.gpsimd.indirect_dma_start(
                            out=keep["queue"], out_offset=bass.IndirectOffsetOnAxis(ap=idx[:, t, n:n + 1], axis=0),
                            in_=row[:, k], in_offset=None, bounds_check=E * CAP - 1, oob_is_err=False,
                        ).then_inc(scattered[k], 16)
                for k in range(RING):
                    alone(pool, scattered[k], i * (RT // RING * 32) + RT // RING * 32, waited_pool)

            def combine(i):
                nc.gpsimd.tensor_copy(idx[:], keep["gather"][:, bass.ds(i * RT, RT), :]).then_inc(idx_ready, 1)
                alone(pool, idx_ready, i * 1 + RUNS + 1, waited_pool)
                for t in range(RT):
                    k = t % RING
                    if t >= RING:
                        alone(pool, combined, i * RT + t - RING + 1, waited_pool)
                    else:
                        alone(pool, combined, i * RT, waited_pool)
                    for n in range(TOPK):
                        nc.gpsimd.indirect_dma_start(
                            out=g_row[:, k, n], out_offset=None, in_=keep["expert_out"],
                            in_offset=bass.IndirectOffsetOnAxis(ap=idx[:, t, n:n + 1], axis=0),
                        ).then_inc(gathered[k], 16)
                for k in range(RING):
                    alone(pool, gathered[k], i * (RT // RING * 32) + RT // RING * 32, waited_pool)

            with pool.Fori(0, RUNS) as i:
                scatter(i)
            for x in range(2):
                alone(pool, eo_stored[x], 16 * E * QC // 2, waited_pool)
            with pool.Fori(0, RUNS) as i:
                combine(i)

        @block.tensor
        def _(pe):
            pe.wait_ge(const_loaded, 16 * 4)

            def shared(run, i):
                for x in range(2):
                    pe.wait_ge(xs_loaded[x], run * 32 + 32)
                    for m in range(MS):
                        n = x * MS + m
                        if n >= 2:
                            pe.wait_ge(s_dve.sem, s_dve.by(f"{(n - 2) // MS}a{(n - 2) % MS}", run))
                        else:
                            pe.wait_ge(s_dve.sem, s_dve.before(run))
                        for side, w in enumerate((wsg, wsu)):
                            for ct in range(KT):
                                ins = pe.matmul(gu[:, 2 * (n % 2) + side, :], w[:, ct, P * m:P * (m + 1)], xs[:, x, ct, :],
                                                start=(ct == 0), stop=(ct == KT - 1))
                        ins.then_inc(s_pe.sem, 1)
                for x in range(2):
                    for k in range(2):
                        if x or k == 0:
                            pe.wait_ge(s_dve.sem, s_dve.by(f"0o{k}" if x else f"0a{MS - 1}", run))
                        for q in range(2):
                            t = 2 * k + q
                            for ct in range(MS):
                                ins = pe.matmul(dn[:, k, C * q:C * (q + 1)], inner[:, x, ct, P * t:P * (t + 1)], wsd[:, ct],
                                                start=(ct == 0), stop=(ct == MS - 1))
                        ins.then_inc(s_pe.sem, 1)

            def expert_run(r, last):
                def turn(x):
                    pe.wait_ge(xg_loaded[x % 2], r * (ITEMS // 2 * 16) + 16 * (x // 2 + 1))
                    if x:
                        pe.wait_ge(e_act.sem, e_act.by(f"t{x - 1}", r))
                        pe.wait_ge(e_dve.sem, e_dve.by(f"t{x - 1}", r))
                    for ct in range(KT):
                        for q in range(QT):
                            ins = pe.transpose(tr[:, ct, P * q:P * (q + 1)], xg[:, x % 2, q, P * ct:P * (ct + 1)], identf[:])
                    ins.then_inc(e_pe.sem, 1)

                pe.wait_ge(e_act.sem, e_act.before(r))
                pe.wait_ge(e_dve.sem, e_dve.before(r))
                turn(0)
                for x in range(ITEMS):
                    par = x // QC
                    if x % QC == 0:
                        pe.wait_ge(w_loaded[par], r * 48 + 48)
                    pe.wait_ge(e_act.sem, e_act.by(f"t{x}", r))
                    pe.wait_ge(e_dve.sem, e_dve.by(f"t{x}", r))
                    for mt in range(KT):
                        for side, w in enumerate((weg, weu)):
                            for ct in range(KT):
                                ins = pe.matmul(gu[:, 2 * mt + side, :], w[:, par, ct, P * mt:P * (mt + 1)], xgT[:, x % 2, ct, :],
                                                start=(ct == 0), stop=(ct == KT - 1))
                        ins.then_inc(e_pe.sem, 1)
                    if x < ITEMS - 1:
                        turn(x + 1)
                    pe.wait_ge(e_dve.sem, e_dve.by(f"a{x}_1", r))
                    for k in range(2):
                        if x and k == 0:
                            pe.wait_ge(e_act.sem, e_act.by(f"o{x - 1}", r))
                        for q in range(2):
                            for ct in range(KT):
                                ins = pe.matmul(dn[:, k, C * q:C * (q + 1)], e_in[:, x % 2, ct, P * (2 * k + q):P * (2 * k + q + 1)],
                                                wed[:, par, ct], start=(ct == 0), stop=(ct == KT - 1))
                        ins.then_inc(e_pe.sem, 1)

            with pe.Fori(0, RUNS) as i:
                shared(i, i)
            pe.wait_ge(s_dve.sem, s_dve.before(RUNS))
            with pe.Fori(0, E // 2 - 1) as r:
                expert_run(r, False)
            expert_run(E // 2 - 1, True)
            pe.wait_ge(e_act.sem, e_act.before(E // 2))
            pe.wait_ge(e_dve.sem, e_dve.before(E // 2))
            with pe.Fori(0, RUNS) as i:
                shared(i + RUNS, i)

        @block.scalar
        def _(act):
            a = nc.scalar.activation

            def shared(run, i):
                for x in range(2):
                    for m in range(MS):
                        n = x * MS + m
                        act.wait_ge(s_pe.sem, s_pe.by(f"{x}g{m}", run))
                        if n >= 2:
                            act.wait_ge(s_dve.sem, s_dve.by(f"{(n - 2) // MS}a{(n - 2) % MS}", run))
                        a(sil[:, n % 2, :], gu[:, 2 * (n % 2), :], ACT.Silu).then_inc(s_act.sem, 1)

            def expert_run(r, last):
                def turn(x):
                    act.wait_ge(e_pe.sem, e_pe.by(f"t{x}", r))
                    a(xgT[:, x % 2, 0, :], tr[:, 0, :], ACT.Copy).then_inc(e_act.sem, 1)

                turn(0)
                for x in range(ITEMS):
                    for mt in range(KT):
                        act.wait_ge(e_pe.sem, e_pe.by(f"g{x}_{mt}", r))
                        if x:
                            act.wait_ge(e_dve.sem, e_dve.by(f"a{x - 1}_{mt}", r))
                        a(e_sil[:, mt, :], gu[:, 2 * mt, :], ACT.Silu).then_inc(e_act.sem, 1)
                    if x < ITEMS - 1:
                        turn(x + 1)
                    act.wait_ge(e_pe.sem, e_pe.by(f"d{x}_0", r))
                    if x >= 2:
                        act.wait_ge(eo_stored[x % 2], r * (ITEMS // 2 * 16) + 16 * (x // 2))
                    else:
                        act.wait_ge(eo_stored[x % 2], r * (ITEMS // 2 * 16))
                    a(eo[:, x % 2, 0:2].rearrange("p t c -> p (t c)"), dn[:, 0, :], ACT.Copy).then_inc(e_act.sem, 1)

            with act.Fori(0, RUNS) as i:
                shared(i, i)
            with act.Fori(0, E // 2 - 1) as r:
                expert_run(r, False)
            expert_run(E // 2 - 1, True)
            with act.Fori(0, RUNS) as i:
                shared(i + RUNS, i)

        @block.vector
        def _(dve):
            tt, stt = nc.vector.tensor_tensor, nc.vector.scalar_tensor_tensor

            def shared(run, i):
                for x in range(2):
                    for m in range(MS):
                        n = x * MS + m
                        dve.wait_ge(s_act.sem, s_act.by(f"{x}s{m}", run))
                        if n == 0:
                            dve.wait_ge(s_pe.sem, s_pe.before(run))
                        tt(inner[:, x, m, :], sil[:, n % 2, :], gu[:, 2 * (n % 2) + 1, :], ALU.mult).then_inc(s_dve.sem, 1)
                for x in range(2):
                    dve.wait_ge(xs_loaded[x], run * 32 + 32)
                    dve.wait_ge(sum_stored[x], run * 16)
                    for k in range(2):
                        dve.wait_ge(s_pe.sem, s_pe.by(f"{x}d{k}", run))
                        tt(out_s[:, x, 2 * k:2 * k + 2].rearrange("p t c -> p (t c)"), dn[:, k, :],
                           hs[:, x, 2 * k:2 * k + 2].rearrange("p t c -> p (t c)"), ALU.add).then_inc(s_dve.sem, 1)

            def expert_run(r, last):
                def turn(x):
                    dve.wait_ge(e_pe.sem, e_pe.by(f"t{x}", r))
                    nc.vector.tensor_copy(xgT[:, x % 2, 1, :], tr[:, 1, :]).then_inc(e_dve.sem, 1)

                turn(0)
                for x in range(ITEMS):
                    for mt in range(KT):
                        dve.wait_ge(e_act.sem, e_act.by(f"s{x}_{mt}", r))
                        tt(e_in[:, x % 2, mt, :], e_sil[:, mt, :], gu[:, 2 * mt + 1, :], ALU.mult).then_inc(e_dve.sem, 1)
                    if x < ITEMS - 1:
                        turn(x + 1)
                    dve.wait_ge(e_pe.sem, e_pe.by(f"d{x}_1", r))
                    dve.wait_ge(eo_stored[x % 2], r * (ITEMS // 2 * 16) + 16 * (x // 2))
                    nc.vector.tensor_copy(eo[:, x % 2, 2:4].rearrange("p t c -> p (t c)"), dn[:, 1, :]).then_inc(e_dve.sem, 1)

            def combine(i):
                nc.vector.tensor_copy(w_now[:], keep["weight"][:, bass.ds(i * RT, RT), :]).then_inc(w_ready, 1)
                dve.wait_ge(w_ready, i * 1 + 1)
                for t in range(RT):
                    k = t % RING
                    dve.wait_ge(base_loaded[k], i * (RT // RING * 16) + 16 * (t // RING + 1))
                    dve.wait_ge(gathered[k], i * (RT // RING * 32) + 32 * (t // RING + 1))
                    dve.wait_ge(out_stored[k], i * (RT // RING * 16) + 16 * (t // RING))
                    stt(out=row[:, k], in0=g_row[:, k, 0], scalar=w_now[:, t, 0:1], in1=row[:, k],
                        op0=ALU.mult, op1=ALU.add).then_inc(half_sum, 1)
                    dve.wait_ge(half_sum, i * RT + t + 1)
                    stt(out=done[:, k], in0=g_row[:, k, 1], scalar=w_now[:, t, 1:2], in1=row[:, k],
                        op0=ALU.mult, op1=ALU.add).then_inc(combined, 1)
                dve.wait_ge(combined, i * RT + RT)

            with dve.Fori(0, RUNS) as i:
                shared(i, i)
            with dve.Fori(0, E // 2 - 1) as r:
                expert_run(r, False)
            expert_run(E // 2 - 1, True)
            with dve.Fori(0, RUNS) as i:
                shared(i + RUNS, i)
                combine(i)



def tower_kernel(nc, io):
    dram = lambda name, shape, dt=F32: nc.dram_tensor(name, shape, dt).ap()
    with ExitStack() as ctx:
        sb = lambda name, shape, dt=F32: ctx.enter_context(nc.sbuf_tensor(name, shape, dt))
        keep = {
            "emb": dram("emb_rows", [N, DIM]), "h": dram("h_rows", [N, C]), "h2": dram("h2_rows", [N, C]),
            "x2": dram("x2_rows", [N, C]), "x2T": dram("x2_cols", [P, KT, N]),
            "parts": dram("qk_parts", [B, 2, PARTS, 2, P, T], BF16),
            "max": dram("max_parts", [UNITS, PARTS, UH * TILES, P], BF16),
            "logits": dram("logits", [B, P, TILES, E]), "queue": dram("queues", [E * CAP, C]),
            "expert_out": dram("expert_out", [E * CAP, C]), "sum": dram("shared_sum", [N, C]),
            "w_qk": sb("w_qk", [P, KT, 2, 3, P]), "w_v": sb("w_v", [P, KT, C]),
            "scatter": sb("scatter_idx", [P, ALLT, TOPK], U32), "gather": sb("gather_idx", [P, ALLT, TOPK], U32),
            "weight": sb("weight", [P, ALLT, TOPK]),
        }
        prepare(nc, io, keep)
        towers(nc, io, keep)
        route(nc, io, keep)
        experts(nc, io, keep)


def constants():
    f = np.float32
    inv = f(1.0) / (f(10000.0) ** (np.arange(0, HALF, 2, dtype=f) / f(HALF)))
    freqs = np.arange(T, dtype=f)[:, None] * inv[None, :]
    angle = np.concatenate((freqs, freqs), axis=-1)
    cols = lambda a: np.ascontiguousarray(np.tile(a.T, (H, 1)).astype(f))
    at = np.arange(P)
    return {
        "cos": cols(np.cos(angle)), "sin": cols(np.sin(angle)),
        "identity": np.eye(P, dtype=f),
        "mask": np.where(at[None, :] > at[:, None], MASKED, 0.0).astype(f),
        "before": (at[:, None] < at[None, :]).astype(f), "ones": np.ones((P, P), f),
        "first": np.ascontiguousarray(np.broadcast_to(np.arange(E, 0, -1, dtype=f), (P, ALLT, E))),
        "start": np.ascontiguousarray(np.broadcast_to(np.arange(E, dtype=f) * CAP, (P, ALLT, E))),
    }


def layouts(a):
    flat = np.asarray(a["x"]).reshape(-1)
    before = np.concatenate([flat[:1], flat[:-1]])
    t = lambda x, *axes: np.ascontiguousarray(np.transpose(np.asarray(x), axes or None))
    side = lambda *x: np.ascontiguousarray(np.concatenate([np.asarray(v) for v in x], axis=1))
    return {
        "ids": side(flat.reshape(ALLT, P), before.reshape(ALLT, P)),
        "embed": np.asarray(a["L0_tok_embed"]), "proj_t": t(a["L0_tok_proj_w"]),
        "scale": np.ascontiguousarray(np.broadcast_to(np.asarray(a["L0_tok_scale"]), (P, 1))),
        "down_q": t(a["L0_attn_Wq_down"]), "down_k": t(a["L0_attn_Wk_down"]), "down_v": t(a["L0_attn_Wv_down"]),
        "up_q": side(a["L0_attn_Wq_up_c"], a["L0_attn_Wq_up_e"]), "up_k": side(a["L0_attn_Wk_up_c"], a["L0_attn_Wk_up_e"]),
        "up_v": np.asarray(a["L0_attn_Wv_up"]), "w_out": np.asarray(a["L0_attn_Wc"]),
        "gate_t": t(a["L0_ffn_gate_w"]),
        "we_gate": t(a["L0_ffn_we_gate"], 0, 2, 1), "we_up": t(a["L0_ffn_we_up"], 0, 2, 1),
        "we_down": t(a["L0_ffn_we_down"], 0, 2, 1),
        "ws_gate": t(a["L0_ffn_ws_gate"]), "ws_up": t(a["L0_ffn_ws_up"]), "ws_down": t(a["L0_ffn_ws_down"]),
    }


def kernel(**inputs):
    import concourse.bacc as bacc
    from concourse.bass_utils import run_bass_kernel_spmd

    nc = bacc.Bacc("TRN2", target_bir_lowering=False, num_devices=1)
    arrays = {f"in_{k}": v for k, v in {**layouts(inputs), **constants()}.items()}
    io = {k[3:]: nc.dram_tensor(k, v.shape, mybir.dt.from_np(v.dtype), kind="ExternalInput").ap() for k, v in arrays.items()}
    io["out"] = nc.dram_tensor("out", (N, C), F32, kind="ExternalOutput").ap()
    tower_kernel(nc, io)
    r = run_bass_kernel_spmd(nc, [arrays], core_ids=[0])
    return r.results[0]["out"].reshape(B, T, C)
```

```python
from contextlib import ExitStack

import numpy as np

import concourse.bass as bass
from concourse import mybir

ALU = mybir.AluOpType
ACT = mybir.ActivationFunctionType
AX = mybir.AxisListType
F32 = mybir.dt.float32
BF16 = mybir.dt.bfloat16
I32 = mybir.dt.int32
U32 = mybir.dt.uint32

P = 128
BANK = 512
B, T, C = 8, 1024, 256
N = B * T
DIM = 64
H, DH, HALF = 16, 16, 8
LAT = 64
KT = C // P
TILES = T // P
ALLT = N // P
HASH_MOD = 65535
MUL_CUR, MUL_PREV = 36313, 27191
EPS = 1e-5
UH = 4
UB = H // UH
UNITS = B * UB
PARTS = 3
AUG = 6 * DH
VW = DH + 1
E, EI, TOPK = 8, 256, 2
CAP = 2560
SH = 512
CH = 512
QC = CAP // CH
FILL = E * CAP // UNITS
MASKED = -1e30

assert CAP == -(-5 * N * TOPK // (4 * E))


class Steps:

    def __init__(self, sem, names, free=1):
        self.sem, self.free, self.per = sem, free, len(names)
        self.at = {name: n + 1 for n, name in enumerate(names)}
        assert len(self.at) == self.per

    def by(self, name, run=0):
        return run * self.per + (self.at[name] + self.free)

    def before(self, run):
        return run * self.per + self.free

    def end(self, run=0):
        return run * self.per + (self.per + self.free)


class Moves:

    def __init__(self, sem, per=1, free=1):
        self.sem, self.per, self.free = sem, per, free

    def by(self, run, n=None):
        return run * (16 * self.per) + 16 * (self.free + (self.per if n is None else n))

    def before(self, run):
        return self.by(run, 0)



def prepare(nc, io, keep):
    with ExitStack() as ctx:
        sb = lambda name, shape, dt=F32: ctx.enter_context(nc.sbuf_tensor(name, shape, dt))
        sem = lambda name: ctx.enter_context(nc.semaphore(name))
        R = ALLT
        ids = sb("ids", [R, 2 * P], I32)
        ia, ib, ic, id_ = (sb(f"hash_{n}", [R, 2 * P], I32) for n in "abcd")
        hashed = sb("hashed", [R, P])
        hash_f = sb("hash_f", [R, P])
        index = keep["index"]
        identf = sb("identf_p", [P, P])
        down_t = sb("down_t", [P, 3, H // 2, C])
        up = sb("up", [P, 3, 2, 3 * HALF])
        ps = ctx.enter_context(nc.psum_tensor("ps_prepare", [P, 8, BANK], F32))
        loaded, up_loaded, down_loaded = sem("ids_loaded"), sem("up_loaded"), sem("down_loaded")
        up_zero, up_rot, chain = sem("up_zero"), sem("up_rot"), sem("hash_chain")
        index_t = sem("index_t")
        eff_made, eff_kept = sem("eff_made"), sem("eff_kept")
        block = ctx.enter_context(nc.Block())

        @block.sync
        def _(sp):
            sp.dma_start(ids[:], io["ids"]).then_inc(loaded, 16)
            sp.dma_start(identf[:], io["identity"]).then_inc(loaded, 16)
            sp.wait_ge(up_zero, 1)
            for m, w in enumerate(("up_q", "up_k", "up_v")):
                for half in range(2):
                    sp.dma_start(up[LAT * half:LAT * (half + 1), m, half, 0:DH], io[w]).then_inc(up_loaded, 16)
            for m, w in enumerate(("down_q", "down_k", "down_v")):
                sp.dma_start(down_t[:, m], io[w].rearrange("(g p) c -> p g c", p=P)).then_inc(down_loaded, 16)
        @block.vector
        def _(dve):
            steps = [0]

            def link(ins):
                steps[0] += 1
                ins.then_inc(chain, 1)
                dve.wait_ge(chain, steps[0])

            ts = nc.vector.tensor_scalar
            tt = nc.vector.tensor_tensor
            nc.vector.memset(up[:], 0.0).then_inc(up_zero, 1)
            dve.wait_ge(loaded, 32)
            halves = ((slice(0, P), MUL_CUR), (slice(P, 2 * P), MUL_PREV))
            link(ts(ia[:], ids[:], 8, None, ALU.logical_shift_right))
            link(ts(ib[:], ids[:], 255, None, ALU.bitwise_and))
            for cols, mul in halves:
                link(ts(ia[:, cols], ia[:, cols], float(mul), None, ALU.mult))
                link(ts(ib[:, cols], ib[:, cols], float(mul), None, ALU.mult))
            link(ts(ic[:], ia[:], 255, 8, ALU.bitwise_and, ALU.logical_shift_left))
            link(ts(id_[:], ib[:], 65535, None, ALU.bitwise_and))
            link(tt(ic[:], ic[:], id_[:], ALU.add))
            link(ts(ia[:], ia[:], 8, None, ALU.logical_shift_right))
            link(ts(ib[:], ib[:], 16, None, ALU.logical_shift_right))
            link(tt(ia[:], ia[:], ib[:], ALU.add))
            link(ts(ib[:], ic[:], 16, None, ALU.logical_shift_right))
            link(tt(ia[:], ia[:], ib[:], ALU.add))
            link(ts(ic[:], ic[:], 65535, None, ALU.bitwise_and))
            link(tt(ia[:, 0:P], ia[:, 0:P], ia[:, P:2 * P], ALU.bitwise_xor))
            link(tt(ic[:, 0:P], ic[:, 0:P], ic[:, P:2 * P], ALU.bitwise_xor))
            link(ts(ib[:, 0:P], ia[:, 0:P], 15, None, ALU.logical_shift_right))
            link(tt(ia[:, 0:P], ia[:, 0:P], ic[:, 0:P], ALU.add))
            link(tt(ia[:, 0:P], ia[:, 0:P], ib[:, 0:P], ALU.subtract))
            link(ts(ib[:, 0:P], ia[:, 0:P], 16, None, ALU.logical_shift_right))
            link(ts(ic[:, 0:P], ia[:, 0:P], 65535, None, ALU.bitwise_and))
            link(tt(ia[:, 0:P], ib[:, 0:P], ic[:, 0:P], ALU.add))
            link(nc.vector.tensor_copy(hashed[:], ia[:, 0:P]))
            link(ts(hash_f[:], hashed[:], float(HASH_MOD), -float(HASH_MOD), ALU.is_ge, ALU.mult))
            link(tt(hashed[:], hashed[:], hash_f[:], ALU.add))
            dve.wait_ge(index_t, 1)
            link(nc.vector.tensor_copy(index[:], ps[:, 0, 0:R]))
            link(nc.vector.memset(index[0:1, 0:R:TILES], HASH_MOD))

            dve.wait_ge(up_loaded, 16 * 6)
            for m in range(2):
                for half in range(2):
                    at = up[LAT * half:LAT * (half + 1), m, half]
                    ts(at[:, DH:DH + HALF:2], at[:, HALF + 1:DH:2], -1.0, None, ALU.mult).then_inc(up_rot, 1)
                    nc.vector.tensor_copy(at[:, DH + 1:DH + HALF:2], at[:, HALF:DH:2]).then_inc(up_rot, 1)
            for m in range(3):
                for ct in range(KT):
                    for g in range(H // 2):
                        n = (m * KT + ct) * (H // 2) + g
                        dve.wait_ge(eff_made, n + 1)
                        src = ps[:, 1 + n % 7, 0:2 * 3 * HALF].rearrange("p (h y d) -> p h y d", h=2, d=HALF)
                        if m < 2:
                            dst = keep["w_qk"][:, ct, m].rearrange("p y (d h) -> p h y d", d=HALF)[:, 2 * g:2 * g + 2]
                            ts(dst, src, DH ** -0.5 if m == 0 else 1.0, None, ALU.mult).then_inc(eff_kept, 1)
                        else:
                            dst = keep["w_v"][:, ct, 2 * DH * g:2 * DH * (g + 1)].rearrange("p (h y d) -> p h y d", h=2, d=HALF)
                            nc.vector.tensor_copy(dst, src[:, :, 0:2, :]).then_inc(eff_kept, 1)

        @block.tensor
        def _(pe):
            pe.wait_ge(chain, 26)
            pe.transpose(ps[:, 0, 0:R], hashed[:], identf[0:R, 0:R]).then_inc(index_t, 1)
            pe.wait_ge(down_loaded, 16 * 3)
            pe.wait_ge(up_rot, 8)
            for m in range(3):
                for ct in range(KT):
                    for g in range(H // 2):
                        n = (m * KT + ct) * (H // 2) + g
                        if n >= 7:
                            pe.wait_ge(eff_kept, n - 6)
                        pe.matmul(ps[:, 1 + n % 7, 0:2 * 3 * HALF], down_t[:, m, g, P * ct:P * (ct + 1)],
                                  up[:, m].rearrange("p a b -> p (a b)"), start=True, stop=True).then_inc(eff_made, 1)



MAX_BLOCKS = [(i, 0, min(BANK, P * (i + 1))) for i in range(TILES)] + \
             [(i, BANK, P * (i + 1) - BANK) for i in range(BANK // P, TILES)]
MAXES = UH * len(MAX_BLOCKS)
STEPS = [(c, j) for c in range(2) for j in range(4 * (c + 1))]
NS = len(STEPS)
DIAG = [s for s, (c, j) in enumerate(STEPS) if j >= 4 * c]
PLAIN = [s for s in range(NS) if s not in DIAG]
LAST_OF = {s: c for s, (c, j) in enumerate(STEPS) if j == 4 * (c + 1) - 1}
MAX_PER = MAXES // NS
assert MAX_PER * NS == MAXES and MAX_PER == 4


def alone(eng, sem, value, waited):
    eng.wait_ge(sem, value)
    if not isinstance(value, int):
        eng.sem_inc(waited, 1)


def at_first(x):
    return isinstance(x, int) and x == 0


def towers(nc, io, keep):
    with ExitStack() as ctx:
        sb = lambda name, shape, dt=F32: ctx.enter_context(nc.sbuf_tensor(name, shape, dt))
        sem = lambda name: ctx.enter_context(nc.semaphore(name))

        st = ctx.enter_context(nc.psum_tensor("st", [P, 4, BANK], F32))
        sm = ctx.enter_context(nc.psum_tensor("sm", [P, 3, BANK], F32))
        pv = ctx.enter_context(nc.psum_tensor("pv", [P, BANK], F32))

        identf, maskf = sb("identf", [P, P]), sb("maskf", [P, P])
        identb, maskb = sb("identb", [P, P], BF16), sb("maskb", [P, P], BF16)
        proj, scale = sb("proj", [P, C]), sb("scale", [P, 1])
        w_out, w_gate = sb("w_out", [P, KT, C]), sb("w_gate", [P, KT, E])
        cos, sin = sb("cos", [P, T]), sb("sin", [P, T])
        emb = sb("emb", [P, TILES, P])
        h = sb("h", [P, TILES, C])
        x2 = sb("x2", [P, TILES, C])
        stats, mv = sb("stats", [P, TILES, 6]), sb("mv", [P, TILES, 2])
        var, lnv, rstd, tmp = (sb(n, [P, TILES]) for n in ("var", "lnv", "rstd", "tmp"))
        big = sb("big", [P, 4, T])
        xn = big[:, 0:2].rearrange("p a t -> p (a t)").rearrange("p (t c) -> p t c", c=C)
        xnT = big[:, 2:4]
        yT_raw = big
        small = sb("small", [P, TILES * C])
        embT = small[:, 0:T]
        y = small[:].rearrange("p (t c) -> p t c", c=C)
        yT = sb("yT", [P, KT, T])
        parts = sb("parts", [P, 2, 2, PARTS, BANK], BF16)
        res = sb("res", [P, 2, BANK])
        rot_a, rot_b, rot_c = sb("rot_a", [P, BANK]), sb("rot_b", [P, BANK]), sb("rot_c", [P, BANK])
        v_next = sb("v_next", [P, TILES, H, DH])
        v = sb("v", [P, TILES, H * VW + DH])
        qa, ka = sb("qa", [P, UB, UH, T], BF16), sb("ka", [P, UB, UH, T], BF16)
        prob = sb("prob", [P, 4, 2, BANK])
        mx = sb("mx", [P, UH, len(MAX_BLOCKS)])
        nmax = sb("nmax", [P, UH, TILES])
        m_parts, m_res = sb("m_parts", [UH * TILES, PARTS, P], BF16), sb("m_res", [UH * TILES, P])
        rden = sb("rden", [P, 2, H])
        lg_sb = sb("lg_sb", [P, TILES, E])
        row_of = sb("row_of", [P, TILES], U32)
        zero = sb("zero", [P, FILL // P, C])

        qk = [f"{a}{s}" for s in range(4) for a in ("c", "e", "r")]
        f_pe = Steps(sem("front_pe"), ["et0", "et1", "h0", "h1", "h2", "h3", "x0", "x1", "x2", "x3"] + qk
                     + [f"v{k}" for k in range(4)])
        f_act = Steps(sem("front_act"), ["et0", "et1", "h0", "h1", "h2", "h3", "ln", "rs", "x0", "x2"]
                      + [f"{a}{s}" for s in range(4) for a in ("hc", "he")] + [f"v{k}" for k in range(4)])
        norm_steps = [f"st{t}" for t in range(TILES)] + [f"ag{t}" for t in range(TILES)] + ["var", "n1", "n2", "n3", "n4"] \
            + [f"xn{t}" for t in range(TILES)]
        f_dve = Steps(sem("front_dve"), norm_steps + ["x1", "x3"]
                      + [f"{a}{s}" for s in range(4) for a in ("rc", "t1", "t2", "qe", "re")])
        f_pool = Steps(sem("front_pool"), [f"{a}{s}" for s in range(4) for a in ("mc", "lc", "me", "le")])
        emb_loaded = Moves(sem("emb_loaded"), TILES, free=0)
        row_of_ready = Steps(sem("row_of_ready"), ["copied"])
        h_stored = Moves(sem("h_stored"))
        parts_stored = [Moves(sem("q_parts_stored"), 4), Moves(sem("k_parts_stored"), 4)]
        v_moved = Steps(sem("v_moved"), ["0", "1"])
        aug_loaded = [Moves(sem(f"aug{q}_loaded"), 9) for q in range(UB)]
        m_pe = Steps(sem("max_pe"), [f"m{k}" for k in range(MAXES)] + ["t"])
        m_dve = Steps(sem("max_dve"), [f"m{k}" for k in range(MAXES)] + ["cp", "mn", "hi", "res", "mid", "lo"])
        m_stored, m_loaded = Moves(sem("m_stored")), Moves(sem("m_loaded"))
        zeroed = Moves(sem("queues_zeroed"), UNITS)
        a_st = Steps(sem("scores"), [f"{n}" for n in range(2 * NS)])
        a_exp = Steps(sem("exps"), [f"{n}" for n in range(2 * NS)], free=2)
        a_mask = Steps(sem("masked"), [f"{2 * s + p}" for s in DIAG for p in range(2)])
        a_pv = Steps(sem("summed"), [f"{s}" for s in range(NS)], free=2)
        a_out = Steps(sem("sums_kept"), ["0", "1"])
        b_pe = Steps(sem("back_pe"), [f"yt{t}" for t in range(TILES)] + [f"z{n}" for n in range(4)]
                     + [f"w{k}" for k in range(4)] + [f"p{n}" for n in range(4)] + ["gate"])
        b_act = Steps(sem("back_act"), ["z0", "z2", "ln", "rs", "p0", "p2"])
        b_dve = Steps(sem("back_dve"), [f"{a}{t}" for t in range(TILES) for a in ("rc", "y")] + ["z1", "z3"]
                      + [f"a{k}" for k in range(4)] + norm_steps + ["p1", "p3", "gate"])
        h_loaded, h2_stored, x2_stored, x2T_stored, lg_stored = (Moves(sem(n)) for n in (
            "h_loaded", "h2_stored", "x2_stored", "x2T_stored", "lg_stored"))
        const_loaded, const_made = sem("const_loaded"), sem("const_made")
        waited_sp, waited_pool, waited_dve, waited_pe = (sem(f"waited_{n}") for n in ("sp", "pool", "dve", "pe"))

        block = ctx.enter_context(nc.Block())

        def in_order(eng, front, maxima, attend, back1, back2):
            front(0)
            maxima()
            front(1)

            def batch(b, left):
                for q in range(UB):
                    attend(UB * b + q, b, q, UB - 1 - q + UB * left)
                back1(b, left > 0)
                if left > 1:
                    front(b + 2)
                back2(b, left > 1)

            with eng.Fori(0, B - 2) as b:
                batch(b, 2)
            batch(B - 2, 1)
            batch(B - 1, 0)

        @block.sync
        def _(sp):
            for dst, src in ((identf[:], io["identity"]), (maskf[:], io["mask"]), (proj[0:DIM, :], io["proj_t"]),
                             (scale[:], io["scale"]), (w_out[:], io["w_out"].rearrange("(k p) c -> p k c", p=P)),
                             (w_gate[:], io["gate_t"].rearrange("(k p) e -> p k e", p=P)),
                             (cos[:], io["cos"]), (sin[:], io["sin"])):
                sp.dma_start(dst, src).then_inc(const_loaded, 16)
            sp.wait_ge(const_made, 4)

            for m in (h_stored, *parts_stored, *aug_loaded, m_stored, m_loaded, zeroed,
                      h_loaded, h2_stored, x2_stored, x2T_stored, lg_stored):
                sp.sem_inc(m.sem, 16)

            def front(b):
                alone(sp, f_act.sem, f_act.by("h3", b), waited_sp)
                sp.dma_start(keep["h"].rearrange("(b t p) c -> b p t c", p=P, t=TILES)[b], h[:]).then_inc(h_stored.sem, 16)
                for s in range(4):
                    c, side = divmod(s, 2)
                    alone(sp, f_pool.sem, f_pool.by(f"le{s}", b), waited_sp)
                    alone(sp, f_act.sem, f_act.by(f"he{s}", b), waited_sp)
                    for y_ in range(2):
                        sp.dma_start(
                            keep["parts"][b, side, :, y_, :, BANK * c:BANK * (c + 1)].rearrange("p r t -> r p t"),
                            parts[:, side, y_]).then_inc(parts_stored[side].sem, 16)

            def load_aug(b, q):
                for side in range(2):
                    alone(sp, parts_stored[side].sem, parts_stored[side].by(b), waited_sp)
                heads = slice(UH * q, UH * (q + 1))
                features = [keep["parts"][b, side].rearrange("part y (d h) t -> (part y d) h t", h=H) for side in range(2)]
                for r0, n in ((0, 3), (3, 2), (5, 1)):
                    sp.dma_start(qa[DH * r0:DH * (r0 + n), q], features[0][0:DH * n, heads]).then_inc(aug_loaded[q].sem, 16)
                for r0, part in enumerate((0, 0, 0, 1, 1, 2)):
                    sp.dma_start(ka[DH * r0:DH * (r0 + 1), q], features[1][DH * part:DH * (part + 1), heads]
                                 ).then_inc(aug_loaded[q].sem, 16)

            def move_max(u, q):
                alone(sp, m_dve.sem, m_dve.by("lo", u), waited_sp)
                sp.dma_start(keep["max"][u].rearrange("p r q -> r p q"), m_parts[:]).then_inc(m_stored.sem, 16)
                alone(sp, m_stored.sem, m_stored.by(u), waited_sp)
                sp.dma_start(qa[AUG:AUG + PARTS, q].rearrange("p h t -> p (h t)"),
                             keep["max"][u].rearrange("p r q -> p (r q)")).then_inc(m_loaded.sem, 16)

            def maxima():
                for q in range(3):
                    load_aug(0, q)
                move_max(0, 0)

            def attend(u, b, q, left):
                alone(sp, a_st.sem, a_st.before(u), waited_sp)
                if left >= 3:
                    load_aug(b + (q + 3) // UB, (q + 3) % UB)
                if left:
                    move_max(u + 1, (q + 1) % UB)
                if q == 0:
                    if left >= UB:
                        alone(sp, f_dve.sem, f_dve.by("xn7", b + 1), waited_sp)
                        alone(sp, h_stored.sem, h_stored.by(b + 1), waited_sp)
                    else:
                        alone(sp, b_dve.sem, b_dve.by("xn7", b - 1), waited_sp)
                        alone(sp, h2_stored.sem, h2_stored.by(b - 1), waited_sp)
                    sp.dma_start(h[:], keep["h"].rearrange("(b t p) c -> b p t c", p=P, t=TILES)[b]).then_inc(h_loaded.sem, 16)
                sp.dma_start(keep["queue"].rearrange("(n p r) c -> n p r c", p=P, r=FILL // P)[u], zero[:]).then_inc(zeroed.sem, 16)

            def back1(b, more):
                alone(sp, b_dve.sem, b_dve.by("a3", b), waited_sp)
                sp.dma_start(keep["h2"].rearrange("(b t p) c -> b p t c", p=P, t=TILES)[b], h[:]).then_inc(h2_stored.sem, 16)
                alone(sp, b_dve.sem, b_dve.by("xn7", b), waited_sp)
                sp.dma_start(keep["x2"].rearrange("(b t p) c -> b p t c", p=P, t=TILES)[b], x2[:]).then_inc(x2_stored.sem, 16)

            def back2(b, ahead):
                alone(sp, b_act.sem, b_act.by("p2", b), waited_sp)
                alone(sp, b_dve.sem, b_dve.by("p3", b), waited_sp)
                sp.dma_start(keep["x2T"].rearrange("p k (b t) -> b p k t", t=T)[b], xnT).then_inc(x2T_stored.sem, 16)
                alone(sp, b_dve.sem, b_dve.by("gate", b), waited_sp)
                sp.dma_start(keep["logits"][b], lg_sb[:]).then_inc(lg_stored.sem, 16)

            in_order(sp, front, maxima, attend, back1, back2)
            for m in (h_stored, h2_stored, x2_stored, x2T_stored, lg_stored):
                alone(sp, m.sem, m.by(B - 1), waited_sp)
            alone(sp, zeroed.sem, zeroed.by(0), waited_sp)

        @block.tensor
        def _(pe):
            pe.wait_ge(const_loaded, 16 * 8)
            pe.wait_ge(const_made, 9)
            for steps in (f_pe, m_pe, a_st, a_pv, b_pe):
                pe.sem_inc(steps.sem, steps.free)

            def front(b):
                pe.wait_ge(emb_loaded.sem, emb_loaded.by(b))
                if isinstance(b, int) and b == 1:
                    pe.wait_ge(f_act.sem, f_act.end(0))
                elif not at_first(b):
                    pe.wait_ge(b_dve.sem, b_dve.by("a3", b - 2))
                for half in range(2):
                    for q in range(4):
                        ins = pe.transpose(st[:, half, P * q:P * (q + 1)], emb[:, 4 * half + q, :], identf[:])
                    ins.then_inc(f_pe.sem, 1)
                for k, bank in enumerate((2, 3, 0, 1)):
                    pe.wait_ge(f_act.sem, f_act.by("et0" if k < 2 else "et1", b))
                    for q in range(2):
                        t = 2 * k + q
                        ins = pe.matmul(st[:, bank, C * q:C * (q + 1)], embT[:, P * t:P * (t + 1)], proj[:],
                                        start=True, stop=True)
                    ins.then_inc(f_pe.sem, 1)
                for ct in range(KT):
                    for half in range(2):
                        for q in range(4):
                            t = 4 * half + q
                            pe.wait_ge(f_dve.sem, f_dve.by(f"xn{t}", b))
                            ins = pe.transpose(st[:, 2 * ct + half, P * q:P * (q + 1)], xn[:, t, P * ct:P * (ct + 1)], identf[:])
                        ins.then_inc(f_pe.sem, 1)
                pe.wait_ge(f_act.sem, f_act.by("x2", b))
                pe.wait_ge(f_dve.sem, f_dve.by("x3", b))
                readers = ("rc", "t1", "t2")
                for s in range(4):
                    c, side = divmod(s, 2)
                    for k in range(3):
                        n = 3 * s + k
                        if n >= 4:
                            pe.wait_ge(f_dve.sem, f_dve.by(f"{readers[(n - 4) % 3]}{(n - 4) // 3}", b))
                        for ct in range(KT):
                            ins = pe.matmul(st[:, n % 4, :], keep["w_qk"][:, ct, side, k], xnT[:, ct, BANK * c:BANK * (c + 1)],
                                            start=(ct == 0), stop=(ct == KT - 1))
                        ins.then_inc(f_pe.sem, 1)
                for k in range(4):
                    n = 8 + k
                    pe.wait_ge(f_dve.sem, f_dve.by(f"{readers[n % 3]}{n // 3}", b))
                    for q in range(2):
                        t = 2 * k + q
                        for ct in range(KT):
                            ins = pe.matmul(st[:, k, C * q:C * (q + 1)], xnT[:, ct, P * t:P * (t + 1)], keep["w_v"][:, ct],
                                            start=(ct == 0), stop=(ct == KT - 1))
                    ins.then_inc(f_pe.sem, 1)

            def max_block(u, slot, k):
                hh, (i, k0, w) = k // len(MAX_BLOCKS), MAX_BLOCKS[k % len(MAX_BLOCKS)]
                if k >= 3:
                    pe.wait_ge(m_dve.sem, m_dve.by(f"m{k - 3}", u))
                elif k == 0 and not at_first(u):
                    pe.wait_ge(m_dve.sem, m_dve.by("res", u - 1))
                diag = k0 + w == P * (i + 1)
                ins = pe.matmul(sm[:, k % 3, 0:w], qa[0:AUG, slot, hh, P * i:P * (i + 1)], ka[0:AUG, slot, hh, k0:k0 + w],
                                start=True, stop=not diag)
                if diag:
                    ins = pe.matmul(sm[:, k % 3, w - P:w], identb[:], maskb[:], start=False, stop=True)
                ins.then_inc(m_pe.sem, 1)

            def max_turn(u):
                alone(pe, m_dve.sem, m_dve.by("mn", u), waited_pe)
                pe.transpose(sm[0:UH * TILES, 0, 0:P], nmax[:].rearrange("p h t -> p (h t)"), identf[:]).then_inc(m_pe.sem, 1)

            def maxima():
                for u in range(2):
                    pe.wait_ge(aug_loaded[u].sem, aug_loaded[u].by(0))
                    for k in range(MAXES):
                        max_block(u, u, k)
                    if u == 0:
                        max_turn(0)

            def attend(u, b, q, left):
                pe.wait_ge(m_loaded.sem, m_loaded.by(u))
                if q == 0:
                    pe.wait_ge(v_moved.sem, v_moved.end(b))
                    if left >= UB:
                        pe.wait_ge(f_act.sem, f_act.end(b + 1))
                    if not at_first(b):
                        pe.wait_ge(b_dve.sem, b_dve.before(b))

                def scores(s, p):
                    c, j = STEPS[s]
                    off = max(0, P * j - BANK * c)
                    n = 2 * s + p
                    pe.wait_ge(a_exp.sem, a_exp.by(str(n), u) - 2)
                    for x in range(2):
                        hh = 2 * p + x
                        ins = pe.matmul(st[:, hh, off:BANK], ka[0:AUG + PARTS, q, hh, P * j:P * (j + 1)],
                                        qa[0:AUG + PARTS, q, hh, BANK * c + off:BANK * (c + 1)], start=True, stop=True)
                    ins.then_inc(a_st.sem, 1)

                def sums(s):
                    c, j = STEPS[s]
                    off = max(0, P * j - BANK * c)
                    if j == 0:
                        pe.wait_ge(a_out.sem, a_out.by(str(c), u) - 1)
                    if s in DIAG:
                        pe.wait_ge(a_mask.sem, a_mask.by(str(2 * s + 1), u))
                    else:
                        pe.wait_ge(a_exp.sem, a_exp.by(str(2 * s + 1), u))
                    for x in range(UH):
                        hh = UH * q + x
                        ins = pe.matmul(pv[32 * x:32 * (x + 1), off:BANK], v[:, j, VW * hh:VW * hh + 32],
                                        prob[:, (2 * s + x // 2) % 4, x % 2, off:BANK],
                                        start=(j == 0), stop=(j == 4 * (c + 1) - 1))
                    ins.then_inc(a_pv.sem, 1)

                if left >= 2:
                    slot = (q + 2) % UB
                    pe.wait_ge(aug_loaded[slot].sem, aug_loaded[slot].by(b + (q + 2) // UB))
                for s in range(NS):
                    blocks = [k for k in range(MAX_PER * s, MAX_PER * (s + 1)) if left >= 2]
                    for p in range(2):
                        scores(s, p)
                        if s == p == 0 and left:
                            max_turn(u + 1)
                        for k in blocks[p:p + 1]:
                            max_block(u + 2, (q + 2) % UB, k)
                    if s:
                        sums(s - 1)
                    for k in blocks[2:]:
                        max_block(u + 2, (q + 2) % UB, k)
                sums(NS - 1)

            def back1(b, more):
                pe.wait_ge(a_out.sem, a_out.before(UB * b + UB))
                pe.wait_ge(a_exp.sem, a_exp.before(UB * b + UB))
                for t in range(TILES):
                    if t >= 4:
                        pe.wait_ge(b_dve.sem, b_dve.by(f"y{t - 4}", b))
                    for g in range(4):
                        ins = pe.transpose(st[:, t % 4, P * g:P * (g + 1)], yT_raw[:, g, P * t:P * (t + 1)], identf[:])
                    ins.then_inc(b_pe.sem, 1)
                for n in range(4):
                    half, ct = divmod(n, 2)
                    pe.wait_ge(b_dve.sem, b_dve.by(f"y{4 + n if n < 2 else 7}", b))
                    for q in range(4):
                        ins = pe.transpose(st[:, n, P * q:P * (q + 1)], y[:, 4 * half + q, P * ct:P * (ct + 1)], identf[:])
                    ins.then_inc(b_pe.sem, 1)
                pe.wait_ge(b_act.sem, b_act.by("z2", b))
                pe.wait_ge(b_dve.sem, b_dve.by("z3", b))
                for k in range(4):
                    for q in range(2):
                        t = 2 * k + q
                        for ct in range(KT):
                            ins = pe.matmul(st[:, k, C * q:C * (q + 1)], yT[:, ct, P * t:P * (t + 1)], w_out[:, ct],
                                            start=(ct == 0), stop=(ct == KT - 1))
                    ins.then_inc(b_pe.sem, 1)

            def back2(b, ahead):
                if ahead:
                    pe.wait_ge(f_act.sem, f_act.end(b + 2))
                pe.wait_ge(b_dve.sem, b_dve.by("xn7", b))
                for n in range(4):
                    half, ct = divmod(n, 2)
                    for q in range(4):
                        ins = pe.transpose(st[:, n, P * q:P * (q + 1)], x2[:, 4 * half + q, P * ct:P * (ct + 1)], identf[:])
                    ins.then_inc(b_pe.sem, 1)
                pe.wait_ge(b_act.sem, b_act.by("p2", b))
                pe.wait_ge(b_dve.sem, b_dve.by("p3", b))
                for t in range(TILES):
                    for ct in range(KT):
                        ins = pe.matmul(st[:, 0, E * t:E * (t + 1)], xnT[:, ct, P * t:P * (t + 1)], w_gate[:, ct],
                                        start=(ct == 0), stop=(ct == KT - 1))
                ins.then_inc(b_pe.sem, 1)

            in_order(pe, front, maxima, attend, back1, back2)

        @block.scalar
        def _(act):
            a = nc.scalar.activation
            act.wait_ge(const_loaded, 16 * 8)
            for steps in (f_act, a_exp, b_act):
                act.sem_inc(steps.sem, steps.free)

            def front(b):
                for k in range(2):
                    act.wait_ge(f_pe.sem, f_pe.by(f"et{k}", b))
                    if k == 0 and not (isinstance(b, int) and b < 2):
                        act.wait_ge(b_pe.sem, b_pe.by("z3", b - 2))
                    a(embT[:, BANK * k:BANK * (k + 1)], st[:, k, :], ACT.Copy).then_inc(f_act.sem, 1)
                if isinstance(b, int) and b == 1:
                    act.wait_ge(f_dve.sem, f_dve.by("xn7", 0))
                    act.wait_ge(h_stored.sem, h_stored.by(0))
                elif not at_first(b):
                    act.wait_ge(b_dve.sem, b_dve.by("xn7", b - 2))
                    act.wait_ge(h2_stored.sem, h2_stored.by(b - 2))
                for k, bank in enumerate((2, 3, 0, 1)):
                    act.wait_ge(f_pe.sem, f_pe.by(f"h{k}", b))
                    a(h[:, 2 * k:2 * k + 2, :].rearrange("p t c -> p (t c)"), st[:, bank, :], ACT.Identity,
                      scale=scale[:, 0:1]).then_inc(f_act.sem, 1)
                rsqrt(f_dve, f_act, b)
                for k in (0, 2):
                    act.wait_ge(f_pe.sem, f_pe.by(f"x{k}", b))
                    a(xnT[:, k // 2, 0:BANK], st[:, k, :], ACT.Copy).then_inc(f_act.sem, 1)
                for s in range(4):
                    c, side = divmod(s, 2)
                    act.wait_ge(parts_stored[side].sem, parts_stored[side].by(b, 2 * (s // 2)))
                    act.wait_ge(f_pe.sem, f_pe.by(f"c{s}", b))
                    a(parts[:, side, 0, 0, :], st[:, 3 * s % 4, :], ACT.Copy).then_inc(f_act.sem, 1)
                    act.wait_ge(f_dve.sem, f_dve.by(f"qe{s}", b))
                    a(parts[:, side, 1, 0, :], rot_c[:], ACT.Copy).then_inc(f_act.sem, 1)
                act.wait_ge(v_moved.sem, v_moved.before(b))
                for k in range(4):
                    act.wait_ge(f_pe.sem, f_pe.by(f"v{k}", b))
                    a(v_next[:, 2 * k:2 * k + 2].rearrange("p t h d -> p (t h d)"), st[:, k, :], ACT.Copy).then_inc(f_act.sem, 1)

            def rsqrt(dve_steps, act_steps, b):
                act.wait_ge(dve_steps.sem, dve_steps.by("var", b))
                a(lnv[:], var[:], ACT.Ln).then_inc(act_steps.sem, 1)
                act.wait_ge(act_steps.sem, act_steps.by("ln", b))
                a(rstd[:], lnv[:], ACT.Exp, scale=-0.5).then_inc(act_steps.sem, 1)

            def attend(u, b, q, left):
                for s, (c, j) in enumerate(STEPS):
                    off = max(0, P * j - BANK * c)
                    act.wait_ge(a_pv.sem, a_pv.by(str(s), u) - 2)
                    for p in range(2):
                        n = 2 * s + p
                        act.wait_ge(a_st.sem, a_st.by(str(n), u))
                        a(prob[:, n % 4, :, off:BANK], st[:, 2 * p:2 * p + 2, off:BANK], ACT.Exp).then_inc(a_exp.sem, 1)

            def back1(b, more):
                for n in (0, 2):
                    half, ct = divmod(n, 2)
                    act.wait_ge(b_pe.sem, b_pe.by(f"z{n}", b))
                    a(yT[:, ct, BANK * half:BANK * (half + 1)], st[:, n, :], ACT.Copy).then_inc(b_act.sem, 1)
                rsqrt(b_dve, b_act, b)

            def back2(b, ahead):
                for n in (0, 2):
                    half, ct = divmod(n, 2)
                    act.wait_ge(b_pe.sem, b_pe.by(f"p{n}", b))
                    a(xnT[:, ct, BANK * half:BANK * (half + 1)], st[:, n, :], ACT.Copy).then_inc(b_act.sem, 1)

            in_order(act, front, lambda: None, attend, back1, back2)

        @block.gpsimd
        def _(pool):
            for steps in (f_pool, a_mask, row_of_ready):
                pool.sem_inc(steps.sem, steps.free)
            pool.wait_ge(const_made, 4)

            def rows_of(b):
                if not at_first(b):
                    alone(pool, emb_loaded.sem, emb_loaded.before(b), waited_pool)
                nc.gpsimd.tensor_copy(row_of[:], keep["index"][:, bass.ds(b * TILES, TILES)]).then_inc(row_of_ready.sem, 1)

            def gather(b, tiles):
                alone(pool, row_of_ready.sem, row_of_ready.end(b), waited_pool)
                for t in tiles:
                    nc.gpsimd.indirect_dma_start(
                        out=emb[:, t, 0:DIM], out_offset=None, in_=io["embed"],
                        in_offset=bass.IndirectOffsetOnAxis(ap=row_of[:, t:t + 1], axis=0),
                    ).then_inc(emb_loaded.sem, 16)

            def front(b):
                if isinstance(b, int):
                    rows_of(b)
                    if b:
                        alone(pool, f_pe.sem, f_pe.by("et1", b - 1), waited_pool)
                    gather(b, range(TILES))
                for s in range(4):
                    c, side = divmod(s, 2)
                    stored = parts_stored[side]
                    alone(pool, stored.sem, stored.by(b, 2 * (s // 2)), waited_pool)
                    for y_, (r, m_, l_) in enumerate((("rc", "mc", "lc"), ("re", "me", "le"))):
                        alone(pool, f_dve.sem, f_dve.by(f"{r}{s}", b), waited_pool)
                        nc.gpsimd.tensor_copy(parts[:, side, y_, 1, :], res[:, y_, :]).then_inc(f_pool.sem, 1)
                        alone(pool, f_pool.sem, f_pool.by(f"{m_}{s}", b), waited_pool)
                        nc.gpsimd.tensor_tensor(parts[:, side, y_, 2, :], res[:, y_, :], parts[:, side, y_, 1, :],
                                                ALU.subtract).then_inc(f_pool.sem, 1)

            def attend(u, b, q, left):
                ahead = left >= UB + UB - q
                if ahead and q == 0:
                    alone(pool, f_pe.sem, f_pe.by("et1", b + 1), waited_pool)
                    rows_of(b + 2)
                for s in range(NS):
                    c, j = STEPS[s]
                    if s in DIAG:
                        off = P * j - BANK * c
                        for p in range(2):
                            n = 2 * s + p
                            alone(pool, a_exp.sem, a_exp.by(str(n), u), waited_pool)
                            at = prob[:, n % 4, :, off:off + P]
                            nc.gpsimd.affine_select(out=at, in_=at, compare_op=ALU.is_ge, fill=0.0, base=0,
                                                    pattern=[[0, 2], [1, P]], channel_multiplier=-1).then_inc(a_mask.sem, 1)
                    elif ahead and s == PLAIN[0]:
                        gather(b + 2, (2 * q, 2 * q + 1))

            nothing = lambda *_: None
            in_order(pool, front, nothing, attend, nothing, nothing)

        @block.vector
        def _(dve):
            ts, tt = nc.vector.tensor_scalar, nc.vector.tensor_tensor
            nc.vector.memset(emb[:], 0.0).then_inc(const_made, 1)
            nc.vector.memset(ka[96:96 + PARTS, :], 1.0).then_inc(const_made, 1)
            nc.vector.memset(v[:], 1.0).then_inc(const_made, 1)
            nc.vector.memset(zero[:], 0.0).then_inc(const_made, 1)
            dve.wait_ge(const_made, 4)
            nc.vector.memset(proj[64:P, :], 0.0).then_inc(const_made, 1)
            for steps in (f_dve, m_dve, a_out, b_dve, v_moved):
                dve.sem_inc(steps.sem, steps.free)
            dve.wait_ge(const_loaded, 16 * 8)
            nc.vector.tensor_copy(identb[:], identf[:]).then_inc(const_made, 1)
            nc.vector.tensor_copy(maskb[:], maskf[:]).then_inc(const_made, 1)
            dve.sem_inc(const_made, 2)
            dve.wait_ge(const_made, 9)

            def norm(steps, run, out):
                for t in range(TILES):
                    nc.vector.bn_stats(stats[:, t, :], h[:, t, :]).then_inc(steps.sem, 1)
                for t in range(TILES):
                    alone(dve, steps.sem, steps.by(f"st{t}", run), waited_dve)
                    nc.vector.bn_aggr(mv[:, t, :], stats[:, t, :]).then_inc(steps.sem, 1)
                dve.wait_ge(steps.sem, steps.by("ag7", run))
                ts(var[:], mv[:, :, 1], EPS, None, ALU.add).then_inc(steps.sem, 1)
                act_steps = f_act if steps is f_dve else b_act
                dve.wait_ge(act_steps.sem, act_steps.by("rs", run))
                dve.wait_ge(steps.sem, steps.by("var", run))
                tt(tmp[:], rstd[:], rstd[:], ALU.mult).then_inc(steps.sem, 1)
                dve.wait_ge(steps.sem, steps.by("n1", run))
                tt(tmp[:], tmp[:], var[:], ALU.mult).then_inc(steps.sem, 1)
                dve.wait_ge(steps.sem, steps.by("n2", run))
                ts(tmp[:], tmp[:], -0.5, 1.5, ALU.mult, ALU.add).then_inc(steps.sem, 1)
                dve.wait_ge(steps.sem, steps.by("n3", run))
                tt(rstd[:], rstd[:], tmp[:], ALU.mult).then_inc(steps.sem, 1)
                dve.wait_ge(steps.sem, steps.by("n4", run))
                for t in range(TILES):
                    ts(out[:, t, :], h[:, t, :], mv[:, t, 0:1], rstd[:, t:t + 1], ALU.subtract, ALU.mult).then_inc(steps.sem, 1)
                dve.wait_ge(steps.sem, steps.by(f"xn{TILES - 1}", run))

            def front(b):
                dve.wait_ge(f_act.sem, f_act.by("h3", b))
                norm(f_dve, b, xn)
                for k in (1, 3):
                    dve.wait_ge(f_pe.sem, f_pe.by(f"x{k}", b))
                    nc.vector.tensor_copy(xnT[:, k // 2, BANK:], st[:, k, :]).then_inc(f_dve.sem, 1)
                for s in range(4):
                    c, side = divmod(s, 2)
                    cols = slice(BANK * c, BANK * (c + 1))
                    bank = [(3 * s + k) % 4 for k in range(3)]
                    if s:
                        dve.wait_ge(f_pool.sem, f_pool.by(f"le{s - 1}", b))
                    else:
                        dve.wait_ge(f_pool.sem, f_pool.before(b))
                    dve.wait_ge(f_act.sem, f_act.by(f"hc{s}", b))
                    tt(res[:, 0, :], st[:, bank[0], :], parts[:, side, 0, 0, :], ALU.subtract).then_inc(f_dve.sem, 1)
                    dve.wait_ge(f_pe.sem, f_pe.by(f"e{s}", b))
                    tt(rot_a[:], st[:, bank[1], :], cos[:, cols], ALU.mult).then_inc(f_dve.sem, 1)
                    dve.wait_ge(f_pe.sem, f_pe.by(f"r{s}", b))
                    tt(rot_b[:], st[:, bank[2], :], sin[:, cols], ALU.mult).then_inc(f_dve.sem, 1)
                    dve.wait_ge(f_dve.sem, f_dve.by(f"t2{s}", b))
                    tt(rot_c[:], rot_a[:], rot_b[:], ALU.add).then_inc(f_dve.sem, 1)
                    dve.wait_ge(f_dve.sem, f_dve.by(f"qe{s}", b))
                    dve.wait_ge(f_act.sem, f_act.by(f"he{s}", b))
                    tt(res[:, 1, :], rot_c[:], parts[:, side, 1, 0, :], ALU.subtract).then_inc(f_dve.sem, 1)
                    dve.wait_ge(f_dve.sem, f_dve.by(f"re{s}", b))
                if at_first(b):
                    move_v(0)

            def move_v(b):
                dve.wait_ge(f_act.sem, f_act.end(b))
                out = v[:, :, 0:H * VW].rearrange("p t (h d) -> p t h d", d=VW)
                for k in range(2):
                    tiles = slice(4 * k, 4 * k + 4)
                    nc.vector.tensor_copy(out[:, tiles, :, 0:DH], v_next[:, tiles]).then_inc(v_moved.sem, 1)

            def max_block(u, k):
                hh, kk = divmod(k, len(MAX_BLOCKS))
                w = MAX_BLOCKS[kk][2]
                dve.wait_ge(m_pe.sem, m_pe.by(f"m{k}", u))
                nc.vector.tensor_reduce(mx[:, hh, kk:kk + 1], sm[:, k % 3, 0:w], AX.X, ALU.max, negate=True).then_inc(m_dve.sem, 1)

            def max_end(u):
                dve.wait_ge(m_dve.sem, m_dve.by(f"m{MAXES - 1}", u))
                q = BANK // P
                nc.vector.tensor_copy(nmax[:, :, 0:q], mx[:, :, 0:q]).then_inc(m_dve.sem, 1)
                tt(nmax[:, :, q:], mx[:, :, q:2 * q], mx[:, :, 2 * q:], ALU.min).then_inc(m_dve.sem, 1)
                dve.wait_ge(m_pe.sem, m_pe.by("t", u))
                dve.wait_ge(m_stored.sem, m_stored.before(u))
                turned = sm[0:UH * TILES, 0, 0:P]
                nc.vector.tensor_copy(m_parts[:, 0, :], turned).then_inc(m_dve.sem, 1)
                dve.wait_ge(m_dve.sem, m_dve.by("hi", u))
                tt(m_res[:], turned, m_parts[:, 0, :], ALU.subtract).then_inc(m_dve.sem, 1)
                dve.wait_ge(m_dve.sem, m_dve.by("res", u))
                nc.vector.tensor_copy(m_parts[:, 1, :], m_res[:]).then_inc(m_dve.sem, 1)
                dve.wait_ge(m_dve.sem, m_dve.by("mid", u))
                tt(m_parts[:, 2, :], m_res[:], m_parts[:, 1, :], ALU.subtract).then_inc(m_dve.sem, 1)

            def maxima():
                for u in range(2):
                    for k in range(MAXES):
                        max_block(u, k)
                    if u == 0:
                        max_end(0)

            def attend(u, b, q, left):
                def sums_out(c):
                    s = max(s_ for s_, c_ in LAST_OF.items() if c_ == c)
                    if q == c == 0:
                        dve.wait_ge(x2T_stored.sem, x2T_stored.before(b))
                        if left >= UB:
                            dve.wait_ge(f_pe.sem, f_pe.end(b + 1))
                        dve.wait_ge(b_pe.sem, b_pe.before(b))
                    dve.wait_ge(a_pv.sem, a_pv.by(str(s), u))
                    nc.vector.tensor_copy(yT_raw[:, q, BANK * c:BANK * (c + 1)], pv[:]).then_inc(a_out.sem, 1)

                if left:
                    max_end(u + 1)
                for s in range(NS):
                    blocks = [k for k in range(MAX_PER * s, MAX_PER * (s + 1)) if left >= 2]
                    for k in blocks[:2]:
                        max_block(u + 2, k)
                    if s - 1 in LAST_OF:
                        sums_out(LAST_OF[s - 1])
                    for k in blocks[2:]:
                        max_block(u + 2, k)
                sums_out(1)

            def back1(b, more):
                for t in range(TILES):
                    dve.wait_ge(b_pe.sem, b_pe.by(f"yt{t}", b))
                    src = st[:, t % 4, :].rearrange("p (h d) -> p h d", d=32)
                    if t >= 2:
                        dve.wait_ge(b_dve.sem, b_dve.by(f"y{t - 2}", b))
                    nc.vector.reciprocal(rden[:, t % 2, :], src[:, :, DH]).then_inc(b_dve.sem, 1)
                    dve.wait_ge(b_dve.sem, b_dve.by(f"rc{t}", b))
                    tt(y[:, t, :].rearrange("p (h d) -> p h d", d=DH), src[:, :, 0:DH],
                       rden[:, t % 2, :].unsqueeze(2).to_broadcast([P, H, DH]), ALU.mult).then_inc(b_dve.sem, 1)
                for n in (1, 3):
                    half, ct = divmod(n, 2)
                    dve.wait_ge(b_pe.sem, b_pe.by(f"z{n}", b))
                    nc.vector.tensor_copy(yT[:, ct, BANK * half:BANK * (half + 1)], st[:, n, :]).then_inc(b_dve.sem, 1)
                dve.wait_ge(h_loaded.sem, h_loaded.by(b))
                for k in range(4):
                    dve.wait_ge(b_pe.sem, b_pe.by(f"w{k}", b))
                    at = h[:, 2 * k:2 * k + 2, :].rearrange("p t c -> p (t c)")
                    tt(at, st[:, k, :], at, ALU.add).then_inc(b_dve.sem, 1)
                dve.wait_ge(b_dve.sem, b_dve.by("a3", b))
                dve.wait_ge(x2_stored.sem, x2_stored.before(b))
                norm(b_dve, b, x2)
                if more:
                    dve.wait_ge(a_pv.sem, a_pv.before(UB * b + UB))
                    move_v(b + 1)

            def back2(b, ahead):
                for n in (1, 3):
                    half, ct = divmod(n, 2)
                    dve.wait_ge(b_pe.sem, b_pe.by(f"p{n}", b))
                    nc.vector.tensor_copy(xnT[:, ct, BANK * half:BANK * (half + 1)], st[:, n, :]).then_inc(b_dve.sem, 1)
                dve.wait_ge(b_pe.sem, b_pe.by("gate", b))
                dve.wait_ge(lg_stored.sem, lg_stored.before(b))
                nc.vector.tensor_copy(lg_sb[:].rearrange("p t e -> p (t e)"), st[:, 0, 0:TILES * E]).then_inc(b_dve.sem, 1)

            in_order(dve, front, maxima, attend, back1, back2)



def route(nc, io, keep):
    shape = [P, ALLT, E]
    with ExitStack() as ctx:
        sb = lambda name, shape, dt=F32: ctx.enter_context(nc.sbuf_tensor(name, shape, dt))
        sem = lambda name: ctx.enter_context(nc.semaphore(name))
        lg, ex, eq, l2, sel = (sb(f"r_{n}", shape) for n in ("lg", "ex", "eq", "l2", "sel"))
        hot = [sb(f"r_hot{k}", shape) for k in range(TOPK)]
        pre_a, pre_b, pos, tmp = (sb(f"r_{n}", shape) for n in ("pre_a", "pre_b", "pos", "tmp"))
        first, start = sb("r_first", shape), sb("r_start", shape)
        best = sb("r_best", [P, ALLT])
        pk, kept, slot = (sb(f"r_{n}", [P, ALLT, TOPK]) for n in ("pk", "kept", "slot"))
        gone = sb("r_gone", [P, ALLT, TOPK])
        total, score = sb("r_total", [P, ALLT]), sb("r_score", [P, ALLT, TOPK])
        before, ones = sb("r_before", [P, P]), sb("r_ones", [P, P])
        ps = ctx.enter_context(nc.psum_tensor("ps_route", [P, 2, BANK], F32))
        loaded, chain, shifted, exped, counted = (sem(n) for n in (
            "route_loaded", "route_chain", "shifted_ready", "exp_ready", "counts_ready"))
        sel_ready = sem("sel_ready")
        block = ctx.enter_context(nc.Block())
        flat = lambda x: x[:].rearrange("p t e -> p (t e)")

        @block.sync
        def _(sp):
            for dst, src in ((lg[:].rearrange("p (b t) e -> p b t e", t=TILES), keep["logits"].rearrange("b p t e -> p b t e")),
                             (first[:], io["first"]), (start[:], io["start"]),
                             (before[:], io["before"]), (ones[:], io["ones"])):
                sp.dma_start(dst, src).then_inc(loaded, 16)

        @block.scalar
        def _(act):
            act.wait_ge(shifted, 1)
            nc.scalar.activation(flat(ex), flat(ex), ACT.Exp).then_inc(exped, 1)

        @block.tensor
        def _(pe):
            pe.wait_ge(loaded, 16 * 5)
            pe.wait_ge(sel_ready, 1)
            pe.matmul(ps[:, 0, :], before[:], flat(sel), start=True, stop=True)
            pe.matmul(ps[:, 1, :], ones[:], flat(sel), start=True, stop=True).then_inc(counted, 1)

        @block.vector
        def _(dve):
            ts, tt, red = nc.vector.tensor_scalar, nc.vector.tensor_tensor, nc.vector.tensor_reduce
            steps = [0]

            def link(ins):
                steps[0] += 1
                ins.then_inc(chain, 1)
                dve.wait_ge(chain, steps[0])

            wide = lambda x: x.unsqueeze(2).to_broadcast(shape)
            dve.wait_ge(loaded, 16 * 5)
            src = lg
            for k in range(TOPK):
                link(red(best[:], src[:], AX.X, ALU.max))
                link(tt(eq[:], src[:], wide(best[:]), ALU.is_equal))
                if k == 0:
                    tt(ex[:], lg[:], wide(best[:]), ALU.subtract).then_inc(shifted, 1)
                link(tt(eq[:], eq[:], first[:], ALU.mult))
                if k == 0:
                    dve.wait_ge(shifted, 1)
                link(red(best[:], eq[:], AX.X, ALU.max))
                link(tt(hot[k][:], eq[:], wide(best[:]), ALU.is_equal))
                if k == 0:
                    link(ts(l2[:], hot[0][:], MASKED, None, ALU.mult))
                    link(tt(l2[:], l2[:], lg[:], ALU.add))
                    src = l2
            tt(sel[:], hot[0][:], hot[1][:], ALU.add).then_inc(sel_ready, 1)
            dve.wait_ge(exped, 1)
            link(red(total[:], ex[:], AX.X, ALU.add))
            link(nc.vector.reciprocal(total[:], total[:]))
            for k in range(TOPK):
                link(tt(tmp[:], hot[k][:], ex[:], ALU.mult))
                link(red(score[:, :, k], tmp[:], AX.X, ALU.add))
                link(tt(score[:, :, k], score[:, :, k], total[:], ALU.mult))
            link(tt(total[:], score[:, :, 0], score[:, :, 1], ALU.add))
            link(ts(total[:], total[:], 1e-20, None, ALU.add))
            link(nc.vector.reciprocal(total[:], total[:]))
            link(tt(score[:], score[:], total[:].unsqueeze(2).to_broadcast([P, ALLT, TOPK]), ALU.mult))
            dve.wait_ge(counted, 1)
            link(nc.vector.tensor_copy(flat(pre_a), ps[:, 1, :]))
            link(tt(flat(pos), ps[:, 0, :], flat(pre_a), ALU.subtract))
            a, b, d = pre_a, pre_b, 1
            while d < ALLT:
                link(nc.vector.tensor_copy(b[:, 0:d, :], a[:, 0:d, :]))
                link(tt(b[:, d:, :], a[:, d:, :], a[:, :ALLT - d, :], ALU.add))
                a, b, d = b, a, 2 * d
            link(tt(pos[:], pos[:], a[:], ALU.add))
            for k in range(TOPK):
                link(tt(tmp[:], hot[k][:], pos[:], ALU.mult))
                link(red(pk[:, :, k], tmp[:], AX.X, ALU.add))
                link(tt(tmp[:], hot[k][:], start[:], ALU.mult))
                link(red(slot[:, :, k], tmp[:], AX.X, ALU.add))
            link(tt(slot[:], slot[:], pk[:], ALU.add))
            link(ts(kept[:], pk[:], float(CAP), None, ALU.is_lt))
            link(tt(keep["weight"][:], score[:], kept[:], ALU.mult))
            link(tt(slot[:], slot[:], kept[:], ALU.mult))
            link(nc.vector.tensor_copy(keep["gather"][:], slot[:]))
            link(ts(gone[:], kept[:], -float(E * CAP), float(E * CAP), ALU.mult, ALU.add))
            link(tt(slot[:], slot[:], gone[:], ALU.add))
            link(nc.vector.tensor_copy(keep["scatter"][:], slot[:]))



RUNS = 4
RS, SRING = ALLT // RUNS, 4
RING = 7
RG = 2 * RING
TAIL = ALLT - RUNS * RG
AHEAD = 5
ITEMS = 2 * QC
MS, QT = SH // P, CH // P
SHARED = [f"{x}a{m}" for x in range(2) for m in range(MS)] + [f"{x}o{k}" for x in range(2) for k in range(2)]
assert all(RG * (i + 1) + (AHEAD if i < RUNS - 1 else 0) <= 2 * QT * (RUNS + i) for i in range(RUNS)) and 0 < TAIL <= RG


def beside(step, tiles):
    return range(tiles * step // len(SHARED), tiles * (step + 1) // len(SHARED))


def experts(nc, io, keep):
    with ExitStack() as ctx:
        sb = lambda name, shape, dt=F32: ctx.enter_context(nc.sbuf_tensor(name, shape, dt))
        sem = lambda name: ctx.enter_context(nc.semaphore(name))
        tr = ctx.enter_context(nc.psum_tensor("tr", [P, KT, BANK], F32))
        gu = ctx.enter_context(nc.psum_tensor("gu", [P, 4, BANK], F32))
        dn = ctx.enter_context(nc.psum_tensor("dn", [P, 2, BANK], F32))
        identf = sb("identf_e", [P, P])
        wsg, wsu = sb("wsg", [P, KT, SH]), sb("wsu", [P, KT, SH])
        wsd = sb("wsd", [P, MS, C])
        xs, hs = sb("xs", [P, 2, KT, CH]), sb("hs", [P, 2, QT, C])
        sil = sb("sil", [P, 2, CH])
        inner = sb("inner", [P, 2, MS, CH])
        out_s = sb("out_s", [P, 2, QT, C])
        row = sb("row", [P, RING, C])
        g_row = sb("g_row", [P, RING, TOPK, C])
        done = sb("done", [P, RING, C])
        idx = sb("idx", [P, RS, TOPK], U32)
        w_now = sb("w_now", [P, RG, TOPK])
        weg, weu, wed = (sb(n, [P, 2, KT, EI]) for n in ("weg", "weu", "wed"))
        xg, xgT = sb("xg", [P, 2, QT, C]), sb("xgT", [P, 2, KT, CH])
        e_sil, e_in = sb("e_sil", [P, 2, CH]), sb("e_in", [P, 2, KT, CH])
        eo = sb("eo", [P, 2, QT, C])

        s_pe = Steps(sem("shared_pe"), [f"{x}g{m}" for x in range(2) for m in range(MS)] + [f"{x}d{k}" for x in range(2) for k in range(2)])
        s_act = Steps(sem("shared_act"), [f"{x}s{m}" for x in range(2) for m in range(MS)])
        s_dve = Steps(sem("shared_dve"), SHARED)
        xs_loaded = [Moves(sem(f"xs{x}_loaded")) for x in range(2)]
        hs_loaded = [Moves(sem(f"hs{x}_loaded")) for x in range(2)]
        sum_stored = [Moves(sem(f"sum{x}_stored")) for x in range(2)]
        const_loaded = sem("const_e_loaded")
        waited_sp, waited_pool = sem("waited_sp_e"), sem("waited_pool_e")
        idx_ready = Steps(sem("idx_ready"), ["copied"])
        row_loaded = [Moves(sem(f"row{k}_loaded"), RS // SRING) for k in range(SRING)]
        scattered = [Moves(sem(f"row{k}_scattered"), TOPK * RS // SRING, free=0) for k in range(SRING)]
        gathered = [Moves(sem(f"row{k}_gathered"), TOPK * RG // RING, free=0) for k in range(RING)]
        base_loaded = [Moves(sem(f"base{k}_loaded"), RG // RING) for k in range(RING)]
        out_stored = [Moves(sem(f"out{k}_stored"), RG // RING) for k in range(RING)]
        w_ready = Steps(sem("w_ready"), ["copied"])
        half_sum = Steps(sem("half_sum"), [f"{t}" for t in range(RG)])
        combined = Steps(sem("combined"), [f"{t}" for t in range(RG)], free=RING)
        e_pe = Steps(sem("expert_pe"), ["t0"] + [n for x in range(ITEMS) for n in (
            [f"g{x}_0", f"g{x}_1"] + ([f"t{x + 1}"] if x < ITEMS - 1 else []) + [f"d{x}_0", f"d{x}_1"])])
        e_act = Steps(sem("expert_act"), ["t0"] + [n for x in range(ITEMS) for n in (
            [f"s{x}_0", f"s{x}_1"] + ([f"t{x + 1}"] if x < ITEMS - 1 else []) + [f"o{x}"])])
        e_dve = Steps(sem("expert_dve"), ["t0"] + [n for x in range(ITEMS) for n in (
            [f"a{x}_0", f"a{x}_1"] + ([f"t{x + 1}"] if x < ITEMS - 1 else []) + [f"o{x}"])])
        xg_loaded = [Moves(sem(f"xg{x}_loaded"), QC) for x in range(2)]
        eo_stored = [Moves(sem(f"eo{x}_stored"), QC) for x in range(2)]
        w_loaded = [Moves(sem(f"we{x}_loaded"), 3) for x in range(2)]

        tiles_of = lambda ap: ap.rearrange("(t p) c -> t p c", p=P)
        chunk_of = lambda ap: ap.rearrange("(n t p) c -> n p t c", p=P, t=CH // P)
        queue_of = lambda ap: ap.rearrange("(n p t) c -> n p t c", p=P, t=CH // P)
        block = ctx.enter_context(nc.Block())

        def in_order(eng, first_half, expert_run, second_half):
            with eng.Fori(0, RUNS) as i:
                first_half(i)
            with eng.Fori(0, E // 2 - 1) as r:
                expert_run(r, False)
            expert_run(E // 2 - 1, True)
            with eng.Fori(0, RUNS - 1) as i:
                second_half(i, False)
            second_half(RUNS - 1, True)

        @block.sync
        def _(sp):
            for m in (*xs_loaded, *hs_loaded, *sum_stored, *row_loaded, *base_loaded,
                      *out_stored, *xg_loaded, *eo_stored, *w_loaded):
                sp.sem_inc(m.sem, 16)
            for dst, src in ((identf[:], io["identity"]), (wsg[:], io["ws_gate"].rearrange("(k p) i -> p k i", p=P)),
                             (wsu[:], io["ws_up"].rearrange("(k p) i -> p k i", p=P)),
                             (wsd[:], io["ws_down"].rearrange("(k p) c -> p k c", p=P))):
                sp.dma_start(dst, src).then_inc(const_loaded, 16)

            def load_weights(e, par):
                for dst, src in ((weg, io["we_gate"]), (weu, io["we_up"]), (wed, io["we_down"])):
                    sp.dma_start(dst[:, par], src[e].rearrange("(k p) i -> p k i", p=P)).then_inc(w_loaded[par].sem, 16)

            def load_xs(run, x):
                sp.dma_start(xs[:, x], keep["x2T"].rearrange("p k (n t) -> n p k t", t=CH)[2 * run + x]).then_inc(xs_loaded[x].sem, 16)

            def load_hs(run, x):
                sp.dma_start(hs[:, x], chunk_of(keep["h2"])[2 * run + x]).then_inc(hs_loaded[x].sem, 16)

            for x in range(2):
                load_xs(0, x)
                load_hs(0, x)
            for x in range(2):
                load_weights(x, x)

            def shared_moves(run, step, more):
                name = SHARED[step]
                x = int(name[0])
                if name[1:] in (f"a{MS - 1}", "o1"):
                    alone(sp, s_dve.sem, s_dve.by(name, run), waited_sp)
                if name[1:] == f"a{MS - 1}" and more:
                    load_xs(run + 1, x)
                if name[1:] == "o1":
                    sp.dma_start(chunk_of(keep["sum"])[2 * run + x], out_s[:, x]).then_inc(sum_stored[x].sem, 16)
                    if more:
                        load_hs(run + 1, x)

            def load_row(i, t):
                sp.dma_start(row[:, t % SRING], tiles_of(keep["x2"])[i * RS + t]).then_inc(row_loaded[t % SRING].sem, 16)

            def first_half(i, last):
                for step in range(len(SHARED)):
                    for t in beside(step, RS):
                        k = t % SRING
                        alone(sp, scattered[k].sem, scattered[k].by(i, TOPK * (t // SRING + 1)), waited_sp)
                        if t + SRING < RS or not last:
                            load_row(i, t + SRING)
                    shared_moves(i, step, True)

            def load_rows(r, x):
                sp.dma_start(xg[:, x % 2], queue_of(keep["queue"])[r * ITEMS + x]).then_inc(xg_loaded[x % 2].sem, 16)

            def expert_run(r, last):
                for x in range(ITEMS):
                    alone(sp, e_pe.sem, e_pe.by(f"t{x}", r), waited_sp)
                    if x + 2 < ITEMS:
                        load_rows(r, x + 2)
                    elif not last:
                        load_rows(r + 1, x + 2 - ITEMS)
                    alone(sp, e_act.sem, e_act.by(f"o{x}", r), waited_sp)
                    alone(sp, e_dve.sem, e_dve.by(f"o{x}", r), waited_sp)
                    sp.dma_start(queue_of(keep["expert_out"])[r * ITEMS + x], eo[:, x % 2]).then_inc(eo_stored[x % 2].sem, 16)
                    if x % QC == QC - 1 and not last:
                        load_weights(2 * r + 2 + x // QC, x // QC)

            def load_base(i, t):
                sp.dma_start(row[:, t % RING], tiles_of(keep["sum"])[i * RG + t]).then_inc(base_loaded[t % RING].sem, 16)

            def store_out(i, t):
                alone(sp, combined.sem, combined.by(f"{t}", i), waited_sp)
                sp.dma_start(tiles_of(io["out"])[i * RG + t], done[:, t % RING]).then_inc(out_stored[t % RING].sem, 16)

            def second_half(i, last):
                for x in range(2):
                    alone(sp, sum_stored[x].sem, sum_stored[x].before(i + RUNS), waited_sp)
                for step in range(len(SHARED)):
                    for t in beside(step, RG):
                        store_out(i, t)
                        if t + AHEAD < RG or not last:
                            load_base(i, t + AHEAD)
                    shared_moves(i + RUNS, step, not last)

            for t in range(SRING):
                load_row(0, t)
            with sp.Fori(0, RUNS - 1) as i:
                first_half(i, False)
            first_half(RUNS - 1, True)
            for x in range(2):
                load_rows(0, x)
            with sp.Fori(0, E // 2 - 1) as r:
                expert_run(r, False)
            expert_run(E // 2 - 1, True)
            for x in range(2):
                alone(sp, sum_stored[x].sem, sum_stored[x].before(RUNS), waited_sp)
            for t in range(AHEAD):
                load_base(0, t)
            with sp.Fori(0, RUNS - 1) as i:
                second_half(i, False)
            second_half(RUNS - 1, True)
            for x in range(2):
                alone(sp, sum_stored[x].sem, sum_stored[x].before(2 * RUNS), waited_sp)
            for t in range(min(RING, TAIL)):
                load_base(RUNS, t)
            for t in range(TAIL):
                store_out(RUNS, t)
                if t + RING < TAIL:
                    load_base(RUNS, t + RING)
            for k in range(RING):
                alone(sp, out_stored[k].sem, out_stored[k].by(RUNS, len(range(k, TAIL, RING))), waited_sp)

        @block.gpsimd
        def _(pool):
            pool.sem_inc(idx_ready.sem, idx_ready.free)

            def scatter(i):
                nc.gpsimd.tensor_copy(idx[:], keep["scatter"][:, bass.ds(i * RS, RS), :]).then_inc(idx_ready.sem, 1)
                alone(pool, idx_ready.sem, idx_ready.by("copied", i), waited_pool)
                for t in range(RS):
                    k = t % SRING
                    alone(pool, row_loaded[k].sem, row_loaded[k].by(i, t // SRING + 1), waited_pool)
                    for n in range(TOPK):
                        nc.gpsimd.indirect_dma_start(
                            out=keep["queue"], out_offset=bass.IndirectOffsetOnAxis(ap=idx[:, t, n:n + 1], axis=0),
                            in_=row[:, k], in_offset=None, bounds_check=E * CAP - 1, oob_is_err=False,
                        ).then_inc(scattered[k].sem, 16)
                for k in range(SRING):
                    alone(pool, scattered[k].sem, scattered[k].by(i), waited_pool)

            def gather(i, tiles):
                nc.gpsimd.tensor_copy(idx[:, 0:tiles], keep["gather"][:, bass.ds(i * RG, tiles), :]).then_inc(idx_ready.sem, 1)
                alone(pool, idx_ready.sem, idx_ready.by("copied", i + RUNS), waited_pool)
                for t in range(tiles):
                    k = t % RING
                    alone(pool, combined.sem, combined.by(f"{t}", i) - RING, waited_pool)
                    for n in range(TOPK):
                        nc.gpsimd.indirect_dma_start(
                            out=g_row[:, k, n], out_offset=None, in_=keep["expert_out"],
                            in_offset=bass.IndirectOffsetOnAxis(ap=idx[:, t, n:n + 1], axis=0),
                        ).then_inc(gathered[k].sem, 16)
                for k in range(RING):
                    if k < tiles:
                        n = len(range(k, tiles, RING))
                        alone(pool, gathered[k].sem, gathered[k].by(i, TOPK * n), waited_pool)

            with pool.Fori(0, RUNS) as i:
                scatter(i)
            for x in range(2):
                alone(pool, eo_stored[x].sem, eo_stored[x].before(E // 2), waited_pool)
            with pool.Fori(0, RUNS) as i:
                gather(i, RG)
            gather(RUNS, TAIL)

        @block.tensor
        def _(pe):
            for steps in (s_pe, e_pe):
                pe.sem_inc(steps.sem, steps.free)
            pe.wait_ge(const_loaded, 16 * 4)

            def shared(run):
                for x in range(2):
                    pe.wait_ge(xs_loaded[x].sem, xs_loaded[x].by(run))
                    for m in range(MS):
                        n = x * MS + m
                        if n >= 2:
                            pe.wait_ge(s_dve.sem, s_dve.by(f"{(n - 2) // MS}a{(n - 2) % MS}", run))
                        else:
                            pe.wait_ge(s_dve.sem, s_dve.before(run))
                        for side, w in enumerate((wsg, wsu)):
                            for ct in range(KT):
                                ins = pe.matmul(gu[:, 2 * (n % 2) + side, :], w[:, ct, P * m:P * (m + 1)], xs[:, x, ct, :],
                                                start=(ct == 0), stop=(ct == KT - 1))
                        ins.then_inc(s_pe.sem, 1)
                for x in range(2):
                    for k in range(2):
                        if x or k == 0:
                            pe.wait_ge(s_dve.sem, s_dve.by(f"0o{k}" if x else f"0a{MS - 1}", run))
                        for q in range(2):
                            t = 2 * k + q
                            for ct in range(MS):
                                ins = pe.matmul(dn[:, k, C * q:C * (q + 1)], inner[:, x, ct, P * t:P * (t + 1)], wsd[:, ct],
                                                start=(ct == 0), stop=(ct == MS - 1))
                        ins.then_inc(s_pe.sem, 1)

            def expert_run(r, last):
                def turn(x):
                    pe.wait_ge(xg_loaded[x % 2].sem, xg_loaded[x % 2].by(r, x // 2 + 1))
                    if x:
                        pe.wait_ge(e_act.sem, e_act.by(f"t{x - 1}", r))
                        pe.wait_ge(e_dve.sem, e_dve.by(f"t{x - 1}", r))
                    for ct in range(KT):
                        for q in range(QT):
                            ins = pe.transpose(tr[:, ct, P * q:P * (q + 1)], xg[:, x % 2, q, P * ct:P * (ct + 1)], identf[:])
                    ins.then_inc(e_pe.sem, 1)

                pe.wait_ge(e_act.sem, e_act.before(r))
                pe.wait_ge(e_dve.sem, e_dve.before(r))
                turn(0)
                for x in range(ITEMS):
                    par = x // QC
                    if x % QC == 0:
                        pe.wait_ge(w_loaded[par].sem, w_loaded[par].by(r))
                    pe.wait_ge(e_act.sem, e_act.by(f"t{x}", r))
                    pe.wait_ge(e_dve.sem, e_dve.by(f"t{x}", r))
                    for mt in range(KT):
                        for side, w in enumerate((weg, weu)):
                            for ct in range(KT):
                                ins = pe.matmul(gu[:, 2 * mt + side, :], w[:, par, ct, P * mt:P * (mt + 1)], xgT[:, x % 2, ct, :],
                                                start=(ct == 0), stop=(ct == KT - 1))
                        ins.then_inc(e_pe.sem, 1)
                    if x < ITEMS - 1:
                        turn(x + 1)
                    pe.wait_ge(e_dve.sem, e_dve.by(f"a{x}_1", r))
                    for k in range(2):
                        if x and k == 0:
                            pe.wait_ge(e_act.sem, e_act.by(f"o{x - 1}", r))
                        for q in range(2):
                            for ct in range(KT):
                                ins = pe.matmul(dn[:, k, C * q:C * (q + 1)], e_in[:, x % 2, ct, P * (2 * k + q):P * (2 * k + q + 1)],
                                                wed[:, par, ct], start=(ct == 0), stop=(ct == KT - 1))
                        ins.then_inc(e_pe.sem, 1)

            with pe.Fori(0, RUNS) as i:
                shared(i)
            pe.wait_ge(s_dve.sem, s_dve.before(RUNS))
            with pe.Fori(0, E // 2 - 1) as r:
                expert_run(r, False)
            expert_run(E // 2 - 1, True)
            pe.wait_ge(e_act.sem, e_act.before(E // 2))
            pe.wait_ge(e_dve.sem, e_dve.before(E // 2))
            with pe.Fori(RUNS, 2 * RUNS) as run:
                shared(run)

        @block.scalar
        def _(act):
            a = nc.scalar.activation
            for steps in (s_act, e_act):
                act.sem_inc(steps.sem, steps.free)

            def shared(run):
                for x in range(2):
                    for m in range(MS):
                        n = x * MS + m
                        act.wait_ge(s_pe.sem, s_pe.by(f"{x}g{m}", run))
                        if n >= 2:
                            act.wait_ge(s_dve.sem, s_dve.by(f"{(n - 2) // MS}a{(n - 2) % MS}", run))
                        a(sil[:, n % 2, :], gu[:, 2 * (n % 2), :], ACT.Silu).then_inc(s_act.sem, 1)

            def expert_run(r, last):
                def turn(x):
                    act.wait_ge(e_pe.sem, e_pe.by(f"t{x}", r))
                    a(xgT[:, x % 2, 0, :], tr[:, 0, :], ACT.Copy).then_inc(e_act.sem, 1)

                turn(0)
                for x in range(ITEMS):
                    for mt in range(KT):
                        act.wait_ge(e_pe.sem, e_pe.by(f"g{x}_{mt}", r))
                        if x:
                            act.wait_ge(e_dve.sem, e_dve.by(f"a{x - 1}_{mt}", r))
                        a(e_sil[:, mt, :], gu[:, 2 * mt, :], ACT.Silu).then_inc(e_act.sem, 1)
                    if x < ITEMS - 1:
                        turn(x + 1)
                    act.wait_ge(e_pe.sem, e_pe.by(f"d{x}_0", r))
                    act.wait_ge(eo_stored[x % 2].sem, eo_stored[x % 2].by(r, x // 2))
                    a(eo[:, x % 2, 0:2].rearrange("p t c -> p (t c)"), dn[:, 0, :], ACT.Copy).then_inc(e_act.sem, 1)

            in_order(act, shared, expert_run, lambda i, last: shared(i + RUNS))

        @block.vector
        def _(dve):
            tt, stt = nc.vector.tensor_tensor, nc.vector.scalar_tensor_tensor
            for steps in (s_dve, e_dve, w_ready, half_sum, combined):
                dve.sem_inc(steps.sem, steps.free)

            def shared(run, step):
                name = SHARED[step]
                x, k = int(name[0]), int(name[2:])
                if name[1] == "a":
                    dve.wait_ge(s_act.sem, s_act.by(f"{x}s{k}", run))
                    if step == 0:
                        dve.wait_ge(s_pe.sem, s_pe.before(run))
                    tt(inner[:, x, k, :], sil[:, step % 2, :], gu[:, 2 * (step % 2) + 1, :], ALU.mult).then_inc(s_dve.sem, 1)
                else:
                    if k == 0:
                        dve.wait_ge(hs_loaded[x].sem, hs_loaded[x].by(run))
                        dve.wait_ge(sum_stored[x].sem, sum_stored[x].before(run))
                    dve.wait_ge(s_pe.sem, s_pe.by(f"{x}d{k}", run))
                    tt(out_s[:, x, 2 * k:2 * k + 2].rearrange("p t c -> p (t c)"), dn[:, k, :],
                       hs[:, x, 2 * k:2 * k + 2].rearrange("p t c -> p (t c)"), ALU.add).then_inc(s_dve.sem, 1)

            def expert_run(r, last):
                def turn(x):
                    dve.wait_ge(e_pe.sem, e_pe.by(f"t{x}", r))
                    nc.vector.tensor_copy(xgT[:, x % 2, 1, :], tr[:, 1, :]).then_inc(e_dve.sem, 1)

                turn(0)
                for x in range(ITEMS):
                    for mt in range(KT):
                        dve.wait_ge(e_act.sem, e_act.by(f"s{x}_{mt}", r))
                        tt(e_in[:, x % 2, mt, :], e_sil[:, mt, :], gu[:, 2 * mt + 1, :], ALU.mult).then_inc(e_dve.sem, 1)
                    if x < ITEMS - 1:
                        turn(x + 1)
                    dve.wait_ge(e_pe.sem, e_pe.by(f"d{x}_1", r))
                    dve.wait_ge(eo_stored[x % 2].sem, eo_stored[x % 2].by(r, x // 2))
                    nc.vector.tensor_copy(eo[:, x % 2, 2:4].rearrange("p t c -> p (t c)"), dn[:, 1, :]).then_inc(e_dve.sem, 1)

            def weights(i, tiles):
                dve.wait_ge(combined.sem, combined.before(i))
                nc.vector.tensor_copy(w_now[:, 0:tiles], keep["weight"][:, bass.ds(i * RG, tiles), :]).then_inc(w_ready.sem, 1)
                dve.wait_ge(w_ready.sem, w_ready.by("copied", i))

            def combine(i, t):
                k, n = t % RING, t // RING
                dve.wait_ge(base_loaded[k].sem, base_loaded[k].by(i, n + 1))
                dve.wait_ge(gathered[k].sem, gathered[k].by(i, TOPK * (n + 1)))
                dve.wait_ge(out_stored[k].sem, out_stored[k].by(i, n))
                stt(out=row[:, k], in0=g_row[:, k, 0], scalar=w_now[:, t, 0:1], in1=row[:, k],
                    op0=ALU.mult, op1=ALU.add).then_inc(half_sum.sem, 1)
                dve.wait_ge(half_sum.sem, half_sum.by(f"{t}", i))
                stt(out=done[:, k], in0=g_row[:, k, 1], scalar=w_now[:, t, 1:2], in1=row[:, k],
                    op0=ALU.mult, op1=ALU.add).then_inc(combined.sem, 1)

            def first_half(i):
                for step in range(len(SHARED)):
                    shared(i, step)

            def second_half(i, last):
                weights(i, RG)
                for step in range(len(SHARED)):
                    for t in beside(step, RG):
                        combine(i, t)
                    shared(i + RUNS, step)

            in_order(dve, first_half, expert_run, second_half)
            weights(RUNS, TAIL)
            for t in range(TAIL):
                combine(RUNS, t)



def tower_kernel(nc, io):
    dram = lambda name, shape, dt=F32: nc.dram_tensor(name, shape, dt).ap()
    with ExitStack() as ctx:
        sb = lambda name, shape, dt=F32: ctx.enter_context(nc.sbuf_tensor(name, shape, dt))
        keep = {
            "h": dram("h_rows", [N, C]), "h2": dram("h2_rows", [N, C]),
            "x2": dram("x2_rows", [N, C]), "x2T": dram("x2_cols", [P, KT, N]),
            "parts": dram("qk_parts", [B, 2, PARTS, 2, P, T], BF16),
            "max": dram("max_parts", [UNITS, PARTS, UH * TILES, P], BF16),
            "logits": dram("logits", [B, P, TILES, E]), "queue": dram("queues", [E * CAP, C]),
            "expert_out": dram("expert_out", [E * CAP, C]), "sum": dram("shared_sum", [N, C]),
            "index": sb("index", [P, ALLT], U32),
            "w_qk": sb("w_qk", [P, KT, 2, 3, P]), "w_v": sb("w_v", [P, KT, C]),
            "scatter": sb("scatter_idx", [P, ALLT, TOPK], U32), "gather": sb("gather_idx", [P, ALLT, TOPK], U32),
            "weight": sb("weight", [P, ALLT, TOPK]),
        }
        prepare(nc, io, keep)
        towers(nc, io, keep)
        route(nc, io, keep)
        experts(nc, io, keep)


def constants():
    f = np.float32
    inv = f(1.0) / (f(10000.0) ** (np.arange(0, HALF, 2, dtype=f) / f(HALF)))
    freqs = np.arange(T, dtype=f)[:, None] * inv[None, :]
    angle = np.concatenate((freqs, freqs), axis=-1)
    cols = lambda a: np.ascontiguousarray(np.repeat(a.T, H, axis=0).astype(f))
    at = np.arange(P)
    return {
        "cos": cols(np.cos(angle)), "sin": cols(np.sin(angle)),
        "identity": np.eye(P, dtype=f),
        "mask": np.where(at[None, :] > at[:, None], MASKED, 0.0).astype(f),
        "before": (at[:, None] < at[None, :]).astype(f), "ones": np.ones((P, P), f),
        "first": np.ascontiguousarray(np.broadcast_to(np.arange(E, 0, -1, dtype=f), (P, ALLT, E))),
        "start": np.ascontiguousarray(np.broadcast_to(np.arange(E, dtype=f) * CAP, (P, ALLT, E))),
    }


def layouts(a):
    flat = np.asarray(a["x"]).reshape(-1)
    before = np.concatenate([flat[:1], flat[:-1]])
    t = lambda x, *axes: np.ascontiguousarray(np.transpose(np.asarray(x), axes or None))
    side = lambda *x: np.ascontiguousarray(np.concatenate([np.asarray(v) for v in x], axis=1))
    return {
        "ids": side(flat.reshape(ALLT, P), before.reshape(ALLT, P)),
        "embed": np.asarray(a["L0_tok_embed"]), "proj_t": t(a["L0_tok_proj_w"]),
        "scale": np.ascontiguousarray(np.broadcast_to(np.asarray(a["L0_tok_scale"]), (P, 1))),
        "down_q": t(a["L0_attn_Wq_down"]), "down_k": t(a["L0_attn_Wk_down"]), "down_v": t(a["L0_attn_Wv_down"]),
        "up_q": side(a["L0_attn_Wq_up_c"], a["L0_attn_Wq_up_e"]), "up_k": side(a["L0_attn_Wk_up_c"], a["L0_attn_Wk_up_e"]),
        "up_v": np.asarray(a["L0_attn_Wv_up"]), "w_out": np.asarray(a["L0_attn_Wc"]),
        "gate_t": t(a["L0_ffn_gate_w"]),
        "we_gate": t(a["L0_ffn_we_gate"], 0, 2, 1), "we_up": t(a["L0_ffn_we_up"], 0, 2, 1),
        "we_down": t(a["L0_ffn_we_down"], 0, 2, 1),
        "ws_gate": t(a["L0_ffn_ws_gate"]), "ws_up": t(a["L0_ffn_ws_up"]), "ws_down": t(a["L0_ffn_ws_down"]),
    }


def kernel(**inputs):
    import concourse.bacc as bacc
    from concourse.bass_utils import run_bass_kernel_spmd

    nc = bacc.Bacc("TRN2", target_bir_lowering=False, num_devices=1)
    arrays = {f"in_{k}": v for k, v in {**layouts(inputs), **constants()}.items()}
    io = {k[3:]: nc.dram_tensor(k, v.shape, mybir.dt.from_np(v.dtype), kind="ExternalInput").ap() for k, v in arrays.items()}
    io["out"] = nc.dram_tensor("out", (N, C), F32, kind="ExternalOutput").ap()
    tower_kernel(nc, io)
    r = run_bass_kernel_spmd(nc, [arrays], core_ids=[0])
    return r.results[0]["out"].reshape(B, T, C)
```

```python
from contextlib import ExitStack

import numpy as np

import concourse.bass as bass
from concourse import mybir

ALU = mybir.AluOpType
ACT = mybir.ActivationFunctionType
AX = mybir.AxisListType
F32 = mybir.dt.float32
BF16 = mybir.dt.bfloat16
F32R = mybir.dt.float32r
I32 = mybir.dt.int32
U32 = mybir.dt.uint32

P = 128
BANK = 512
B, T, C = 8, 1024, 256
N = B * T
DIM = 64
H, DH, HALF = 16, 16, 8
LAT = 64
KT = C // P
TILES = T // P
ALLT = N // P
HASH_MOD = 65535
MUL_CUR, MUL_PREV = 36313, 27191
EPS = 1e-5
UH = 4
UB = H // UH
UNITS = B * UB
PARTS = 3
AUG = 6 * DH
VW = DH + 1
E, EI, TOPK = 8, 256, 2
CAP = 2560
SH = 512
CH = 512
QC = CAP // CH
FILL = E * CAP // UNITS
MASKED = -1e30

assert CAP == -(-5 * N * TOPK // (4 * E))


class Steps:

    def __init__(self, sem, names, free=1):
        self.sem, self.free, self.per = sem, free, len(names)
        self.at = {name: n + 1 for n, name in enumerate(names)}
        assert len(self.at) == self.per

    def by(self, name, run=0):
        return run * self.per + (self.at[name] + self.free)

    def last(self, name, run):
        return run * self.per + (self.at[name] + self.free - self.per)

    def before(self, run):
        return run * self.per + self.free

    def end(self, run=0):
        return run * self.per + (self.per + self.free)


class Moves:

    def __init__(self, sem, per=1, free=1):
        self.sem, self.per, self.free = sem, per, free

    def by(self, run, n=None):
        return run * (16 * self.per) + 16 * (self.free + (self.per if n is None else n))

    def before(self, run):
        return self.by(run, 0)



def prepare(nc, io, keep):
    with ExitStack() as ctx:
        sb = lambda name, shape, dt=F32: ctx.enter_context(nc.sbuf_tensor(name, shape, dt))
        sem = lambda name: ctx.enter_context(nc.semaphore(name))
        R = ALLT
        ids = sb("ids", [R, 2 * P], I32)
        ia, ib, ic, id_ = (sb(f"hash_{n}", [R, 2 * P], I32) for n in "abcd")
        hashed = sb("hashed", [R, P])
        hash_f = sb("hash_f", [R, P])
        index = keep["index"]
        identf = sb("identf_p", [P, P])
        down_t = sb("down_t", [P, 3, H // 2, C])
        up = sb("up", [P, 3, 2, 3 * HALF])
        ps = ctx.enter_context(nc.psum_tensor("ps_prepare", [P, 8, BANK], F32))
        loaded, up_loaded, down_loaded = sem("ids_loaded"), sem("up_loaded"), [sem(f"down_{m}_loaded") for m in "qkv"]
        up_zero, up_rot, chain = sem("up_zero"), sem("up_rot"), sem("hash_chain")
        index_t, index_ok, row_of_made, gathered, emb_zero = (sem(n) for n in (
            "index_t", "index_ok", "first_rows_numbered", "first_rows_gathered", "emb_zero"))
        eff_made = sem("eff_made")
        block = ctx.enter_context(nc.Block())

        @block.sync
        def _(sp):
            sp.dma_start(ids[:], io["ids"]).then_inc(loaded, 16)
            sp.dma_start(identf[:], io["identity"]).then_inc(loaded, 16)
            sp.wait_ge(up_zero, 1)
            for m, w in enumerate(("up_q", "up_k", "up_v")):
                for half in range(2):
                    sp.dma_start(up[LAT * half:LAT * (half + 1), m, half, 0:DH], io[w]).then_inc(up_loaded, 16)
            for m, w in enumerate(("down_q", "down_k", "down_v")):
                sp.dma_start(down_t[:, m], io[w].rearrange("(g p) c -> p g c", p=P)).then_inc(down_loaded[m], 16)
        @block.vector
        def _(dve):
            steps = [0]

            def link(ins):
                steps[0] += 1
                ins.then_inc(chain, 1)
                dve.wait_ge(chain, steps[0])

            ts = nc.vector.tensor_scalar
            tt = nc.vector.tensor_tensor
            nc.vector.memset(up[:], 0.0).then_inc(up_zero, 1)
            dve.wait_ge(loaded, 32)
            halves = ((slice(0, P), MUL_CUR), (slice(P, 2 * P), MUL_PREV))
            link(ts(ia[:], ids[:], 8, None, ALU.logical_shift_right))
            link(ts(ib[:], ids[:], 255, None, ALU.bitwise_and))
            for cols, mul in halves:
                link(ts(ia[:, cols], ia[:, cols], float(mul), None, ALU.mult))
                link(ts(ib[:, cols], ib[:, cols], float(mul), None, ALU.mult))
            link(ts(ic[:], ia[:], 255, 8, ALU.bitwise_and, ALU.logical_shift_left))
            link(ts(id_[:], ib[:], 65535, None, ALU.bitwise_and))
            link(tt(ic[:], ic[:], id_[:], ALU.add))
            link(ts(ia[:], ia[:], 8, None, ALU.logical_shift_right))
            link(ts(ib[:], ib[:], 16, None, ALU.logical_shift_right))
            link(tt(ia[:], ia[:], ib[:], ALU.add))
            link(ts(ib[:], ic[:], 16, None, ALU.logical_shift_right))
            link(tt(ia[:], ia[:], ib[:], ALU.add))
            link(ts(ic[:], ic[:], 65535, None, ALU.bitwise_and))
            link(tt(ia[:, 0:P], ia[:, 0:P], ia[:, P:2 * P], ALU.bitwise_xor))
            link(tt(ic[:, 0:P], ic[:, 0:P], ic[:, P:2 * P], ALU.bitwise_xor))
            link(ts(ib[:, 0:P], ia[:, 0:P], 15, None, ALU.logical_shift_right))
            link(tt(ia[:, 0:P], ia[:, 0:P], ic[:, 0:P], ALU.add))
            link(tt(ia[:, 0:P], ia[:, 0:P], ib[:, 0:P], ALU.subtract))
            link(ts(ib[:, 0:P], ia[:, 0:P], 16, None, ALU.logical_shift_right))
            link(ts(ic[:, 0:P], ia[:, 0:P], 65535, None, ALU.bitwise_and))
            link(tt(ia[:, 0:P], ib[:, 0:P], ic[:, 0:P], ALU.add))
            link(nc.vector.tensor_copy(hashed[:], ia[:, 0:P]))
            link(ts(hash_f[:], hashed[:], float(HASH_MOD), -float(HASH_MOD), ALU.is_ge, ALU.mult))
            link(tt(hashed[:], hashed[:], hash_f[:], ALU.add))
            dve.wait_ge(index_t, 1)
            link(nc.vector.tensor_copy(index[:], ps[:, 0, 0:R]))
            link(nc.vector.memset(index[0:1, 0:R:TILES], HASH_MOD))
            dve.sem_inc(index_ok, 1)

            dve.wait_ge(up_loaded, 16 * 6)
            for m in range(2):
                for half in range(2):
                    at = up[LAT * half:LAT * (half + 1), m, half]
                    ts(at[:, DH:DH + HALF:2], at[:, HALF + 1:DH:2], -1.0, None, ALU.mult).then_inc(up_rot, 1)
                    nc.vector.tensor_copy(at[:, DH + 1:DH + HALF:2], at[:, HALF:DH:2]).then_inc(up_rot, 1)
            for m in range(3):
                for ct in range(KT):
                    n = m * KT + ct
                    dve.wait_ge(eff_made, n + 1)
                    src = ps[:, 1 + n, 0:H * 3 * HALF].rearrange("p (h y d) -> p h y d", y=3, d=HALF)
                    if m < 2:
                        dst = keep["w_qk"][:, ct, m].rearrange("p y (d h) -> p h y d", d=HALF)
                        ts(dst, src, DH ** -0.5 if m == 0 else 1.0, None, ALU.mult)
                    else:
                        dst = keep["w_v"][:, ct].rearrange("p (h y d) -> p h y d", h=H, d=HALF)
                        nc.vector.tensor_copy(dst, src[:, :, 0:2, :])

        @block.gpsimd
        def _(pool):
            nc.gpsimd.memset(keep["emb"][:], 0.0).then_inc(emb_zero, 1)
            pool.wait_ge(index_ok, 1)
            nc.gpsimd.tensor_copy(keep["row_of"][:], index[:, 0:TILES]).then_inc(row_of_made, 1)
            pool.wait_ge(emb_zero, 1)
            pool.wait_ge(row_of_made, 1)
            for t in range(TILES):
                nc.gpsimd.indirect_dma_start(
                    out=keep["emb"][:, t, 0:DIM], out_offset=None, in_=io["embed"],
                    in_offset=bass.IndirectOffsetOnAxis(ap=keep["row_of"][:, t:t + 1], axis=0),
                ).then_inc(gathered, 16)
            pool.wait_ge(gathered, 16 * TILES)

        @block.tensor
        def _(pe):
            pe.wait_ge(chain, 26)
            pe.transpose(ps[:, 0, 0:R], hashed[:], identf[0:R, 0:R]).then_inc(index_t, 1)
            pe.wait_ge(up_rot, 8)
            for m in range(3):
                pe.wait_ge(down_loaded[m], 16)
                for ct in range(KT):
                    for g in range(H // 2):
                        ins = pe.matmul(ps[:, 1 + m * KT + ct, 2 * 3 * HALF * g:2 * 3 * HALF * (g + 1)],
                                        down_t[:, m, g, P * ct:P * (ct + 1)],
                                        up[:, m].rearrange("p a b -> p (a b)"), start=True, stop=True)
                    ins.then_inc(eff_made, 1)



MAX_BLOCKS = [(i, 0, min(BANK, P * (i + 1))) for i in range(TILES)] + \
             [(i, BANK, P * (i + 1) - BANK) for i in range(BANK // P, TILES)]
MAXES = UH * len(MAX_BLOCKS)
ENDS = [range(0, 4), range(8, 12)]
MAX_ORDER = [(hh, k) for hh in (0, 1) for part in ENDS for k in part] \
    + [(hh, k) for hh in range(UH) for k in range(4, 8)] \
    + [(hh, k) for hh in (2, 3) for part in ENDS for k in part]
assert sorted(MAX_ORDER) == [(hh, k) for hh in range(UH) for k in range(len(MAX_BLOCKS))]
STEPS = [(c, j) for c in range(2) for j in range(4 * (c + 1))]
NS = len(STEPS)
DIAG = [s for s, (c, j) in enumerate(STEPS) if j >= 4 * c]
PLAIN = [s for s in range(NS) if s not in DIAG]
LAST_OF = {s: c for s, (c, j) in enumerate(STEPS) if j == 4 * (c + 1) - 1}
TURN_AT = 4
TURN_BANK = 1
max_bank = lambda k: k % 3 if k < TURN_AT else (2, 0)[k % 2] if k < TURN_AT + 4 else (k - 7) % 3
MAX_AFTER, held = [], {max_bank(k): k - MAXES for k in range(MAXES)}
for k in range(MAXES):
    if k == TURN_AT:
        held[TURN_BANK] = "turn"
    MAX_AFTER.append(held[max_bank(k)])
    held[max_bank(k)] = k
assert MAX_AFTER[TURN_AT + 4] == "turn"
MAX_PER = MAXES // NS
assert MAX_PER * NS == MAXES and MAX_PER == 4


def alone(eng, sem, value, waited):
    eng.wait_ge(sem, value)
    if not isinstance(value, int):
        eng.sem_inc(waited, 1)


def at_first(x):
    return isinstance(x, int) and x == 0


def towers(nc, io, keep):
    with ExitStack() as ctx:
        sb = lambda name, shape, dt=F32: ctx.enter_context(nc.sbuf_tensor(name, shape, dt))
        sem = lambda name: ctx.enter_context(nc.semaphore(name))

        st = ctx.enter_context(nc.psum_tensor("st", [P, 4, BANK], F32))
        sm = ctx.enter_context(nc.psum_tensor("sm", [P, 3, BANK], F32))
        pv = ctx.enter_context(nc.psum_tensor("pv", [P, BANK], F32))

        identf, maskf = sb("identf", [P, P]), sb("maskf", [P, P])
        identb, maskb = sb("identb", [P, P], BF16), sb("maskb", [P, P], BF16)
        proj, scale = sb("proj", [P, C]), sb("scale", [P, 1])
        w_out, w_gate = sb("w_out", [P, KT, C]), sb("w_gate", [P, KT, E])
        cos, sin = sb("cos", [P, T]), sb("sin", [P, T])
        emb, row_of = keep["emb"], keep["row_of"]
        hx = sb("hx", [P, TILES, C])
        h = sb("h", [P, TILES, C])
        x2 = sb("x2", [P, TILES, C])
        stats, mv = sb("stats", [P, TILES, 6]), sb("mv", [P, TILES, 2])
        var, lnv, rstd, tmp = (sb(n, [P, TILES]) for n in ("var", "lnv", "rstd", "tmp"))
        big = sb("big", [P, 4, T])
        xnT = big[:, 2:4]
        yT_raw = big
        embT = sb("embT", [P, T])
        y = x2
        yT = sb("yT", [P, KT, T])
        parts = sb("parts", [P, 2, 2, PARTS, BANK], BF16)
        res = sb("res", [P, 2, 2, BANK])
        rot, rot_b = sb("rot", [P, BANK]), sb("rot_b", [P, BANK])
        v_next = sb("v_next", [P, TILES, H, DH])
        v = sb("v", [P, TILES, H * VW + DH])
        qa, ka = sb("qa", [P, UB, UH, T], BF16), sb("ka", [P, UB, UH, T], BF16)
        prob = sb("prob", [P, 4, 2, BANK])
        mx = sb("mx", [P, UH, len(MAX_BLOCKS)])
        nmax = sb("nmax", [P, UH, TILES])
        m_parts, m_res = sb("m_parts", [UH * TILES, PARTS, P], BF16), sb("m_res", [UH * TILES, P])
        rden = sb("rden", [P, 2, H])
        zero = sb("zero", [P, C])
        ones = sb("ones", [PARTS, P], BF16)

        qk = [f"{a}{s}" for s in range(4) for a in ("c", "e", "r")]
        f_pe = Steps(sem("front_pe"), ["et0", "et1", "h0", "h1", "h2", "h3", "x0", "x1", "x2", "x3"] + qk
                     + [f"v{k}" for k in range(4)])
        f_act = Steps(sem("front_act"), ["et0", "et1", "h0", "h1", "h2", "h3", "ln", "rs", "x0", "x2"]
                      + [f"{a}{s}" for s in range(4) for a in ("hc", "mc", "he", "me")] + [f"v{k}" for k in range(4)])
        norm_steps = [f"st{t}" for t in range(TILES)] + [f"ag{t}" for t in range(TILES)] + ["var", "n1", "n2", "n3", "n4"] \
            + [f"xn{t}" for t in range(TILES)]
        f_dve = Steps(sem("front_dve"), norm_steps + ["x1", "x3"]
                      + [f"{a}{s}" for s in range(4) for a in ("rc", "t1", "t2", "qe", "re")])
        f_pool = Steps(sem("front_pool"), [f"{a}{s}" for s in range(4) for a in ("lc", "le")])
        emb_loaded = Moves(sem("emb_loaded"), TILES, free=0)
        row_of_ready = Steps(sem("row_of_ready"), ["copied"])
        h_stored = Moves(sem("h_stored"))
        parts_stored = [Moves(sem("q_parts_stored"), 4), Moves(sem("k_parts_stored"), 4)]
        v_moved = Steps(sem("v_moved"), ["0", "1"])
        aug_loaded = [Moves(sem(f"aug{q}_loaded"), 9) for q in range(UB)]
        m_pe = Steps(sem("max_pe"), [f"m{k}" for k in range(MAXES)])
        m_dve = Steps(sem("max_dve"), [f"m{k}" for k in range(MAXES)])
        t_pe = Steps(sem("turn_pe"), ["t"])
        t_dve = Steps(sem("turn_dve"), ["cp", "mn", "hi", "res", "mid", "lo"])
        m_stored, m_loaded = Moves(sem("m_stored")), Moves(sem("m_loaded"))
        zeroed = Moves(sem("queues_zeroed"), UNITS)
        a_st = Steps(sem("scores"), [f"{n}" for n in range(2 * NS)])
        a_exp = Steps(sem("exps"), [f"{n}" for n in range(2 * NS)], free=2)
        a_mask = Steps(sem("masked"), [f"{2 * s + p}" for s in DIAG for p in range(2)])
        a_pv = Steps(sem("summed"), [f"{s}" for s in range(NS)], free=2)
        a_out = Steps(sem("sums_kept"), ["0", "1"])
        b_pe = Steps(sem("back_pe"), [f"yt{t}" for t in range(TILES)] + [f"z{n}" for n in range(4)]
                     + [f"w{k}" for k in range(4)] + [f"p{n}" for n in range(4)] + ["gate"])
        b_act = Steps(sem("back_act"), ["z0", "z2", "ln", "rs", "p0", "p2"])
        b_dve = Steps(sem("back_dve"), [f"{a}{t}" for t in range(TILES) for a in ("rc", "y")] + ["z1", "z3"]
                      + [f"a{k}" for k in range(4)] + norm_steps + ["p1", "p3", "gate"])
        h_loaded, h2_stored, x2_stored, x2T_stored = (Moves(sem(n)) for n in (
            "h_loaded", "h2_stored", "x2_stored", "x2T_stored"))
        first_loaded, const_loaded, const_made, ones_loaded = (sem(n) for n in (
            "first_loaded", "const_loaded", "const_made", "ones_loaded"))
        waited_sp, waited_pool, waited_dve, waited_pe = (sem(f"waited_{n}") for n in ("sp", "pool", "dve", "pe"))

        block = ctx.enter_context(nc.Block())

        def norm_beside(b, q, left):
            if q < 2 and not at_first(b):
                return b_dve, b_act, b - 1, h, x2
            if q >= 2 and left >= UB + UB - q:
                return f_dve, f_act, b + 2, hx, hx
            return None

        def in_order(eng, front1, norm, front2, maxima, attend, between, back):
            front1(0)
            norm(f_dve, f_act, 0, hx, hx)
            front2(0)
            front1(1)
            norm(f_dve, f_act, 1, hx, hx)
            maxima()
            front2(1)

            def batch(b, left):
                for q in range(UB):
                    attend(UB * b + q, b, q, UB - 1 - q + UB * left)
                    if q == 1:
                        between(b - 1, None if at_first(b) else b - 1, b + 2 if left > 1 else None)
                back(b, left > 0)
                if left > 1:
                    front2(b + 2)

            batch(0, 2)
            with eng.Fori(1, B - 2) as b:
                batch(b, 2)
            batch(B - 2, 1)
            batch(B - 1, 0)
            norm(b_dve, b_act, B - 1, h, x2)
            between(B - 1, B - 1, None)

        @block.sync
        def _(sp):
            for dst, src in ((identf[:], io["identity"]), (proj[0:DIM, :], io["proj_t"]), (scale[:], io["scale"])):
                sp.dma_start(dst, src).then_inc(first_loaded, 16)
            for dst, src in ((maskf[:], io["mask"]), (w_out[:], io["w_out"].rearrange("(k p) c -> p k c", p=P)),
                             (w_gate[:], io["gate_t"].rearrange("(k p) e -> p k e", p=P)),
                             (cos[:], io["cos"]), (sin[:], io["sin"])):
                sp.dma_start(dst, src).then_inc(const_loaded, 16)
            sp.wait_ge(const_made, 2)

            for m in (h_stored, *parts_stored, *aug_loaded, m_stored, m_loaded, zeroed,
                      h_loaded, h2_stored, x2_stored, x2T_stored):
                sp.sem_inc(m.sem, 16)

            for q in range(UB):
                sp.dma_start(ka[AUG:AUG + PARTS, q].rearrange("r h (n t) -> r (h n) t", t=P),
                             ones[:].unsqueeze(1).to_broadcast([PARTS, UH * TILES, P])).then_inc(ones_loaded, 16)
            rows = lambda name, b: keep[name].rearrange("(b t p) c -> b p t c", p=P, t=TILES)[b]

            def front1(b):
                alone(sp, f_act.sem, f_act.by("h3", b), waited_sp)
                sp.dma_start(rows("h", b), hx[:]).then_inc(h_stored.sem, 16)

            def front2(b):
                for s in range(4):
                    c, side = divmod(s, 2)
                    alone(sp, f_pool.sem, f_pool.by(f"le{s}", b), waited_sp)
                    alone(sp, f_act.sem, f_act.by(f"me{s}", b), waited_sp)
                    for y_ in range(2):
                        sp.dma_start(
                            keep["parts"][b, side, :, y_, :, BANK * c:BANK * (c + 1)].rearrange("p r t -> r p t"),
                            parts[:, side, y_]).then_inc(parts_stored[side].sem, 16)

            def load_aug(b, q):
                for side in range(2):
                    alone(sp, parts_stored[side].sem, parts_stored[side].by(b), waited_sp)
                heads = slice(UH * q, UH * (q + 1))
                features = [keep["parts"][b, side].rearrange("part y (d h) t -> (part y d) h t", h=H) for side in range(2)]
                for r0, n in ((0, 3), (3, 2), (5, 1)):
                    sp.dma_start(qa[DH * r0:DH * (r0 + n), q], features[0][0:DH * n, heads]).then_inc(aug_loaded[q].sem, 16)
                for r0, part in enumerate((0, 0, 0, 1, 1, 2)):
                    sp.dma_start(ka[DH * r0:DH * (r0 + 1), q], features[1][DH * part:DH * (part + 1), heads]
                                 ).then_inc(aug_loaded[q].sem, 16)

            def move_max(u, q):
                alone(sp, t_dve.sem, t_dve.by("lo", u), waited_sp)
                sp.dma_start(keep["max"][u].rearrange("p r q -> r p q"), m_parts[:]).then_inc(m_stored.sem, 16)
                alone(sp, m_stored.sem, m_stored.by(u), waited_sp)
                sp.dma_start(qa[AUG:AUG + PARTS, q].rearrange("p h t -> p (h t)"),
                             keep["max"][u].rearrange("p r q -> p (r q)")).then_inc(m_loaded.sem, 16)

            def maxima():
                for q in range(3):
                    load_aug(0, q)
                move_max(0, 0)

            def attend(u, b, q, left):
                alone(sp, a_st.sem, a_st.before(u), waited_sp)
                if left >= 3:
                    load_aug(b + (q + 3) // UB, (q + 3) % UB)
                if left:
                    move_max(u + 1, (q + 1) % UB)
                if q == 2:
                    alone(sp, h_stored.sem, h_stored.by(b), waited_sp)
                    if not at_first(b):
                        alone(sp, b_dve.sem, b_dve.by("xn7", b - 1), waited_sp)
                        alone(sp, h2_stored.sem, h2_stored.by(b - 1), waited_sp)
                    sp.dma_start(h[:], rows("h", b)).then_inc(h_loaded.sem, 16)
                sp.dma_start(keep["queue"].rearrange("(n p r) c -> n p r c", p=P, r=FILL // P)[u],
                             zero[:].unsqueeze(1).to_broadcast([P, FILL // P, C])).then_inc(zeroed.sem, 16)

            def between(_, old, new):
                if old is not None:
                    alone(sp, b_dve.sem, b_dve.by("xn7", old), waited_sp)
                    sp.dma_start(rows("x2", old), x2[:]).then_inc(x2_stored.sem, 16)
                if new is not None:
                    front1(new)
                if old is not None:
                    alone(sp, b_act.sem, b_act.by("p2", old), waited_sp)
                    alone(sp, b_dve.sem, b_dve.by("p3", old), waited_sp)
                    sp.dma_start(keep["x2T"].rearrange("p k (b t) -> b p k t", t=T)[old], yT[:]).then_inc(x2T_stored.sem, 16)

            def back(b, more):
                alone(sp, b_dve.sem, b_dve.by("a3", b), waited_sp)
                sp.dma_start(rows("h2", b), h[:]).then_inc(h2_stored.sem, 16)

            nothing = lambda *_: None
            in_order(sp, front1, nothing, front2, maxima, attend, between, back)
            for m in (h_stored, h2_stored, x2_stored, x2T_stored):
                alone(sp, m.sem, m.by(B - 1), waited_sp)
            alone(sp, zeroed.sem, zeroed.by(0), waited_sp)

        @block.tensor
        def _(pe):
            pe.wait_ge(first_loaded, 16 * 3)
            pe.wait_ge(const_made, 4)
            for steps in (f_pe, m_pe, t_pe, a_st, a_pv, b_pe):
                pe.sem_inc(steps.sem, steps.free)

            def embed_turn(b):
                if not at_first(b):
                    pe.wait_ge(emb_loaded.sem, emb_loaded.by(b - 1))
                for half in range(2):
                    for x in range(4):
                        ins = pe.transpose(st[:, half, P * x:P * (x + 1)], emb[:, 4 * half + x, :], identf[:])
                    ins.then_inc(f_pe.sem, 1)

            def embed(b, old):
                for k, bank in enumerate((2, 3, 0, 1)):
                    pe.wait_ge(f_act.sem, f_act.by("et0" if k < 2 else "et1", b))
                    if old is not None:
                        pe.wait_ge(*((b_dve.sem, b_dve.by(f"p{bank_turn[k]}", old)) if bank_turn[k] % 2 else
                                     (b_act.sem, b_act.by(f"p{bank_turn[k]}", old))))
                    for x in range(2):
                        t = 2 * k + x
                        ins = pe.matmul(st[:, bank, C * x:C * (x + 1)], embT[:, P * t:P * (t + 1)], proj[:],
                                        start=True, stop=True)
                    ins.then_inc(f_pe.sem, 1)

            bank_turn = (0, 1, 2, 3)

            def front1(b):
                if b:
                    pe.wait_ge(f_act.sem, f_act.end(b - 1))
                embed_turn(b)
                embed(b, None)

            def front2(b):
                if isinstance(b, int) and b < 2:
                    pe.wait_ge(f_act.sem, f_act.by("h3", b))
                else:
                    pe.wait_ge(b_dve.sem, b_dve.by("a3", b - 2))
                for ct in range(KT):
                    for half in range(2):
                        for x in range(4):
                            t = 4 * half + x
                            pe.wait_ge(f_dve.sem, f_dve.by(f"xn{t}", b))
                            ins = pe.transpose(st[:, 2 * ct + half, P * x:P * (x + 1)], hx[:, t, P * ct:P * (ct + 1)], identf[:])
                        ins.then_inc(f_pe.sem, 1)
                pe.wait_ge(f_act.sem, f_act.by("x2", b))
                pe.wait_ge(f_dve.sem, f_dve.by("x3", b))
                readers = ("rc", "t1", "t2")
                for s in range(4):
                    c, side = divmod(s, 2)
                    for k in range(3):
                        n = 3 * s + k
                        if n >= 4:
                            pe.wait_ge(f_dve.sem, f_dve.by(f"{readers[(n - 4) % 3]}{(n - 4) // 3}", b))
                        for ct in range(KT):
                            ins = pe.matmul(st[:, n % 4, :], keep["w_qk"][:, ct, side, k], xnT[:, ct, BANK * c:BANK * (c + 1)],
                                            start=(ct == 0), stop=(ct == KT - 1))
                        ins.then_inc(f_pe.sem, 1)
                for k in range(4):
                    n = 8 + k
                    pe.wait_ge(f_dve.sem, f_dve.by(f"{readers[n % 3]}{n // 3}", b))
                    for q in range(2):
                        t = 2 * k + q
                        for ct in range(KT):
                            ins = pe.matmul(st[:, k, C * q:C * (q + 1)], xnT[:, ct, P * t:P * (t + 1)], keep["w_v"][:, ct],
                                            start=(ct == 0), stop=(ct == KT - 1))
                    ins.then_inc(f_pe.sem, 1)

            def max_block(u, slot, k):
                hh, kk = MAX_ORDER[k]
                i, k0, w = MAX_BLOCKS[kk]
                last = MAX_AFTER[k]
                if last == "turn":
                    if not at_first(u):
                        pe.wait_ge(t_dve.sem, t_dve.by("res", u - 1))
                elif last >= 0:
                    pe.wait_ge(m_dve.sem, m_dve.by(f"m{last}", u))
                elif not at_first(u):
                    pe.wait_ge(m_dve.sem, m_dve.by(f"m{last + MAXES}", u - 1))
                diag = k0 + w == P * (i + 1)
                ins = pe.matmul(sm[:, max_bank(k), 0:w], qa[0:AUG, slot, hh, P * i:P * (i + 1)], ka[0:AUG, slot, hh, k0:k0 + w],
                                start=True, stop=not diag)
                if diag:
                    ins = pe.matmul(sm[:, max_bank(k), w - P:w], identb[:], maskb[:], start=False, stop=True)
                ins.then_inc(m_pe.sem, 1)

            def max_turn(u):
                alone(pe, t_dve.sem, t_dve.by("mn", u), waited_pe)
                pe.transpose(sm[0:UH * TILES, 1, 0:P], nmax[:].rearrange("p h t -> p (h t)"), identf[:]).then_inc(t_pe.sem, 1)

            def maxima():
                pe.wait_ge(const_loaded, 16 * 5)
                pe.wait_ge(const_made, 6)
                for u in range(2):
                    pe.wait_ge(aug_loaded[u].sem, aug_loaded[u].by(0))
                    for k in range(MAXES):
                        if u and k == TURN_AT:
                            pe.wait_ge(m_dve.sem, m_dve.by(f"m{TURN_AT - 3}", u))
                            max_turn(0)
                        max_block(u, u, k)

            def attend(u, b, q, left):
                pe.wait_ge(m_loaded.sem, m_loaded.by(u))
                if q == 0:
                    pe.wait_ge(v_moved.sem, v_moved.end(b))
                    if left >= UB:
                        pe.wait_ge(f_act.sem, f_act.end(b + 1))
                    else:
                        pe.wait_ge(b_dve.sem, b_dve.by("a3", b - 1))
                if at_first(u):
                    pe.wait_ge(ones_loaded, 16 * UB)
                if q == 2:
                    if left >= UB + 2:
                        pe.wait_ge(f_act.sem, f_act.by("h3", b + 2))
                    if not at_first(b):
                        pe.wait_ge(b_act.sem, b_act.end(b - 1))
                        pe.wait_ge(b_dve.sem, b_dve.end(b - 1))

                def scores(s, p):
                    c, j = STEPS[s]
                    off = max(0, P * j - BANK * c)
                    n = 2 * s + p
                    pe.wait_ge(a_exp.sem, a_exp.by(str(n), u) - 2)
                    for x in range(2):
                        hh = 2 * p + x
                        ins = pe.matmul(st[:, hh, off:BANK], ka[0:AUG + PARTS, q, hh, P * j:P * (j + 1)],
                                        qa[0:AUG + PARTS, q, hh, BANK * c + off:BANK * (c + 1)], start=True, stop=True)
                    ins.then_inc(a_st.sem, 1)

                def sums(u, q, s):
                    c, j = STEPS[s]
                    off = max(0, P * j - BANK * c)
                    if j == 0:
                        pe.wait_ge(a_out.sem, a_out.by(str(c), u) - 1)
                    if s in DIAG:
                        pe.wait_ge(a_mask.sem, a_mask.by(str(2 * s + 1), u))
                    else:
                        pe.wait_ge(a_exp.sem, a_exp.by(str(2 * s + 1), u))
                    for x in range(UH):
                        hh = UH * q + x
                        ins = pe.matmul(pv[32 * x:32 * (x + 1), off:BANK], v[:, j, VW * hh:VW * hh + 32],
                                        prob[:, (2 * s + x // 2) % 4, x % 2, off:BANK],
                                        start=(j == 0), stop=(j == 4 * (c + 1) - 1))
                    ins.then_inc(a_pv.sem, 1)

                if left >= 2:
                    slot = (q + 2) % UB
                    pe.wait_ge(aug_loaded[slot].sem, aug_loaded[slot].by(b + (q + 2) // UB))
                for s in range(NS):
                    blocks = [k for k in range(MAX_PER * s, MAX_PER * (s + 1)) if left >= 2]
                    for p in range(2):
                        scores(s, p)
                        if s * MAX_PER == TURN_AT and p == 0 and left:
                            if left >= 2:
                                pe.wait_ge(m_dve.sem, m_dve.by(f"m{TURN_AT - 3}", u + 2))
                            max_turn(u + 1)
                        for k in blocks[p:p + 1]:
                            max_block(u + 2, (q + 2) % UB, k)
                    if s:
                        sums(u, q, s - 1)
                    elif q % 2:
                        sums(u - 1, q - 1, NS - 1)
                    for k in blocks[2:]:
                        max_block(u + 2, (q + 2) % UB, k)
                if q % 2:
                    sums(u, q, NS - 1)

            def back(b, more):
                pe.wait_ge(a_out.sem, a_out.before(UB * b + UB))
                pe.wait_ge(a_exp.sem, a_exp.before(UB * b + UB))
                for t in range(TILES):
                    if t >= 4:
                        pe.wait_ge(b_dve.sem, b_dve.by(f"y{t - 4}", b))
                    for g in range(4):
                        ins = pe.transpose(st[:, t % 4, P * g:P * (g + 1)], yT_raw[:, g, P * t:P * (t + 1)], identf[:])
                    ins.then_inc(b_pe.sem, 1)
                for n in range(4):
                    half, ct = divmod(n, 2)
                    pe.wait_ge(b_dve.sem, b_dve.by(f"y{4 + n if n < 2 else 7}", b))
                    for q in range(4):
                        ins = pe.transpose(st[:, n, P * q:P * (q + 1)], y[:, 4 * half + q, P * ct:P * (ct + 1)], identf[:])
                    ins.then_inc(b_pe.sem, 1)
                pe.wait_ge(b_act.sem, b_act.by("z2", b))
                pe.wait_ge(b_dve.sem, b_dve.by("z3", b))
                for k in range(4):
                    for q in range(2):
                        t = 2 * k + q
                        for ct in range(KT):
                            ins = pe.matmul(st[:, k, C * q:C * (q + 1)], yT[:, ct, P * t:P * (t + 1)], w_out[:, ct],
                                            start=(ct == 0), stop=(ct == KT - 1))
                    ins.then_inc(b_pe.sem, 1)

            def between(b, old, new):
                if isinstance(b, int) and b == B - 1:
                    pe.wait_ge(b_dve.sem, b_dve.by("a3", b))
                else:
                    pe.wait_ge(a_exp.sem, a_exp.before(UB * b + UB + 2))
                if new is not None:
                    embed_turn(new)
                if old is not None:
                    pe.wait_ge(b_dve.sem, b_dve.by("xn7", old))
                    for n, bank in enumerate((2, 3, 0, 1)):
                        half, ct = divmod(n, 2)
                        if new is not None and n >= 2:
                            pe.wait_ge(f_act.sem, f_act.by(f"et{bank}", new))
                        for x in range(4):
                            ins = pe.transpose(st[:, bank, P * x:P * (x + 1)], x2[:, 4 * half + x, P * ct:P * (ct + 1)], identf[:])
                        ins.then_inc(b_pe.sem, 1)
                if new is not None:
                    embed(new, old)
                if old is not None:
                    if new is not None:
                        pe.wait_ge(f_act.sem, f_act.by("h0", new))
                    pe.wait_ge(b_act.sem, b_act.by("p2", old))
                    pe.wait_ge(b_dve.sem, b_dve.by("p3", old))
                    for t in range(TILES):
                        for ct in range(KT):
                            ins = pe.matmul(st[:, 2, E * t:E * (t + 1)], yT[:, ct, P * t:P * (t + 1)], w_gate[:, ct],
                                            start=(ct == 0), stop=(ct == KT - 1))
                    ins.then_inc(b_pe.sem, 1)

            in_order(pe, front1, lambda *_: None, front2, maxima, attend, between, back)

        @block.scalar
        def _(act):
            a = nc.scalar.activation
            act.wait_ge(first_loaded, 16 * 3)
            for steps in (f_act, a_exp, a_out, b_act):
                act.sem_inc(steps.sem, steps.free)

            def embed_turn(b):
                for k in range(2):
                    act.wait_ge(f_pe.sem, f_pe.by(f"et{k}", b))
                    a(embT[:, BANK * k:BANK * (k + 1)], st[:, k, :], ACT.Copy).then_inc(f_act.sem, 1)

            def embed(b):
                for k, bank in enumerate((2, 3, 0, 1)):
                    act.wait_ge(f_pe.sem, f_pe.by(f"h{k}", b))
                    a(hx[:, 2 * k:2 * k + 2, :].rearrange("p t c -> p (t c)"), st[:, bank, :], ACT.Identity,
                      scale=scale[:, 0:1]).then_inc(f_act.sem, 1)

            def front1(b):
                embed_turn(b)
                embed(b)

            def front2(b):
                for k in (0, 2):
                    act.wait_ge(f_pe.sem, f_pe.by(f"x{k}", b))
                    a(xnT[:, k // 2, 0:BANK], st[:, k, :], ACT.Copy).then_inc(f_act.sem, 1)
                for s in range(4):
                    c, side = divmod(s, 2)
                    act.wait_ge(parts_stored[side].sem, parts_stored[side].by(b, 2 * (s // 2)))
                    act.wait_ge(f_pe.sem, f_pe.by(f"c{s}", b))
                    a(parts[:, side, 0, 0, :], st[:, 3 * s % 4, :], ACT.Copy).then_inc(f_act.sem, 1)
                    act.wait_ge(f_dve.sem, f_dve.by(f"rc{s}", b))
                    a(parts[:, side, 0, 1, :], res[:, s % 2, 0, :], ACT.Copy).then_inc(f_act.sem, 1)
                    act.wait_ge(f_dve.sem, f_dve.by(f"qe{s}", b))
                    a(parts[:, side, 1, 0, :], rot[:], ACT.Copy).then_inc(f_act.sem, 1)
                    act.wait_ge(f_dve.sem, f_dve.by(f"re{s}", b))
                    a(parts[:, side, 1, 1, :], res[:, s % 2, 1, :], ACT.Copy).then_inc(f_act.sem, 1)
                act.wait_ge(v_moved.sem, v_moved.before(b))
                for k in range(4):
                    act.wait_ge(f_pe.sem, f_pe.by(f"v{k}", b))
                    a(v_next[:, 2 * k:2 * k + 2].rearrange("p t h d -> p (t h d)"), st[:, k, :], ACT.Copy).then_inc(f_act.sem, 1)

            def rsqrt(dve_steps, act_steps, b, *_):
                act.wait_ge(dve_steps.sem, dve_steps.by("var", b))
                a(lnv[:], var[:], ACT.Ln).then_inc(act_steps.sem, 1)
                act.wait_ge(act_steps.sem, act_steps.by("ln", b))
                a(rstd[:], lnv[:], ACT.Exp, scale=-0.5).then_inc(act_steps.sem, 1)

            def attend(u, b, q, left):
                norm = norm_beside(b, q, left)

                def sums_out(u, q, c):
                    if q == c == 0:
                        if left >= UB:
                            act.wait_ge(f_pe.sem, f_pe.end(b + 1))
                        else:
                            act.wait_ge(b_pe.sem, b_pe.by("yt7", b - 1))
                    s = max(s_ for s_, c_ in LAST_OF.items() if c_ == c)
                    act.wait_ge(a_pv.sem, a_pv.by(str(s), u))
                    a(yT_raw[:, q, BANK * c:BANK * (c + 1)], pv[:], ACT.Copy).then_inc(a_out.sem, 1)

                for s, (c, j) in enumerate(STEPS):
                    if norm and q % 2 == 0 and s == NS - 1:
                        rsqrt(*norm)
                    off = max(0, P * j - BANK * c)
                    act.wait_ge(a_pv.sem, a_pv.by(str(s), u) - 2)
                    for p in range(2):
                        n = 2 * s + p
                        act.wait_ge(a_st.sem, a_st.by(str(n), u))
                        a(prob[:, n % 4, :, off:BANK], st[:, 2 * p:2 * p + 2, off:BANK], ACT.Exp).then_inc(a_exp.sem, 1)
                    if s == 0 and q % 2:
                        sums_out(u - 1, q - 1, 1)
                    if s - 1 in LAST_OF:
                        sums_out(u, q, LAST_OF[s - 1])
                if q % 2:
                    sums_out(u, q, 1)

            def between(_, old, new):
                if new is not None:
                    embed_turn(new)
                if old is not None:
                    for n, bank in ((0, 2), (2, 0)):
                        half, ct = divmod(n, 2)
                        act.wait_ge(b_pe.sem, b_pe.by(f"p{n}", old))
                        a(yT[:, ct, BANK * half:BANK * (half + 1)], st[:, bank, :], ACT.Copy).then_inc(b_act.sem, 1)
                if new is not None:
                    embed(new)

            def back(b, more):
                act.wait_ge(x2T_stored.sem, x2T_stored.before(b))
                for n in (0, 2):
                    half, ct = divmod(n, 2)
                    act.wait_ge(b_pe.sem, b_pe.by(f"z{n}", b))
                    a(yT[:, ct, BANK * half:BANK * (half + 1)], st[:, n, :], ACT.Copy).then_inc(b_act.sem, 1)

            in_order(act, front1, rsqrt, front2, lambda: None, attend, between, back)

        @block.gpsimd
        def _(pool):
            for steps in (f_pool, a_mask, row_of_ready):
                pool.sem_inc(steps.sem, steps.free)

            def rows_of(b):
                if not (isinstance(b, int) and b == 1):
                    alone(pool, emb_loaded.sem, emb_loaded.before(b - 1), waited_pool)
                nc.gpsimd.tensor_copy(row_of[:], keep["index"][:, bass.ds(b * TILES, TILES)]).then_inc(row_of_ready.sem, 1)

            def gather(b, tiles):
                alone(pool, row_of_ready.sem, row_of_ready.before(b), waited_pool)
                for t in tiles:
                    nc.gpsimd.indirect_dma_start(
                        out=emb[:, t, 0:DIM], out_offset=None, in_=io["embed"],
                        in_offset=bass.IndirectOffsetOnAxis(ap=row_of[:, t:t + 1], axis=0),
                    ).then_inc(emb_loaded.sem, 16)

            rows_of(1)
            alone(pool, f_pe.sem, f_pe.by("et1", 0), waited_pool)
            gather(1, range(TILES))

            def front2(b):
                for s in range(4):
                    c, side = divmod(s, 2)
                    stored = parts_stored[side]
                    alone(pool, stored.sem, stored.by(b, 2 * (s // 2)), waited_pool)
                    for y_, (r, m_) in enumerate((("rc", "mc"), ("re", "me"))):
                        alone(pool, f_dve.sem, f_dve.by(f"{r}{s}", b), waited_pool)
                        alone(pool, f_act.sem, f_act.by(f"{m_}{s}", b), waited_pool)
                        nc.gpsimd.tensor_tensor(parts[:, side, y_, 2, :], res[:, s % 2, y_, :], parts[:, side, y_, 1, :],
                                                ALU.subtract).then_inc(f_pool.sem, 1)

            def attend(u, b, q, left):
                ahead = q < 2 and left >= UB + UB - q
                if ahead and q == 0:
                    alone(pool, f_pe.sem, f_pe.by("et1", b + 1), waited_pool)
                    rows_of(b + 2)
                for s in range(NS):
                    c, j = STEPS[s]
                    if s in DIAG:
                        off = P * j - BANK * c
                        for p in range(2):
                            n = 2 * s + p
                            alone(pool, a_exp.sem, a_exp.by(str(n), u), waited_pool)
                            at = prob[:, n % 4, :, off:off + P]
                            nc.gpsimd.affine_select(out=at, in_=at, compare_op=ALU.is_ge, fill=0.0, base=0,
                                                    pattern=[[0, 2], [1, P]], channel_multiplier=-1).then_inc(a_mask.sem, 1)
                    elif ahead and s == PLAIN[0]:
                        gather(b + 2, range(4 * q, 4 * q + 4))

            nothing = lambda *_: None
            in_order(pool, nothing, nothing, front2, nothing, attend, nothing, nothing)

        @block.vector
        def _(dve):
            ts, tt = nc.vector.tensor_scalar, nc.vector.tensor_tensor
            nc.vector.memset(ones[:], 1.0).then_inc(const_made, 1)
            nc.vector.memset(zero[:], 0.0).then_inc(const_made, 1)
            nc.vector.memset(v[:], 1.0).then_inc(const_made, 1)
            nc.vector.memset(proj[64:P, :], 0.0).then_inc(const_made, 1)
            for steps in (f_dve, m_dve, t_dve, b_dve, v_moved):
                dve.sem_inc(steps.sem, steps.free)
            dve.wait_ge(first_loaded, 16 * 3)
            dve.wait_ge(const_loaded, 16 * 5)
            nc.vector.tensor_copy(identb[:], identf[:]).then_inc(const_made, 1)
            nc.vector.tensor_copy(maskb[:], maskf[:]).then_inc(const_made, 1)
            dve.wait_ge(const_made, 6)

            def norm_stats(steps, run, src, tiles):
                for t in tiles:
                    nc.vector.bn_stats(stats[:, t, :], src[:, t, :]).then_inc(steps.sem, 1)

            def norm_var(steps, run):
                for t in range(TILES):
                    alone(dve, steps.sem, steps.by(f"st{t}", run), waited_dve)
                    nc.vector.bn_aggr(mv[:, t, :], stats[:, t, :]).then_inc(steps.sem, 1)
                dve.wait_ge(steps.sem, steps.by("ag7", run))
                ts(var[:], mv[:, :, 1], EPS, None, ALU.add).then_inc(steps.sem, 1)

            def norm_root(steps, act_steps, run):
                dve.wait_ge(act_steps.sem, act_steps.by("rs", run))
                dve.wait_ge(steps.sem, steps.by("var", run))
                tt(tmp[:], rstd[:], rstd[:], ALU.mult).then_inc(steps.sem, 1)
                dve.wait_ge(steps.sem, steps.by("n1", run))
                tt(tmp[:], tmp[:], var[:], ALU.mult).then_inc(steps.sem, 1)
                dve.wait_ge(steps.sem, steps.by("n2", run))
                ts(tmp[:], tmp[:], -0.5, 1.5, ALU.mult, ALU.add).then_inc(steps.sem, 1)
                dve.wait_ge(steps.sem, steps.by("n3", run))
                tt(rstd[:], rstd[:], tmp[:], ALU.mult).then_inc(steps.sem, 1)
                dve.wait_ge(steps.sem, steps.by("n4", run))

            def norm_place(steps, run):
                if steps is f_dve:
                    dve.wait_ge(h_stored.sem, h_stored.by(run))
                else:
                    dve.wait_ge(x2_stored.sem, x2_stored.before(run))

            def norm_apply(steps, run, src, out, tiles):
                for t in tiles:
                    ts(out[:, t, :], src[:, t, :], mv[:, t, 0:1], rstd[:, t:t + 1], ALU.subtract, ALU.mult).then_inc(steps.sem, 1)

            def norm_done(steps, run):
                dve.wait_ge(steps.sem, steps.by(f"xn{TILES - 1}", run))

            def norm_input(steps, run):
                if steps is f_dve:
                    dve.wait_ge(f_act.sem, f_act.by("h3", run))
                else:
                    dve.wait_ge(b_dve.sem, b_dve.by("a3", run))

            def norm(steps, act_steps, run, src, out):
                norm_input(steps, run)
                norm_stats(steps, run, src, range(TILES))
                norm_var(steps, run)
                norm_root(steps, act_steps, run)
                norm_place(steps, run)
                norm_apply(steps, run, src, out, range(TILES))
                norm_done(steps, run)

            def front2(b):
                for k in (1, 3):
                    dve.wait_ge(f_pe.sem, f_pe.by(f"x{k}", b))
                    nc.vector.tensor_copy(xnT[:, k // 2, BANK:], st[:, k, :]).then_inc(f_dve.sem, 1)
                for s in range(4):
                    c, side = divmod(s, 2)
                    cols = slice(BANK * c, BANK * (c + 1))
                    bank = [(3 * s + k) % 4 for k in range(3)]
                    dve.wait_ge(f_pool.sem, f_pool.by(f"le{s - 2}", b) if s >= 2 else f_pool.before(b))
                    dve.wait_ge(f_act.sem, f_act.by(f"hc{s}", b))
                    tt(res[:, s % 2, 0, :], st[:, bank[0], :], parts[:, side, 0, 0, :], ALU.subtract).then_inc(f_dve.sem, 1)
                    dve.wait_ge(f_pe.sem, f_pe.by(f"e{s}", b))
                    tt(rot[:], st[:, bank[1], :], cos[:, cols], ALU.mult).then_inc(f_dve.sem, 1)
                    dve.wait_ge(f_pe.sem, f_pe.by(f"r{s}", b))
                    tt(rot_b[:], st[:, bank[2], :], sin[:, cols], ALU.mult).then_inc(f_dve.sem, 1)
                    dve.wait_ge(f_dve.sem, f_dve.by(f"t2{s}", b))
                    tt(rot[:], rot[:], rot_b[:], ALU.add).then_inc(f_dve.sem, 1)
                    dve.wait_ge(f_dve.sem, f_dve.by(f"qe{s}", b))
                    dve.wait_ge(f_act.sem, f_act.by(f"he{s}", b))
                    tt(res[:, s % 2, 1, :], rot[:], parts[:, side, 1, 0, :], ALU.subtract).then_inc(f_dve.sem, 1)
                    dve.wait_ge(f_dve.sem, f_dve.by(f"re{s}", b))
                if at_first(b):
                    move_v(0)

            def move_v(b):
                dve.wait_ge(f_act.sem, f_act.end(b))
                out = v[:, :, 0:H * VW].rearrange("p t (h d) -> p t h d", d=VW)
                for k in range(2):
                    tiles = slice(4 * k, 4 * k + 4)
                    nc.vector.tensor_copy(out[:, tiles, :, 0:DH], v_next[:, tiles]).then_inc(v_moved.sem, 1)

            def max_block(u, k):
                hh, kk = MAX_ORDER[k]
                w = MAX_BLOCKS[kk][2]
                dve.wait_ge(m_pe.sem, m_pe.by(f"m{k}", u))
                nc.vector.tensor_reduce(mx[:, hh, kk:kk + 1], sm[:, max_bank(k), 0:w], AX.X, ALU.max, negate=True).then_inc(m_dve.sem, 1)

            def max_end(u):
                dve.wait_ge(m_dve.sem, m_dve.by(f"m{MAXES - 1}", u))
                x = BANK // P
                nc.vector.tensor_copy(nmax[:, :, 0:x], mx[:, :, 0:x]).then_inc(t_dve.sem, 1)
                tt(nmax[:, :, x:], mx[:, :, x:2 * x], mx[:, :, 2 * x:], ALU.min).then_inc(t_dve.sem, 1)
                dve.wait_ge(t_dve.sem, t_dve.by("mn", u))

            def max_parts(u):
                dve.wait_ge(t_pe.sem, t_pe.by("t", u))
                dve.wait_ge(m_stored.sem, m_stored.before(u))
                turned = sm[0:UH * TILES, 1, 0:P]
                nc.vector.tensor_copy(m_parts[:, 0, :], turned).then_inc(t_dve.sem, 1)
                dve.wait_ge(t_dve.sem, t_dve.by("hi", u))
                tt(m_res[:], turned, m_parts[:, 0, :], ALU.subtract).then_inc(t_dve.sem, 1)
                dve.wait_ge(t_dve.sem, t_dve.by("res", u))
                nc.vector.tensor_copy(m_parts[:, 1, :], m_res[:]).then_inc(t_dve.sem, 1)
                dve.wait_ge(t_dve.sem, t_dve.by("mid", u))
                tt(m_parts[:, 2, :], m_res[:], m_parts[:, 1, :], ALU.subtract).then_inc(t_dve.sem, 1)

            def maxima():
                for u in range(2):
                    for k in range(MAXES):
                        if u and k == TURN_AT:
                            max_parts(0)
                        max_block(u, k)
                    if u == 0:
                        max_end(0)

            def attend(u, b, q, left):
                beside = norm_beside(b, q, left)

                def norm_step(s):
                    if not beside:
                        return
                    steps, act_steps, run, src, out = beside
                    if q % 2 == 0:
                        if s == 0:
                            norm_input(steps, run)
                        if s < TILES:
                            norm_stats(steps, run, src, [s])
                        if s == TILES:
                            norm_var(steps, run)
                    else:
                        if s == 0:
                            norm_root(steps, act_steps, run)
                        if s == 2:
                            norm_place(steps, run)
                        if 2 <= s < TILES + 2:
                            norm_apply(steps, run, src, out, [s - 2])
                        if s == TILES + 2:
                            norm_done(steps, run)

                if left:
                    max_end(u + 1)
                for s in range(NS):
                    if s * MAX_PER == TURN_AT and left:
                        max_parts(u + 1)
                    for k in range(MAX_PER * s, MAX_PER * (s + 1)):
                        if left >= 2:
                            max_block(u + 2, k)
                    norm_step(s)

            def back(b, more):
                dve.wait_ge(x2_stored.sem, x2_stored.before(b))
                for t in range(TILES):
                    dve.wait_ge(b_pe.sem, b_pe.by(f"yt{t}", b))
                    src = st[:, t % 4, :].rearrange("p (h d) -> p h d", d=32)
                    if t >= 2:
                        dve.wait_ge(b_dve.sem, b_dve.by(f"y{t - 2}", b))
                    nc.vector.reciprocal(rden[:, t % 2, :], src[:, :, DH]).then_inc(b_dve.sem, 1)
                    dve.wait_ge(b_dve.sem, b_dve.by(f"rc{t}", b))
                    tt(y[:, t, :].rearrange("p (h d) -> p h d", d=DH), src[:, :, 0:DH],
                       rden[:, t % 2, :].unsqueeze(2).to_broadcast([P, H, DH]), ALU.mult).then_inc(b_dve.sem, 1)
                dve.wait_ge(x2T_stored.sem, x2T_stored.before(b))
                for n in (1, 3):
                    half, ct = divmod(n, 2)
                    dve.wait_ge(b_pe.sem, b_pe.by(f"z{n}", b))
                    nc.vector.tensor_copy(yT[:, ct, BANK * half:BANK * (half + 1)], st[:, n, :]).then_inc(b_dve.sem, 1)
                dve.wait_ge(h_loaded.sem, h_loaded.by(b))
                for k in range(4):
                    dve.wait_ge(b_pe.sem, b_pe.by(f"w{k}", b))
                    at = h[:, 2 * k:2 * k + 2, :].rearrange("p t c -> p (t c)")
                    tt(at, st[:, k, :], at, ALU.add).then_inc(b_dve.sem, 1)
                if more:
                    dve.wait_ge(a_pv.sem, a_pv.before(UB * b + UB))
                    move_v(b + 1)

            def between(_, old, new):
                if old is None:
                    return
                for n, bank in ((1, 3), (3, 1)):
                    half, ct = divmod(n, 2)
                    dve.wait_ge(b_pe.sem, b_pe.by(f"p{n}", old))
                    nc.vector.tensor_copy(yT[:, ct, BANK * half:BANK * (half + 1)], st[:, bank, :]).then_inc(b_dve.sem, 1)
                dve.wait_ge(b_pe.sem, b_pe.by("gate", old))
                nc.vector.tensor_copy(keep["logits"][:, bass.ds(old * (TILES * E), TILES * E)], st[:, 2, 0:TILES * E]).then_inc(b_dve.sem, 1)

            in_order(dve, lambda b: None, norm, front2, maxima, attend, between, back)



FIRST, SECOND = 5, 3
RS, SRING = ALLT // (FIRST - 1), 4
RING = 7
RG = 2 * RING
FULL, REST = divmod(ALLT, RG)
AHEAD = 5
ITEMS = 2 * QC
MS, QT = SH // P, CH // P
SPLIT_AT = (5, 7)
SHARED = [f"{x}a{m}" for x in range(2) for m in range(MS)] + [f"{x}o{k}" for x in range(2) for k in range(2)]
assert all(RG * (i + 1) + AHEAD <= 2 * QT * (FIRST + i) for i in range(SECOND)) and FULL >= SECOND and REST > 0


def products(pe, out, w, x, contraction):
    for ct in range(contraction):
        (wh, wl), (xh, xl) = w(ct), x(ct)
        for n, (a, b) in enumerate(((wh, xh), (wh, xl), (wl, xh))):
            ins = pe.matmul(out, a, b, start=(ct == n == 0), stop=(ct == contraction - 1 and n == 2))
    return ins


def beside(step, tiles):
    return range(tiles * step // len(SHARED), tiles * (step + 1) // len(SHARED))


def experts(nc, io, keep):
    with ExitStack() as ctx:
        sb = lambda name, shape, dt=F32: ctx.enter_context(nc.sbuf_tensor(name, shape, dt))
        sem = lambda name: ctx.enter_context(nc.semaphore(name))
        tr = ctx.enter_context(nc.psum_tensor("tr", [P, KT, BANK], F32))
        gu = ctx.enter_context(nc.psum_tensor("gu", [P, 4, BANK], F32))
        dn = ctx.enter_context(nc.psum_tensor("dn", [P, 2, BANK], F32))
        identf = sb("identf_e", [P, P])
        room = sb("room", [P, RING * TOPK * C])
        ws = room[:, 0:2 * KT * SH].rearrange("p (n k i) -> p n k i", n=2, k=KT)
        ws_h, ws_l = sb("ws_h", [P, 2, KT, SH], F32R), sb("ws_l", [P, 2, KT, SH], F32R)
        wsd = sb("wsd", [P, MS, C])
        xs_h, xs_l = sb("xs_h", [P, 2, KT, CH], F32R), sb("xs_l", [P, 2, KT, CH], F32R)
        xs, hs = sb("xs", [P, 2, KT, CH]), sb("hs", [P, 2, QT, C])
        sil = sb("sil", [P, 2, CH])
        inner = sb("inner", [P, 2, MS, CH])
        out_s = sb("out_s", [P, 2, QT, C])
        row = sb("row", [P, RING, C])
        g_row = room[:].rearrange("p (k n c) -> p k n c", k=RING, n=TOPK)
        done = sb("done", [P, RING, C])
        idx = sb("idx", [P, RS, TOPK], U32)
        w_now = sb("w_now", [P, RG, TOPK])
        we, wed = sb("we", [P, 2, 2, KT, EI]), sb("wed", [P, 2, KT, EI])
        we_h, we_l = sb("we_h", [P, 2, 2, KT, EI], F32R), sb("we_l", [P, 2, 2, KT, EI], F32R)
        xg = sb("xg", [P, 2, QT, C])
        xg_h, xg_l = sb("xg_h", [P, 2, KT, CH], F32R), sb("xg_l", [P, 2, KT, CH], F32R)
        e_sil, e_in = sb("e_sil", [P, 2, CH]), sb("e_in", [P, 2, KT, CH])
        eo = sb("eo", [P, 2, QT, C])

        places = [t[:, n].rearrange("p a b -> p (a b)")[:, half * BANK:(half + 1) * BANK].rearrange("p (t e) -> p t e", e=E)
                  for t in (xg, eo, e_in) for n in range(2) for half in range(2)]
        ex, eq, l2, sel, hot0, hot1, pre_a, pre_b, pos, rtmp = places[:10]
        hot = (hot0, hot1)
        lg = keep["logits"][:].rearrange("p (t e) -> p t e", e=E)
        falling, starts = sb("falling", [P, E]), sb("starts", [P, E])
        first, start = (t[:].unsqueeze(1).to_broadcast([P, ALLT, E]) for t in (falling, starts))
        best, total = sb("best", [P, ALLT]), sb("total", [P, ALLT])
        pk, kept, slot, gone, score = (sb(n, [P, ALLT, TOPK]) for n in ("pk", "kept", "slot", "gone", "score"))
        before, ones = sb("before", [P, P]), sb("ones_e", [P, P])
        route_loaded, chain, shifted, exped, sel_ready, counted, routed = (sem(n) for n in (
            "route_loaded", "route_chain", "shifted_ready", "exp_ready", "sel_ready", "counts_ready", "routed"))
        s_pe = Steps(sem("shared_pe"), [f"{x}g{m}" for x in range(2) for m in range(MS)] + [f"{x}d{k}" for x in range(2) for k in range(2)])
        s_act = Steps(sem("shared_act"), [f"{x}s{m}" for x in range(2) for m in range(MS)])
        s_dve = Steps(sem("shared_dve"), SHARED)
        x_act = Steps(sem("shared_x_high"), ["0", "1"])
        x_dve = Steps(sem("shared_x_low"), ["0", "1"])
        ws_high, ws_low = sem("shared_weights_high"), sem("shared_weights_low")
        xs_loaded = [Moves(sem(f"xs{x}_loaded")) for x in range(2)]
        hs_loaded = [Moves(sem(f"hs{x}_loaded")) for x in range(2)]
        sum_stored = [Moves(sem(f"sum{x}_stored")) for x in range(2)]
        const_loaded, ws_loaded = sem("const_e_loaded"), sem("shared_weights_loaded")
        waited_sp, waited_pool = sem("waited_sp_e"), sem("waited_pool_e")
        idx_ready = Steps(sem("idx_ready"), ["0", "1"])
        row_loaded = [Moves(sem(f"row{k}_loaded"), RS // SRING) for k in range(SRING)]
        scattered = [Moves(sem(f"row{k}_scattered"), TOPK * RS // SRING, free=0) for k in range(SRING)]
        gathered = [Moves(sem(f"row{k}_gathered"), TOPK * RG // RING, free=0) for k in range(RING)]
        base_loaded = [Moves(sem(f"base{k}_loaded"), RG // RING) for k in range(RING)]
        out_stored = [Moves(sem(f"out{k}_stored"), RG // RING) for k in range(RING)]
        w_ready = Steps(sem("w_ready"), ["copied"])
        half_sum = Steps(sem("half_sum"), [f"{t}" for t in range(RG)])
        combined = Steps(sem("combined"), [f"{t}" for t in range(RG)], free=RING)
        e_pe = Steps(sem("expert_pe"), [n for x in range(ITEMS) for n in (
            f"g{x}_0", f"g{x}_1", f"t{x + 1}", f"d{x}_0", f"d{x}_1")], free=3)
        e_act = Steps(sem("expert_act"), [n for x in range(ITEMS) for n in (
            f"s{x}_0", f"s{x}_1", f"t{x + 1}_0", f"t{x + 1}_1", f"o{x}")], free=3)
        e_dve = Steps(sem("expert_dve"), [n for x in range(ITEMS) for n in (
            f"a{x}_0", f"a{x}_1", f"t{x + 1}_0", f"t{x + 1}_1", f"o{x}")], free=3)

        def turned(steps, x, r, part=""):
            return steps.by(f"t{x}{part}", r) if x else steps.last(f"t{ITEMS}{part}", r)

        xg_loaded = [Moves(sem(f"xg{x}_loaded"), QC) for x in range(2)]
        eo_stored = [Moves(sem(f"eo{x}_stored"), QC) for x in range(2)]
        we_loaded = [Moves(sem(f"we{x}_loaded"), 2) for x in range(2)]
        wed_loaded = [Moves(sem(f"wed{x}_loaded")) for x in range(2)]
        we_split = Steps(sem("expert_weights_split"), [f"{a}{x}" for x in range(2) for a in ("high", "low")])

        tiles_of = lambda ap: ap.rearrange("(t p) c -> t p c", p=P)
        chunk_of = lambda ap: ap.rearrange("(n t p) c -> n p t c", p=P, t=CH // P)
        queue_of = lambda ap: ap.rearrange("(n p t) c -> n p t c", p=P, t=CH // P)
        block = ctx.enter_context(nc.Block())

        def in_order(eng, first_half, lead_in, expert_run, second_half):
            first_half(0)
            with eng.Fori(1, FIRST) as i:
                first_half(i)
            lead_in()
            with eng.Fori(0, E // 2 - 1) as r:
                expert_run(r, False)
            expert_run(E // 2 - 1, True)
            with eng.Fori(0, SECOND - 1) as i:
                second_half(i, False)
            second_half(SECOND - 1, True)

        @block.sync
        def _(sp):
            for m in (*xs_loaded, *hs_loaded, *sum_stored, *row_loaded, *base_loaded,
                      *out_stored, *xg_loaded, *eo_stored, *we_loaded, *wed_loaded):
                sp.sem_inc(m.sem, 16)
            for dst, src in ((falling[:], io["first"]), (starts[:], io["start"]), (before[:], io["before"]), (ones[:], io["ones"])):
                sp.dma_start(dst, src).then_inc(route_loaded, 16)
            for dst, src in ((ws[:, 0], io["ws_gate"].rearrange("(k p) i -> p k i", p=P)),
                             (ws[:, 1], io["ws_up"].rearrange("(k p) i -> p k i", p=P))):
                sp.dma_start(dst, src).then_inc(ws_loaded, 16)

            def load_weights(e, par):
                for n, src in enumerate((io["we_gate"], io["we_up"])):
                    sp.dma_start(we[:, par, n], src[e].rearrange("(k p) i -> p k i", p=P)).then_inc(we_loaded[par].sem, 16)

            def load_down(e, par):
                sp.dma_start(wed[:, par], io["we_down"][e].rearrange("(k p) i -> p k i", p=P)).then_inc(wed_loaded[par].sem, 16)

            def load_xs(run, x):
                sp.dma_start(xs[:, x], keep["x2T"].rearrange("p k (n t) -> n p k t", t=CH)[2 * run + x]).then_inc(xs_loaded[x].sem, 16)

            def load_hs(run, x):
                sp.dma_start(hs[:, x], chunk_of(keep["h2"])[2 * run + x]).then_inc(hs_loaded[x].sem, 16)

            for x in range(2):
                load_xs(0, x)
            for x in range(2):
                load_hs(0, x)
            for dst, src in ((identf[:], io["identity"]), (wsd[:], io["ws_down"].rearrange("(k p) c -> p k c", p=P))):
                sp.dma_start(dst, src).then_inc(const_loaded, 16)
            for x in range(2):
                load_weights(x, x)
                load_down(x, x)

            def shared_moves(run, step, more):
                name = SHARED[step]
                x = int(name[0])
                if name == "0a0" and more:
                    for n in range(2):
                        alone(sp, x_act.sem, x_act.by(f"{n}", run), waited_sp)
                        alone(sp, x_dve.sem, x_dve.by(f"{n}", run), waited_sp)
                        load_xs(run + 1, n)
                if name[1:] == "o1":
                    alone(sp, s_dve.sem, s_dve.by(name, run), waited_sp)
                    sp.dma_start(chunk_of(keep["sum"])[2 * run + x], out_s[:, x]).then_inc(sum_stored[x].sem, 16)
                    if more:
                        load_hs(run + 1, x)

            def load_row(i, t):
                sp.dma_start(row[:, t % SRING], tiles_of(keep["x2"])[i * RS + t]).then_inc(row_loaded[t % SRING].sem, 16)

            def row_used(i, t):
                place = scattered[t % SRING]
                alone(sp, place.sem, place.by(i, TOPK * (t // SRING + 1)), waited_sp)

            def first_half(run, last):
                for step in range(len(SHARED)):
                    if not at_first(run):
                        for t in beside(step, RS):
                            if t + SRING < RS or not last:
                                row_used(run - 1, t + SRING)
                            if t + 2 * SRING < RS or not last:
                                load_row(run - 1, t + 2 * SRING)
                    elif step >= len(SHARED) - SRING:
                        t = step - (len(SHARED) - SRING)
                        row_used(0, t)
                        load_row(0, t + SRING)
                    shared_moves(run, step, True)

            def load_rows(r, x):
                sp.dma_start(xg[:, x % 2], queue_of(keep["queue"])[r * ITEMS + x]).then_inc(xg_loaded[x % 2].sem, 16)

            def expert_run(r, last):
                if not last:
                    for par in range(2):
                        alone(sp, we_split.sem, we_split.by(f"low{par}", r), waited_sp)
                        load_weights(2 * r + 2 + par, par)
                for x in range(ITEMS):
                    alone(sp, e_pe.sem, turned(e_pe, x, r), waited_sp)
                    if x + 2 < ITEMS:
                        load_rows(r, x + 2)
                    elif not last:
                        load_rows(r + 1, x + 2 - ITEMS)
                    alone(sp, e_act.sem, e_act.by(f"o{x}", r), waited_sp)
                    alone(sp, e_dve.sem, e_dve.by(f"o{x}", r), waited_sp)
                    sp.dma_start(queue_of(keep["expert_out"])[r * ITEMS + x], eo[:, x % 2]).then_inc(eo_stored[x % 2].sem, 16)
                    if x % QC == QC - 1 and not last:
                        load_down(2 * r + 2 + x // QC, x // QC)

            def load_base(i, t):
                sp.dma_start(row[:, t % RING], tiles_of(keep["sum"])[i * RG + t]).then_inc(base_loaded[t % RING].sem, 16)

            def store_out(i, t):
                alone(sp, combined.sem, combined.by(f"{t}", i), waited_sp)
                sp.dma_start(tiles_of(io["out"])[i * RG + t], done[:, t % RING]).then_inc(out_stored[t % RING].sem, 16)

            def second_half(i, last):
                for x in range(2):
                    alone(sp, sum_stored[x].sem, sum_stored[x].before(i + FIRST), waited_sp)
                for step in range(len(SHARED)):
                    for t in beside(step, RG):
                        store_out(i, t)
                        load_base(i, t + AHEAD)
                    shared_moves(i + FIRST, step, not last)

            for t in range(SRING):
                load_row(0, t)
            first_half(0, False)
            with sp.Fori(1, FIRST - 1) as run:
                first_half(run, False)
            first_half(FIRST - 1, True)
            for x in range(2):
                load_rows(0, x)
            with sp.Fori(0, E // 2 - 1) as r:
                expert_run(r, False)
            expert_run(E // 2 - 1, True)
            for x in range(2):
                alone(sp, sum_stored[x].sem, sum_stored[x].before(FIRST), waited_sp)
            for t in range(AHEAD):
                load_base(0, t)
            with sp.Fori(0, SECOND - 1) as i:
                second_half(i, False)
            second_half(SECOND - 1, True)
            for x in range(2):
                alone(sp, sum_stored[x].sem, sum_stored[x].before(FIRST + SECOND), waited_sp)
            left = [(i, t) for i in range(SECOND, FULL + 1) for t in range(RG if i < FULL else REST)]
            for n, (i, t) in enumerate(left):
                store_out(i, t)
                if n + AHEAD < len(left):
                    load_base(*left[n + AHEAD])
            for k in range(RING):
                alone(sp, out_stored[k].sem, out_stored[k].by(FULL, len(range(k, REST, RING))), waited_sp)

        @block.gpsimd
        def _(pool):
            for steps in (idx_ready, we_split):
                pool.sem_inc(steps.sem, steps.free)

            def split_weights(r, par):
                alone(pool, we_loaded[par].sem, we_loaded[par].by(r), waited_pool)
                nc.gpsimd.tensor_copy(we_h[:, par], we[:, par]).then_inc(we_split.sem, 1)
                alone(pool, we_split.sem, we_split.by(f"high{par}", r), waited_pool)
                nc.gpsimd.tensor_tensor(we_l[:, par], we[:, par], we_h[:, par], ALU.subtract).then_inc(we_split.sem, 1)

            for par in range(2):
                split_weights(0, par)

            def numbers(source, run, i, tiles, half, n):
                at = half * n
                tiles = min(n, tiles - at)
                nc.gpsimd.tensor_copy(idx[:, at:at + tiles], keep[source][:, bass.ds(i * run + at, tiles), :]).then_inc(idx_ready.sem, 1)

            def scatter(i, last):
                half = RS // 2
                for x in range(2):
                    if x:
                        if not at_first(i):
                            for k in range(SRING):
                                alone(pool, scattered[k].sem, scattered[k].before(i), waited_pool)
                        numbers("scatter", RS, i, RS, 1, half)
                    alone(pool, idx_ready.sem, idx_ready.by(f"{x}", i), waited_pool)
                    for t in range(x * half, (x + 1) * half):
                        k = t % SRING
                        alone(pool, row_loaded[k].sem, row_loaded[k].by(i, t // SRING + 1), waited_pool)
                        for n in range(TOPK):
                            nc.gpsimd.indirect_dma_start(
                                out=keep["queue"], out_offset=bass.IndirectOffsetOnAxis(ap=idx[:, t, n:n + 1], axis=0),
                                in_=row[:, k], in_offset=None, bounds_check=E * CAP - 1, oob_is_err=False,
                            ).then_inc(scattered[k].sem, 16)
                if not last:
                    for k in range(SRING):
                        alone(pool, scattered[k].sem, scattered[k].by(i, TOPK * half // SRING), waited_pool)
                    numbers("scatter", RS, i + 1, RS, 0, half)

            def gather(i, tiles):
                run = i + FIRST - 1
                for x in range(2):
                    if x:
                        if not at_first(i):
                            for k in range(RING):
                                alone(pool, gathered[k].sem, gathered[k].before(i), waited_pool)
                        numbers("gather", RG, i, tiles, 1, RING)
                    alone(pool, idx_ready.sem, idx_ready.by(f"{x}", run), waited_pool)
                    for t in range(x * RING, min((x + 1) * RING, tiles)):
                        k = t % RING
                        alone(pool, combined.sem, combined.by(f"{t}", i) - RING, waited_pool)
                        for n in range(TOPK):
                            nc.gpsimd.indirect_dma_start(
                                out=g_row[:, k, n], out_offset=None, in_=keep["expert_out"],
                                in_offset=bass.IndirectOffsetOnAxis(ap=idx[:, t, n:n + 1], axis=0),
                            ).then_inc(gathered[k].sem, 16)
                if tiles == RG:
                    for k in range(RING):
                        alone(pool, gathered[k].sem, gathered[k].by(i, TOPK), waited_pool)
                    numbers("gather", RG, i + 1, RING, 0, RING)

            pool.wait_ge(routed, 1)
            numbers("scatter", RS, 0, RS, 0, RS // 2)
            scatter(0, False)
            with pool.Fori(1, FIRST - 2) as i:
                scatter(i, False)
            scatter(FIRST - 2, True)
            for k in range(SRING):
                alone(pool, scattered[k].sem, scattered[k].before(FIRST - 1), waited_pool)
            numbers("gather", RG, 0, RING, 0, RING)
            with pool.Fori(0, E // 2 - 1) as r:
                for par in range(2):
                    alone(pool, e_pe.sem, e_pe.by(f"g{QC * par + QC - 1}_1", r), waited_pool)
                    split_weights(r + 1, par)
            for x in range(2):
                alone(pool, eo_stored[x].sem, eo_stored[x].before(E // 2), waited_pool)
            gather(0, RG)
            with pool.Fori(1, FULL) as i:
                gather(i, RG)
            gather(FULL, REST)

        @block.tensor
        def _(pe):
            pe.sem_inc(s_pe.sem, s_pe.free)
            pe.wait_ge(route_loaded, 16 * 4)
            pe.wait_ge(sel_ready, 1)
            for k, w in enumerate((before, ones)):
                ins = pe.matmul(tr[:, k, :], w[:], sel.rearrange("p t e -> p (t e)"), start=True, stop=True)
            ins.then_inc(counted, 1)
            pe.wait_ge(ws_high, 2)
            pe.wait_ge(ws_low, 2)
            pe.wait_ge(const_loaded, 16 * 2)

            def shared(run):
                for x in range(2):
                    pe.wait_ge(x_act.sem, x_act.by(f"{x}", run))
                    pe.wait_ge(x_dve.sem, x_dve.by(f"{x}", run))
                    for m in range(MS):
                        n = x * MS + m
                        if n >= 2:
                            pe.wait_ge(s_dve.sem, s_dve.by(f"{(n - 2) // MS}a{(n - 2) % MS}", run))
                        else:
                            pe.wait_ge(s_dve.sem, s_dve.before(run))
                        for side in range(2):
                            ins = products(pe, gu[:, 2 * (n % 2) + side, :],
                                           lambda ct: [w[:, side, ct, P * m:P * (m + 1)] for w in (ws_h, ws_l)],
                                           lambda ct: (xs_h[:, x, ct, :], xs_l[:, x, ct, :]), KT)
                        ins.then_inc(s_pe.sem, 1)
                for x in range(2):
                    for k in range(2):
                        if x or k == 0:
                            pe.wait_ge(s_dve.sem, s_dve.by(f"0o{k}" if x else f"0a{MS - 1}", run))
                        for q in range(2):
                            t = 2 * k + q
                            for ct in range(MS):
                                ins = pe.matmul(dn[:, k, C * q:C * (q + 1)], inner[:, x, ct, P * t:P * (t + 1)], wsd[:, ct],
                                                start=(ct == 0), stop=(ct == MS - 1))
                        ins.then_inc(s_pe.sem, 1)

            def turn(r, x):
                pe.wait_ge(xg_loaded[x % 2].sem, xg_loaded[x % 2].by(r, x // 2 + 1))
                if x:
                    pe.wait_ge(e_dve.sem, turned(e_dve, x - 1, r, "_1"))
                for ct in range(KT):
                    for q in range(QT):
                        ins = pe.transpose(tr[:, ct, P * q:P * (q + 1)], xg[:, x % 2, q, P * ct:P * (ct + 1)], identf[:])
                ins.then_inc(e_pe.sem, 1)

            def expert_run(r, last):
                for x in range(ITEMS):
                    par = x // QC
                    if x % QC == 0:
                        pe.wait_ge(we_split.sem, we_split.by(f"low{par}", r))
                        pe.wait_ge(wed_loaded[par].sem, wed_loaded[par].by(r))
                    pe.wait_ge(e_act.sem, turned(e_act, x, r, "_1"))
                    pe.wait_ge(e_dve.sem, turned(e_dve, x, r, "_1"))
                    for mt in range(KT):
                        for side in range(2):
                            ins = products(pe, gu[:, 2 * mt + side, :],
                                           lambda ct: [w[:, par, side, ct, P * mt:P * (mt + 1)] for w in (we_h, we_l)],
                                           lambda ct: (xg_h[:, x % 2, ct, :], xg_l[:, x % 2, ct, :]), KT)
                        ins.then_inc(e_pe.sem, 1)
                    if x < ITEMS - 1 or not last:
                        turn(r, x + 1)
                    else:
                        pe.wait_ge(e_pe.sem, e_pe.by(f"g{x}_1", r))
                        pe.sem_inc(e_pe.sem, 1)
                    pe.wait_ge(e_dve.sem, e_dve.by(f"a{x}_1", r))
                    for k in range(2):
                        if k == 0:
                            pe.wait_ge(e_act.sem, e_act.by(f"o{x - 1}", r) if x else e_act.before(r))
                        for q in range(2):
                            for ct in range(KT):
                                ins = pe.matmul(dn[:, k, C * q:C * (q + 1)], e_in[:, x % 2, ct, P * (2 * k + q):P * (2 * k + q + 1)],
                                                wed[:, par, ct], start=(ct == 0), stop=(ct == KT - 1))
                        ins.then_inc(e_pe.sem, 1)

            shared(0)
            with pe.Fori(1, FIRST) as i:
                shared(i)
            pe.wait_ge(s_dve.sem, s_dve.before(FIRST))
            turn(0, 0)
            pe.wait_ge(e_pe.sem, 1)
            pe.sem_inc(e_pe.sem, e_pe.free - 1)
            with pe.Fori(0, E // 2 - 1) as r:
                expert_run(r, False)
            expert_run(E // 2 - 1, True)
            pe.wait_ge(e_act.sem, e_act.before(E // 2))
            pe.wait_ge(e_dve.sem, e_dve.before(E // 2))
            with pe.Fori(FIRST, FIRST + SECOND) as run:
                shared(run)

        @block.scalar
        def _(act):
            a = nc.scalar.activation
            for steps in (s_act, x_act):
                act.sem_inc(steps.sem, steps.free)
            act.wait_ge(shifted, 1)
            a(ex, ex, ACT.Exp).then_inc(exped, 1)
            act.wait_ge(ws_loaded, 16 * 2)
            for n in range(2):
                a(ws_h[:, n], ws[:, n], ACT.Copy).then_inc(ws_high, 1)

            def x_high(run, x):
                act.wait_ge(xs_loaded[x].sem, xs_loaded[x].by(run))
                a(xs_h[:, x], xs[:, x], ACT.Copy).then_inc(x_act.sem, 1)

            for x in range(2):
                x_high(0, x)

            def shared(run, more):
                for x in range(2):
                    for m in range(MS):
                        n = x * MS + m
                        act.wait_ge(s_pe.sem, s_pe.by(f"{x}g{m}", run))
                        if n >= 2:
                            act.wait_ge(s_dve.sem, s_dve.by(f"{(n - 2) // MS}a{(n - 2) % MS}", run))
                        a(sil[:, n % 2, :], gu[:, 2 * (n % 2), :], ACT.Silu).then_inc(s_act.sem, 1)
                        if more and n in SPLIT_AT:
                            x_high(run + 1, SPLIT_AT.index(n))

            def turn(r, x):
                act.wait_ge(e_pe.sem, e_pe.by(f"t{x}", r) if x else 1)
                for ct in range(KT):
                    a(xg_h[:, x % 2, ct, :], tr[:, ct, :], ACT.Copy).then_inc(e_act.sem, 1)

            def expert_run(r, last):
                for x in range(ITEMS):
                    for mt in range(KT):
                        act.wait_ge(e_pe.sem, e_pe.by(f"g{x}_{mt}", r))
                        if x:
                            act.wait_ge(e_dve.sem, e_dve.by(f"a{x - 1}_{mt}", r))
                        a(e_sil[:, mt, :], gu[:, 2 * mt, :], ACT.Silu).then_inc(e_act.sem, 1)
                    if x < ITEMS - 1 or not last:
                        turn(r, x + 1)
                    else:
                        act.wait_ge(e_act.sem, e_act.by(f"s{x}_1", r))
                        act.sem_inc(e_act.sem, 2)
                    act.wait_ge(e_pe.sem, e_pe.by(f"d{x}_0", r))
                    act.wait_ge(eo_stored[x % 2].sem, eo_stored[x % 2].by(r, x // 2))
                    a(eo[:, x % 2, 0:2].rearrange("p t c -> p (t c)"), dn[:, 0, :], ACT.Copy).then_inc(e_act.sem, 1)

            def lead_in():
                turn(0, 0)
                act.wait_ge(e_act.sem, 2)
                act.sem_inc(e_act.sem, e_act.free - 2)

            in_order(act, lambda i: shared(i, True), lead_in, expert_run, lambda i, last: shared(i + FIRST, not last))

        @block.vector
        def _(dve):
            tt, stt = nc.vector.tensor_tensor, nc.vector.scalar_tensor_tensor
            for steps in (s_dve, x_dve, w_ready, half_sum, combined):
                dve.sem_inc(steps.sem, steps.free)
            def x_low(run, x):
                dve.wait_ge(x_act.sem, x_act.by(f"{x}", run))
                tt(xs_l[:, x], xs[:, x], xs_h[:, x], ALU.subtract).then_inc(x_dve.sem, 1)


            def shared(run, step, more):
                name = SHARED[step]
                x, k = int(name[0]), int(name[2:])
                if name[1] == "a":
                    dve.wait_ge(s_act.sem, s_act.by(f"{x}s{k}", run))
                    if step == 0:
                        dve.wait_ge(s_pe.sem, s_pe.before(run))
                    tt(inner[:, x, k, :], sil[:, step % 2, :], gu[:, 2 * (step % 2) + 1, :], ALU.mult).then_inc(s_dve.sem, 1)
                    if more and step in SPLIT_AT:
                        x_low(run + 1, SPLIT_AT.index(step))
                else:
                    if k == 0:
                        dve.wait_ge(hs_loaded[x].sem, hs_loaded[x].by(run))
                        dve.wait_ge(sum_stored[x].sem, sum_stored[x].before(run))
                    dve.wait_ge(s_pe.sem, s_pe.by(f"{x}d{k}", run))
                    tt(out_s[:, x, 2 * k:2 * k + 2].rearrange("p t c -> p (t c)"), dn[:, k, :],
                       hs[:, x, 2 * k:2 * k + 2].rearrange("p t c -> p (t c)"), ALU.add).then_inc(s_dve.sem, 1)

            def turn(r, x):
                for ct in range(KT):
                    dve.wait_ge(e_act.sem, e_act.by(f"t{x}_{ct}", r) if x else ct + 1)
                    tt(xg_l[:, x % 2, ct, :], tr[:, ct, :], xg_h[:, x % 2, ct, :], ALU.subtract).then_inc(e_dve.sem, 1)

            def expert_run(r, last):
                for x in range(ITEMS):
                    for mt in range(KT):
                        dve.wait_ge(e_act.sem, e_act.by(f"s{x}_{mt}", r))
                        tt(e_in[:, x % 2, mt, :], e_sil[:, mt, :], gu[:, 2 * mt + 1, :], ALU.mult).then_inc(e_dve.sem, 1)
                    if x < ITEMS - 1 or not last:
                        turn(r, x + 1)
                    else:
                        dve.wait_ge(e_dve.sem, e_dve.by(f"a{x}_1", r))
                        dve.sem_inc(e_dve.sem, 2)
                    dve.wait_ge(e_pe.sem, e_pe.by(f"d{x}_1", r))
                    dve.wait_ge(eo_stored[x % 2].sem, eo_stored[x % 2].by(r, x // 2))
                    nc.vector.tensor_copy(eo[:, x % 2, 2:4].rearrange("p t c -> p (t c)"), dn[:, 1, :]).then_inc(e_dve.sem, 1)

            def weights(i, tiles):
                dve.wait_ge(combined.sem, combined.before(i))
                nc.vector.tensor_copy(w_now[:, 0:tiles], keep["weight"][:, bass.ds(i * RG, tiles), :]).then_inc(w_ready.sem, 1)
                dve.wait_ge(w_ready.sem, w_ready.by("copied", i))

            def combine(i, t):
                k, n = t % RING, t // RING
                dve.wait_ge(base_loaded[k].sem, base_loaded[k].by(i, n + 1))
                dve.wait_ge(gathered[k].sem, gathered[k].by(i, TOPK * (n + 1)))
                dve.wait_ge(out_stored[k].sem, out_stored[k].by(i, n))
                stt(out=row[:, k], in0=g_row[:, k, 0], scalar=w_now[:, t, 0:1], in1=row[:, k],
                    op0=ALU.mult, op1=ALU.add).then_inc(half_sum.sem, 1)
                dve.wait_ge(half_sum.sem, half_sum.by(f"{t}", i))
                stt(out=done[:, k], in0=g_row[:, k, 1], scalar=w_now[:, t, 1:2], in1=row[:, k],
                    op0=ALU.mult, op1=ALU.add).then_inc(combined.sem, 1)

            def link(ins):
                links[0] += 1
                ins.then_inc(chain, 1)
                dve.wait_ge(chain, links[0])

            links = [0]
            ts, red, copy = nc.vector.tensor_scalar, nc.vector.tensor_reduce, nc.vector.tensor_copy
            wide = lambda x: x.unsqueeze(2).to_broadcast([P, ALLT, E])

            def highest(src):
                link(red(best[:], src, AX.X, ALU.max))
                link(tt(eq, src, wide(best[:]), ALU.is_equal))

            def first_of_equals(k):
                link(tt(eq, eq, first, ALU.mult))
                link(red(best[:], eq, AX.X, ALU.max))
                link(tt(hot[k], eq, wide(best[:]), ALU.is_equal))

            def score_of(k):
                link(tt(rtmp, hot[k], ex, ALU.mult))
                link(red(score[:, :, k], rtmp, AX.X, ALU.add))
                link(tt(score[:, :, k], score[:, :, k], total[:], ALU.mult))

            def place_of(k):
                link(tt(rtmp, hot[k], pos, ALU.mult))
                link(red(pk[:, :, k], rtmp, AX.X, ALU.add))
                link(tt(rtmp, hot[k], start, ALU.mult))
                link(red(slot[:, :, k], rtmp, AX.X, ALU.add))

            def tiles_before(a, b, d):
                link(copy(b[:, 0:d, :], a[:, 0:d, :]))
                link(tt(b[:, d:, :], a[:, d:, :], a[:, :ALLT - d, :], ALU.add))

            def route(step):
                if step == 0:
                    dve.wait_ge(route_loaded, 16 * 4)
                    highest(lg)
                    tt(ex, lg, wide(best[:]), ALU.subtract).then_inc(shifted, 1)
                    dve.wait_ge(shifted, 1)
                elif step == 1:
                    first_of_equals(0)
                    link(ts(l2, hot0, MASKED, None, ALU.mult))
                    link(tt(l2, l2, lg, ALU.add))
                elif step == 2:
                    highest(l2)
                    first_of_equals(1)
                    tt(sel, hot0, hot1, ALU.add).then_inc(sel_ready, 1)
                elif step == 3:
                    dve.wait_ge(exped, 1)
                    link(red(total[:], ex, AX.X, ALU.add))
                    link(nc.vector.reciprocal(total[:], total[:]))
                    score_of(0)
                elif step == 4:
                    score_of(1)
                    link(tt(total[:], score[:, :, 0], score[:, :, 1], ALU.add))
                    link(ts(total[:], total[:], 1e-20, None, ALU.add))
                    link(nc.vector.reciprocal(total[:], total[:]))
                    link(tt(score[:], score[:], total[:].unsqueeze(2).to_broadcast([P, ALLT, TOPK]), ALU.mult))
                elif step == 5:
                    dve.wait_ge(counted, 1)
                    flat = lambda x: x.rearrange("p t e -> p (t e)")
                    link(copy(flat(pre_a), tr[:, 1, :]))
                    link(tt(flat(pos), tr[:, 0, :], flat(pre_a), ALU.subtract))
                elif step == 6:
                    tiles_before(pre_a, pre_b, 1)
                    tiles_before(pre_b, pre_a, 2)
                    tiles_before(pre_a, pre_b, 4)
                elif step == 7:
                    tiles_before(pre_b, pre_a, 8)
                    tiles_before(pre_a, pre_b, 16)
                    tiles_before(pre_b, pre_a, 32)
                elif step == 8:
                    link(tt(pos, pos, pre_a, ALU.add))
                    place_of(0)
                elif step == 9:
                    place_of(1)
                    link(tt(slot[:], slot[:], pk[:], ALU.add))
                elif step == 10:
                    link(ts(kept[:], pk[:], float(CAP), None, ALU.is_lt))
                    link(tt(keep["weight"][:], score[:], kept[:], ALU.mult))
                    link(tt(slot[:], slot[:], kept[:], ALU.mult))
                    link(copy(keep["gather"][:], slot[:]))
                    link(ts(gone[:], kept[:], -float(E * CAP), float(E * CAP), ALU.mult, ALU.add))
                    link(tt(slot[:], slot[:], gone[:], ALU.add))
                    link(copy(keep["scatter"][:], slot[:]))
                    dve.sem_inc(routed, 1)

            assert ALLT == 64 and ALLT * E == BANK
            for step in range(3):
                route(step)
            for n in range(2):
                dve.wait_ge(ws_loaded, 16 * 2)
                dve.wait_ge(ws_high, n + 1)
                tt(ws_l[:, n], ws[:, n], ws_h[:, n], ALU.subtract).then_inc(ws_low, 1)
            for x in range(2):
                x_low(0, x)

            def first_half(run):
                for step in range(len(SHARED)):
                    shared(run, step, True)
                    if at_first(run) and step < 4:
                        route(3 + 2 * step)
                        route(4 + 2 * step)

            def second_half(i, last):
                weights(i, RG)
                for step in range(len(SHARED)):
                    for t in beside(step, RG):
                        combine(i, t)
                    shared(i + FIRST, step, not last)

            def lead_in():
                turn(0, 0)
                dve.wait_ge(e_dve.sem, 2)
                dve.sem_inc(e_dve.sem, e_dve.free - 2)

            in_order(dve, first_half, lead_in, expert_run, second_half)
            for i in range(SECOND, FULL + 1):
                tiles = RG if i < FULL else REST
                weights(i, tiles)
                for t in range(tiles):
                    combine(i, t)



def tower_kernel(nc, io):
    dram = lambda name, shape, dt=F32: nc.dram_tensor(name, shape, dt).ap()
    with ExitStack() as ctx:
        sb = lambda name, shape, dt=F32: ctx.enter_context(nc.sbuf_tensor(name, shape, dt))
        keep = {
            "h": dram("h_rows", [N, C]), "h2": dram("h2_rows", [N, C]),
            "x2": dram("x2_rows", [N, C]), "x2T": dram("x2_cols", [P, KT, N]),
            "parts": dram("qk_parts", [B, 2, PARTS, 2, P, T], BF16),
            "max": dram("max_parts", [UNITS, PARTS, UH * TILES, P], BF16),
            "logits": sb("logits", [P, ALLT * E]), "queue": dram("queues", [E * CAP, C]),
            "expert_out": dram("expert_out", [E * CAP, C]), "sum": dram("shared_sum", [N, C]),
            "index": sb("index", [P, ALLT], U32),
            "emb": sb("emb", [P, TILES, P]), "row_of": sb("row_of", [P, TILES], U32),
            "w_qk": sb("w_qk", [P, KT, 2, 3, P]), "w_v": sb("w_v", [P, KT, C]),
            "scatter": sb("scatter_idx", [P, ALLT, TOPK], U32), "gather": sb("gather_idx", [P, ALLT, TOPK], U32),
            "weight": sb("weight", [P, ALLT, TOPK]),
        }
        prepare(nc, io, keep)
        towers(nc, io, keep)
        experts(nc, io, keep)


def constants():
    f = np.float32
    inv = f(1.0) / (f(10000.0) ** (np.arange(0, HALF, 2, dtype=f) / f(HALF)))
    freqs = np.arange(T, dtype=f)[:, None] * inv[None, :]
    angle = np.concatenate((freqs, freqs), axis=-1)
    cols = lambda a: np.ascontiguousarray(np.repeat(a.T, H, axis=0).astype(f))
    at = np.arange(P)
    return {
        "cos": cols(np.cos(angle)), "sin": cols(np.sin(angle)),
        "identity": np.eye(P, dtype=f),
        "mask": np.where(at[None, :] > at[:, None], MASKED, 0.0).astype(f),
        "before": (at[:, None] < at[None, :]).astype(f), "ones": np.ones((P, P), f),
        "first": np.ascontiguousarray(np.broadcast_to(np.arange(E, 0, -1, dtype=f), (P, E))),
        "start": np.ascontiguousarray(np.broadcast_to(np.arange(E, dtype=f) * CAP, (P, E))),
    }


def layouts(a):
    flat = np.asarray(a["x"]).reshape(-1)
    before = np.concatenate([flat[:1], flat[:-1]])
    t = lambda x, *axes: np.ascontiguousarray(np.transpose(np.asarray(x), axes or None))
    side = lambda *x: np.ascontiguousarray(np.concatenate([np.asarray(v) for v in x], axis=1))
    return {
        "ids": side(flat.reshape(ALLT, P), before.reshape(ALLT, P)),
        "embed": np.asarray(a["L0_tok_embed"]), "proj_t": t(a["L0_tok_proj_w"]),
        "scale": np.ascontiguousarray(np.broadcast_to(np.asarray(a["L0_tok_scale"]), (P, 1))),
        "down_q": t(a["L0_attn_Wq_down"]), "down_k": t(a["L0_attn_Wk_down"]), "down_v": t(a["L0_attn_Wv_down"]),
        "up_q": side(a["L0_attn_Wq_up_c"], a["L0_attn_Wq_up_e"]), "up_k": side(a["L0_attn_Wk_up_c"], a["L0_attn_Wk_up_e"]),
        "up_v": np.asarray(a["L0_attn_Wv_up"]), "w_out": np.asarray(a["L0_attn_Wc"]),
        "gate_t": t(a["L0_ffn_gate_w"]),
        "we_gate": t(a["L0_ffn_we_gate"], 0, 2, 1), "we_up": t(a["L0_ffn_we_up"], 0, 2, 1),
        "we_down": t(a["L0_ffn_we_down"], 0, 2, 1),
        "ws_gate": t(a["L0_ffn_ws_gate"]), "ws_up": t(a["L0_ffn_ws_up"]), "ws_down": t(a["L0_ffn_ws_down"]),
    }


def kernel(**inputs):
    import concourse.bacc as bacc
    from concourse.bass_utils import run_bass_kernel_spmd

    nc = bacc.Bacc("TRN2", target_bir_lowering=False, num_devices=1)
    arrays = {f"in_{k}": v for k, v in {**layouts(inputs), **constants()}.items()}
    io = {k[3:]: nc.dram_tensor(k, v.shape, mybir.dt.from_np(v.dtype), kind="ExternalInput").ap() for k, v in arrays.items()}
    io["out"] = nc.dram_tensor("out", (N, C), F32, kind="ExternalOutput").ap()
    tower_kernel(nc, io)
    r = run_bass_kernel_spmd(nc, [arrays], core_ids=[0])
    return r.results[0]["out"].reshape(B, T, C)
```
